# Optimizing a Trainium2 kernel written in Bass

```python
import numpy as np
import jax
import jax.numpy as jnp

def _softmax(x, axis=-1):
    return jax.nn.softmax(x, axis=axis)

def _gelu(x):
    return jax.nn.gelu(x, approximate=True)

def _silu(x):
    return jax.nn.silu(x)

def _sigmoid(x):
    return jax.nn.sigmoid(x)

def _layernorm(x, axis=-1, eps=1e-05):
    m = jnp.mean(x, axis=axis, keepdims=True)
    v = jnp.var(x, axis=axis, keepdims=True)
    return (x - m) / jnp.sqrt(v + eps)

def _scatter_add(tgt, idx, src, axis=0):
    return tgt.at[idx].add(src)

def _segment_sum(src, seg, n):
    return jax.ops.segment_sum(src, seg, n)
kernel_name = 'mk_flamingo_gated_d4_seqx_r4_f0d18e'

def setup_inputs(seed: int=0):
    np.random.seed(seed)
    _w = jnp.asarray

    def _rec_inputs():
        import jax
        import jax.numpy as jnp
        _rk = jax.random.key(seed)
        x = 7.22e-05 + 1 * jax.random.normal(jax.random.fold_in(_rk, 1), (32, 128, 256), jnp.float32)
        _lenS = 128 - jax.random.randint(jax.random.fold_in(_rk, 7), (32,), 0, max(1, 128 // 4) + 1, jnp.int32)
        _lenS2 = 128 - jax.random.randint(jax.random.fold_in(_rk, 8), (32,), 0, max(1, 128 // 4) + 1, jnp.int32)
        _ctx_768P = jax.random.normal(jax.random.fold_in(_rk, 11), (32, 16, 192), jnp.float32)
        _ctx_768c = jax.random.dirichlet(jax.random.fold_in(_rk, 511), 0.3 * jnp.ones((16,), jnp.float32), (32, 128))
        _ctx_768t = jnp.einsum('bsk,bkd->bsd', _ctx_768c, _ctx_768P)
        _ctx_768t = _ctx_768t * jax.lax.rsqrt(jnp.mean(jnp.square(_ctx_768t)) + 1e-12) * 0.953939
        ctx_768 = -0.000191848 + 0.999787 * (_ctx_768t + 0.3 * jax.random.normal(jax.random.fold_in(_rk, 611), (32, 128, 192), jnp.float32))
        _g = jax.random.normal(jax.random.fold_in(_rk, 9001), (2, 4), jnp.float32)
        _g = jnp.sign(_g) * jnp.maximum(jnp.abs(_g), 1.0) + (_g == 0) * 1.0
        g_xattn = _g[0]
        g_ffn = _g[1]
        return (x, ctx_768, g_xattn, g_ffn)
    x, ctx_768, g_xattn, g_ffn = _rec_inputs()

    def _L0_xattn_setup():
        import jax, jax.numpy as jnp
        import numpy as np
        N_HEADS = 16
        key = jax.random.key(seed)
        ks = jax.random.split(key, 8)
        b, l, m = (8, 256, 256)
        d_embed, d_cross = (256, 192)
        s_q = 1.0 / np.sqrt(d_embed)
        s_kv = 1.0 / np.sqrt(d_cross)
        return {'x': jax.random.normal(ks[0], (b, l, d_embed), jnp.float32), 'y': jax.random.normal(ks[1], (b, m, d_cross), jnp.float32), 'Wq': jax.random.normal(ks[2], (d_embed, d_embed), jnp.float32) * s_q, 'bq': jax.random.normal(ks[3], (d_embed,), jnp.float32) * 0.01, 'Wkv': jax.random.normal(ks[4], (2 * d_embed, d_cross), jnp.float32) * s_kv, 'bkv': jax.random.normal(ks[5], (2 * d_embed,), jnp.float32) * 0.01, 'Wo': jax.random.normal(ks[6], (d_embed, d_embed), jnp.float32) * s_q, 'bo': jax.random.normal(ks[7], (d_embed,), jnp.float32) * 0.01}
    _L0_xattn_all = _L0_xattn_setup()
    _L0_xattn_in = {k: v for k, v in _L0_xattn_all.items() if k in ('Wq', 'bq', 'Wkv', 'bkv', 'Wo', 'bo')}
    del _L0_xattn_all

    def _L0_ffn_setup():
        import jax, jax.numpy as jnp
        import numpy as np
        B, S, D_MODEL, D_HIDDEN = (4, 512, 256, 1024)

        def act_quant(x):
            scale = 127.0 / jnp.clip(jnp.max(jnp.abs(x), axis=-1, keepdims=True), 1e-05)
            return jnp.clip(jnp.round(x * scale), -128, 127) / scale

        def weight_quant(w):
            scale = 1.0 / jnp.clip(jnp.mean(jnp.abs(w)), 1e-05)
            return jnp.clip(jnp.round(w * scale), -1, 1) / scale

        def bit_linear(x, w):
            xq = x + jax.lax.stop_gradient(act_quant(x) - x)
            wq = w + jax.lax.stop_gradient(weight_quant(w) - w)
            return jnp.einsum('bsd,hd->bsh', xq, wq)

        def depthwise_conv1d(x_bcl, w, b):
            y = jax.lax.conv_general_dilated(x_bcl, w, window_strides=(1,), padding=[(1, 1)], dimension_numbers=('NCH', 'OIH', 'NCH'), feature_group_count=x_bcl.shape[1])
            return y + b[None, :, None]
        key = jax.random.key(seed)
        ks = jax.random.split(key, 5)
        lim1 = 1.0 / np.sqrt(D_MODEL)
        lim2 = 1.0 / np.sqrt(D_HIDDEN)
        limc = 1.0 / np.sqrt(3.0)
        return {'x': jax.random.normal(ks[0], (B, S, D_MODEL), dtype=jnp.float32), 'w1': jax.random.uniform(ks[1], (D_HIDDEN, D_MODEL), jnp.float32, -lim1, lim1), 'conv_w': jax.random.uniform(ks[2], (D_HIDDEN, 1, 3), jnp.float32, -limc, limc), 'conv_b': jax.random.uniform(ks[3], (D_HIDDEN,), jnp.float32, -limc, limc), 'w2': jax.random.uniform(ks[4], (D_MODEL, D_HIDDEN), jnp.float32, -lim2, lim2)}
    _L0_ffn_all = _L0_ffn_setup()
    _L0_ffn_in = {k: v for k, v in _L0_ffn_all.items() if k in ('w1', 'conv_w', 'conv_b', 'w2')}
    del _L0_ffn_all

    def _L1_xattn_setup():
        import jax, jax.numpy as jnp
        import numpy as np
        N_HEADS = 16
        D_HEAD = 64
        key = jax.random.key(seed)
        ks = jax.random.split(key, 7)
        B, SQ, SKV = (2, 512, 512)
        D_MODEL, D_COND, D_ATTN = (256, 192, N_HEADS * D_HEAD)
        return {'x': jax.random.normal(ks[0], (B, SQ, D_MODEL), jnp.float32), 'cond': jax.random.normal(ks[1], (B, SKV, D_COND), jnp.float32), 'w_q': jax.random.normal(ks[2], (D_MODEL, D_ATTN), jnp.float32) * D_MODEL ** (-0.5), 'w_k': jax.random.normal(ks[3], (D_COND, D_ATTN), jnp.float32) * D_COND ** (-0.5), 'w_v': jax.random.normal(ks[4], (D_COND, D_ATTN), jnp.float32) * D_COND ** (-0.5), 'w_out': jax.random.normal(ks[5], (D_ATTN, D_MODEL), jnp.float32) * D_ATTN ** (-0.5), 'b_out': jnp.zeros((D_MODEL,), jnp.float32)}
    _L1_xattn_all = _L1_xattn_setup()
    _L1_xattn_in = {k: v for k, v in _L1_xattn_all.items() if k in ('w_q', 'w_k', 'w_v', 'w_out', 'b_out')}
    del _L1_xattn_all

    def _L1_ffn_setup():
        import jax, jax.numpy as jnp
        import numpy as np
        B, S, H, E = (4, 512, 256, 8)
        key = jax.random.key(seed)
        k1, k2, k3 = jax.random.split(key, 3)
        scale_w = 1.0 / np.sqrt(H)
        return {'x': jax.random.normal(k1, (B, S, H), dtype=jnp.float32), 'router_w': jax.random.normal(k2, (H, E), dtype=jnp.float32) * scale_w, 'router_b': jnp.zeros((E,), dtype=jnp.float32), 'expert_w': jax.random.normal(k3, (E, H, H), dtype=jnp.float32) * scale_w, 'expert_b': jnp.zeros((E, H), dtype=jnp.float32)}
    _L1_ffn_all = _L1_ffn_setup()
    _L1_ffn_in = {k: v for k, v in _L1_ffn_all.items() if k in ('router_w', 'router_b', 'expert_w', 'expert_b')}
    del _L1_ffn_all

    def _L2_xattn_setup():
        import jax, jax.numpy as jnp
        import numpy as np
        NUM_HEADS = 16
        CLAMP = 10000.0
        key = jax.random.key(seed)
        ks = jax.random.split(key, 8)
        B, Nq, Nkv, Cq, Ckv = (4, 512, 512, 256, 192)
        s_q = 1.0 / np.sqrt(Cq)
        s_kv = 1.0 / np.sqrt(Ckv)
        return {'query': jax.random.normal(ks[0], (B, Nq, Cq), jnp.float32), 'key_value': jax.random.normal(ks[1], (B, Nkv, Ckv), jnp.float32), 'Wq': jax.random.normal(ks[2], (Cq, Cq), jnp.float32) * s_q, 'bq': jnp.zeros((Cq,), jnp.float32), 'Wk': jax.random.normal(ks[3], (Ckv, Cq), jnp.float32) * s_kv, 'bk': jnp.zeros((Cq,), jnp.float32), 'Wv': jax.random.normal(ks[4], (Ckv, Cq), jnp.float32) * s_kv, 'bv': jnp.zeros((Cq,), jnp.float32), 'Wo': jax.random.normal(ks[5], (Cq, Cq), jnp.float32) * s_q, 'bo': jnp.zeros((Cq,), jnp.float32)}
    _L2_xattn_all = _L2_xattn_setup()
    _L2_xattn_in = {k: v for k, v in _L2_xattn_all.items() if k in ('Wq', 'bq', 'Wk', 'bk', 'Wv', 'bv', 'Wo', 'bo')}
    del _L2_xattn_all

    def _L2_ffn_setup():
        import jax, jax.numpy as jnp
        import numpy as np
        D, H, NE, K, ED = (256, 16, 8, 2, 1024)
        B, S = (4, 256)
        EPS = 1e-06

        def rmsnorm(x, w):
            ms = jnp.mean(jnp.square(x.astype(jnp.float32)), axis=-1, keepdims=True)
            return x * jax.lax.rsqrt(ms + EPS).astype(x.dtype) * w

        def attn(x, qkv_w, o_w):
            b, s, d = x.shape
            hd = d // H
            qkv = (x @ qkv_w.T).reshape(b, s, 3, H, hd).transpose(2, 0, 3, 1, 4)
            q, k, v = (qkv[0], qkv[1], qkv[2])
            a = jnp.einsum('bhqd,bhkd->bhqk', q, k) * hd ** (-0.5)
            mask = jnp.triu(jnp.ones((s, s), dtype=bool), 1)
            a = jax.nn.softmax(jnp.where(mask, -1000000000.0, a), axis=-1)
            out = jnp.einsum('bhqk,bhkd->bhqd', a, v).transpose(0, 2, 1, 3).reshape(b, s, d)
            return out @ o_w.T

        def moe(x, gate_w, up_w, down_w):
            b, s, d = x.shape
            xf = x.reshape(b * s, d)
            gp = jax.nn.softmax(xf @ gate_w.T, axis=-1)
            ew, _ = jax.lax.top_k(gp, K)
            ew = ew / (jnp.sum(ew, axis=-1, keepdims=True) + 1e-09)
            ef = jax.nn.silu(xf @ up_w.T) @ down_w.T
            out = ef * jnp.sum(ew, axis=-1, keepdims=True)
            return out.reshape(b, s, d)
        key = jax.random.key(seed)
        ks = jax.random.split(key, 8)
        sd = 1.0 / np.sqrt(D)
        se = 1.0 / np.sqrt(ED)
        return {'x': jax.random.normal(ks[0], (B, S, D), dtype=jnp.float32), 'n1_w': jnp.ones((D,), jnp.float32), 'qkv_w': jax.random.normal(ks[1], (3 * D, D), jnp.float32) * sd, 'o_w': jax.random.normal(ks[2], (D, D), jnp.float32) * sd, 'n2_w': jnp.ones((D,), jnp.float32), 'gate_w': jax.random.normal(ks[3], (NE, D), jnp.float32) * sd, 'up_w': jax.random.normal(ks[4], (ED, D), jnp.float32) * sd, 'down_w': jax.random.normal(ks[5], (D, ED), jnp.float32) * se}
    _L2_ffn_all = _L2_ffn_setup()
    _L2_ffn_in = {k: v for k, v in _L2_ffn_all.items() if k in ('n1_w', 'qkv_w', 'o_w', 'n2_w', 'gate_w', 'up_w', 'down_w')}
    del _L2_ffn_all

    def _L3_xattn_setup():
        import jax, jax.numpy as jnp
        import numpy as np
        EMBED_DIM = 256
        Q_DIM = 256
        KV_DIM = 192
        NUM_HEADS = 16
        HEAD_DIM = EMBED_DIM // NUM_HEADS
        SCALE = NUM_HEADS ** (-0.5)

        def _linear_params(key, in_dim, out_dim):
            kw, kb = jax.random.split(key)
            bound = 1.0 / np.sqrt(in_dim)
            W = jax.random.uniform(kw, (in_dim, out_dim), minval=-bound, maxval=bound, dtype=jnp.float32)
            b = jax.random.uniform(kb, (out_dim,), minval=-bound, maxval=bound, dtype=jnp.float32)
            return (W, b)
        key = jax.random.key(seed)
        ks = jax.random.split(key, 8)
        B, N1, N2 = (2, 512, 512)
        query = jax.random.normal(ks[0], (B, N1, Q_DIM), dtype=jnp.float32)
        k_in = jax.random.normal(ks[1], (B, N2, KV_DIM), dtype=jnp.float32)
        v_in = jax.random.normal(ks[2], (B, N2, KV_DIM), dtype=jnp.float32)
        Wq, bq = _linear_params(ks[3], Q_DIM, EMBED_DIM)
        Wk, bk = _linear_params(ks[4], KV_DIM, EMBED_DIM)
        Wv, bv = _linear_params(ks[5], KV_DIM, EMBED_DIM)
        Wo, bo = _linear_params(ks[6], EMBED_DIM, EMBED_DIM)
        return {'query': query, 'key': k_in, 'value': v_in, 'Wq': Wq, 'bq': bq, 'Wk': Wk, 'bk': bk, 'Wv': Wv, 'bv': bv, 'Wo': Wo, 'bo': bo}
    _L3_xattn_all = _L3_xattn_setup()
    _L3_xattn_in = {k: v for k, v in _L3_xattn_all.items() if k in ('Wq', 'bq', 'Wk', 'bk', 'Wv', 'bv', 'Wo', 'bo')}
    del _L3_xattn_all

    def _L3_ffn_setup():
        import jax, jax.numpy as jnp
        import numpy as np
        GROUP = 16
        EPS = 1e-05

        def _dequant(q, scale):
            w = q.astype(jnp.float32) / 7.5 - 1.0
            return w * jnp.repeat(scale, GROUP, axis=1)

        def _qlora_linear(x, q, scale, bias, la, lb):
            w = _dequant(q, scale)
            base = jnp.einsum('btd,od->bto', x, w) + bias
            lora = jnp.einsum('btr,or->bto', jnp.einsum('btd,rd->btr', x, la), lb)
            return base + lora

        def _layernorm(x, g, b):
            mu = jnp.mean(x, axis=-1, keepdims=True)
            var = jnp.mean(jnp.square(x - mu), axis=-1, keepdims=True)
            return (x - mu) * jax.lax.rsqrt(var + EPS) * g + b
        key = jax.random.key(seed)
        ks = jax.random.split(key, 6)
        D, R, B, T = (256, 32, 8, 1024)
        x = jax.random.normal(ks[0], (B, T, D), dtype=jnp.float32)
        qweights = jax.random.randint(ks[1], (6, D, D), 0, 16, dtype=jnp.int32)
        scales = jax.random.uniform(ks[2], (6, D, D // GROUP), dtype=jnp.float32)
        biases = jax.random.normal(ks[3], (6, D), dtype=jnp.float32) * 0.02
        lora_a = jax.random.normal(ks[4], (6, R, D), dtype=jnp.float32) * 0.02
        lora_b = jax.random.normal(ks[5], (6, D, R), dtype=jnp.float32) * 0.02
        ln_gamma = jnp.ones((3, D), dtype=jnp.float32)
        ln_beta = jnp.zeros((3, D), dtype=jnp.float32)
        return {'x': x, 'qweights': qweights, 'scales': scales, 'biases': biases, 'lora_a': lora_a, 'lora_b': lora_b, 'ln_gamma': ln_gamma, 'ln_beta': ln_beta}
    _L3_ffn_all = _L3_ffn_setup()
    _L3_ffn_in = {k: v for k, v in _L3_ffn_all.items() if k in ('qweights', 'scales', 'biases', 'lora_a', 'lora_b', 'ln_gamma', 'ln_beta')}
    del _L3_ffn_all
    return {'x': x, 'ctx_768': ctx_768, 'g_xattn': g_xattn, 'g_ffn': g_ffn, 'L0_xattn_Wq': _L0_xattn_in['Wq'], 'L0_xattn_bq': _L0_xattn_in['bq'], 'L0_xattn_Wkv': _L0_xattn_in['Wkv'], 'L0_xattn_bkv': _L0_xattn_in['bkv'], 'L0_xattn_Wo': _L0_xattn_in['Wo'], 'L0_xattn_bo': _L0_xattn_in['bo'], 'L0_ffn_w1': _L0_ffn_in['w1'], 'L0_ffn_conv_w': _L0_ffn_in['conv_w'], 'L0_ffn_conv_b': _L0_ffn_in['conv_b'], 'L0_ffn_w2': _L0_ffn_in['w2'], 'L1_xattn_w_q': _L1_xattn_in['w_q'], 'L1_xattn_w_k': _L1_xattn_in['w_k'], 'L1_xattn_w_v': _L1_xattn_in['w_v'], 'L1_xattn_w_out': _L1_xattn_in['w_out'], 'L1_xattn_b_out': _L1_xattn_in['b_out'], 'L1_ffn_router_w': _L1_ffn_in['router_w'], 'L1_ffn_router_b': _L1_ffn_in['router_b'], 'L1_ffn_expert_w': _L1_ffn_in['expert_w'], 'L1_ffn_expert_b': _L1_ffn_in['expert_b'], 'L2_xattn_Wq': _L2_xattn_in['Wq'], 'L2_xattn_bq': _L2_xattn_in['bq'], 'L2_xattn_Wk': _L2_xattn_in['Wk'], 'L2_xattn_bk': _L2_xattn_in['bk'], 'L2_xattn_Wv': _L2_xattn_in['Wv'], 'L2_xattn_bv': _L2_xattn_in['bv'], 'L2_xattn_Wo': _L2_xattn_in['Wo'], 'L2_xattn_bo': _L2_xattn_in['bo'], 'L2_ffn_n1_w': _L2_ffn_in['n1_w'], 'L2_ffn_qkv_w': _L2_ffn_in['qkv_w'], 'L2_ffn_o_w': _L2_ffn_in['o_w'], 'L2_ffn_n2_w': _L2_ffn_in['n2_w'], 'L2_ffn_gate_w': _L2_ffn_in['gate_w'], 'L2_ffn_up_w': _L2_ffn_in['up_w'], 'L2_ffn_down_w': _L2_ffn_in['down_w'], 'L3_xattn_Wq': _L3_xattn_in['Wq'], 'L3_xattn_bq': _L3_xattn_in['bq'], 'L3_xattn_Wk': _L3_xattn_in['Wk'], 'L3_xattn_bk': _L3_xattn_in['bk'], 'L3_xattn_Wv': _L3_xattn_in['Wv'], 'L3_xattn_bv': _L3_xattn_in['bv'], 'L3_xattn_Wo': _L3_xattn_in['Wo'], 'L3_xattn_bo': _L3_xattn_in['bo'], 'L3_ffn_qweights': _L3_ffn_in['qweights'], 'L3_ffn_scales': _L3_ffn_in['scales'], 'L3_ffn_biases': _L3_ffn_in['biases'], 'L3_ffn_lora_a': _L3_ffn_in['lora_a'], 'L3_ffn_lora_b': _L3_ffn_in['lora_b'], 'L3_ffn_ln_gamma': _L3_ffn_in['ln_gamma'], 'L3_ffn_ln_beta': _L3_ffn_in['ln_beta']}

def reference(x, ctx_768, g_xattn, g_ffn, L0_xattn_Wq, L0_xattn_bq, L0_xattn_Wkv, L0_xattn_bkv, L0_xattn_Wo, L0_xattn_bo, L0_ffn_w1, L0_ffn_conv_w, L0_ffn_conv_b, L0_ffn_w2, L1_xattn_w_q, L1_xattn_w_k, L1_xattn_w_v, L1_xattn_w_out, L1_xattn_b_out, L1_ffn_router_w, L1_ffn_router_b, L1_ffn_expert_w, L1_ffn_expert_b, L2_xattn_Wq, L2_xattn_bq, L2_xattn_Wk, L2_xattn_bk, L2_xattn_Wv, L2_xattn_bv, L2_xattn_Wo, L2_xattn_bo, L2_ffn_n1_w, L2_ffn_qkv_w, L2_ffn_o_w, L2_ffn_n2_w, L2_ffn_gate_w, L2_ffn_up_w, L2_ffn_down_w, L3_xattn_Wq, L3_xattn_bq, L3_xattn_Wk, L3_xattn_bk, L3_xattn_Wv, L3_xattn_bv, L3_xattn_Wo, L3_xattn_bo, L3_ffn_qweights, L3_ffn_scales, L3_ffn_biases, L3_ffn_lora_a, L3_ffn_lora_b, L3_ffn_ln_gamma, L3_ffn_ln_beta):
    import jax
    import jax.numpy as jnp

    def _L0_xattn_ref(x, y, Wq, bq, Wkv, bkv, Wo, bo):
        import jax, jax.numpy as jnp
        import numpy as np
        N_HEADS = 16
        b, l, d = x.shape
        m = y.shape[1]
        h = N_HEADS
        dh = d // h
        q = (jnp.einsum('bld,ed->ble', x, Wq) + bq).reshape(b, l, h, dh)
        kv = (jnp.einsum('bmc,ec->bme', y, Wkv) + bkv).reshape(b, m, h, 2 * dh)
        k, v = (kv[..., :dh], kv[..., dh:])
        scale = 1.0 / jnp.sqrt(jnp.asarray(dh, x.dtype))
        att = jax.nn.softmax(jnp.einsum('blhd,bmhd->blmh', q, k) * scale, axis=2)
        out = jnp.einsum('blmh,bmhd->blhd', att, v).reshape(b, l, d)
        return jnp.einsum('bld,ed->ble', out, Wo) + bo

    def _L0_ffn_ref(x, w1, conv_w, conv_b, w2):
        import jax, jax.numpy as jnp
        import numpy as np
        B, S, D_MODEL, D_HIDDEN = (4, 512, 256, 1024)

        def act_quant(x):
            scale = 127.0 / jnp.clip(jnp.max(jnp.abs(x), axis=-1, keepdims=True), 1e-05)
            return jnp.clip(jnp.round(x * scale), -128, 127) / scale

        def weight_quant(w):
            scale = 1.0 / jnp.clip(jnp.mean(jnp.abs(w)), 1e-05)
            return jnp.clip(jnp.round(w * scale), -1, 1) / scale

        def bit_linear(x, w):
            xq = x + jax.lax.stop_gradient(act_quant(x) - x)
            wq = w + jax.lax.stop_gradient(weight_quant(w) - w)
            return jnp.einsum('bsd,hd->bsh', xq, wq)

        def depthwise_conv1d(x_bcl, w, b):
            y = jax.lax.conv_general_dilated(x_bcl, w, window_strides=(1,), padding=[(1, 1)], dimension_numbers=('NCH', 'OIH', 'NCH'), feature_group_count=x_bcl.shape[1])
            return y + b[None, :, None]
        h = bit_linear(x, w1)
        h = depthwise_conv1d(h.transpose(0, 2, 1), conv_w, conv_b)
        h = h.transpose(0, 2, 1)
        h = jax.nn.silu(h)
        return bit_linear(h, w2)

    def _L1_xattn_ref(x, cond, w_q, w_k, w_v, w_out, b_out):
        import jax, jax.numpy as jnp
        import numpy as np
        N_HEADS = 16
        D_HEAD = 64
        B, SQ, _ = x.shape
        SKV = cond.shape[1]
        scale = D_HEAD ** (-0.5)
        q = (x @ w_q).reshape(B, SQ, N_HEADS, D_HEAD)
        k = (cond @ w_k).reshape(B, SKV, N_HEADS, D_HEAD)
        v = (cond @ w_v).reshape(B, SKV, N_HEADS, D_HEAD)
        attn = jnp.einsum('bqhd,bkhd->bhqk', q, k) * scale
        attn = jax.nn.softmax(attn, axis=-1)
        out = jnp.einsum('bhqk,bkhd->bqhd', attn, v).reshape(B, SQ, N_HEADS * D_HEAD)
        return out @ w_out + b_out

    def _L1_ffn_ref(x, router_w, router_b, expert_w, expert_b):
        import jax, jax.numpy as jnp
        import numpy as np
        B, S, H, E = (4, 512, 256, 8)
        b, s, h = x.shape
        xt = x.reshape(b * s, h)
        logits = xt @ router_w + router_b
        probs = jax.nn.softmax(logits, axis=-1)
        gate = jnp.max(probs, axis=-1)
        idx = jnp.argmax(probs, axis=-1)
        out_all = jnp.einsum('th,ehd->ted', xt, expert_w) + expert_b[None, :, :]
        e_out = jnp.take_along_axis(out_all, idx[:, None, None], axis=1)[:, 0, :]
        y = gate[:, None] * e_out
        return y.reshape(b, s, h)

    def _L2_xattn_ref(query, key_value, Wq, bq, Wk, bk, Wv, bv, Wo, bo):
        import jax, jax.numpy as jnp
        import numpy as np
        NUM_HEADS = 16
        CLAMP = 10000.0
        B, Nq, Cq = query.shape
        Nkv = key_value.shape[1]
        H = NUM_HEADS
        D = Cq // H
        scale = D ** (-0.5)
        q = (query @ Wq + bq).reshape(B, Nq, H, D).transpose(0, 2, 1, 3)
        k = (key_value @ Wk + bk).reshape(B, Nkv, H, D).transpose(0, 2, 1, 3)
        v = (key_value @ Wv + bv).reshape(B, Nkv, H, D).transpose(0, 2, 1, 3)
        attn = jnp.einsum('bhqd,bhkd->bhqk', q, k) * scale
        attn = jnp.clip(attn, -CLAMP, CLAMP)
        attn = jax.nn.softmax(attn, axis=-1)
        attn = jnp.where(jnp.any(jnp.isnan(attn)), jnp.asarray(1.0 / Nkv, attn.dtype), attn)
        x = jnp.einsum('bhqk,bhkd->bqhd', attn, v).reshape(B, Nq, Cq)
        return x @ Wo + bo

    def _L2_ffn_ref(x, n1_w, qkv_w, o_w, n2_w, gate_w, up_w, down_w):
        import jax, jax.numpy as jnp
        import numpy as np
        D, H, NE, K, ED = (256, 16, 8, 2, 1024)
        B, S = (4, 256)
        EPS = 1e-06

        def rmsnorm(x, w):
            ms = jnp.mean(jnp.square(x.astype(jnp.float32)), axis=-1, keepdims=True)
            return x * jax.lax.rsqrt(ms + EPS).astype(x.dtype) * w

        def attn(x, qkv_w, o_w):
            b, s, d = x.shape
            hd = d // H
            qkv = (x @ qkv_w.T).reshape(b, s, 3, H, hd).transpose(2, 0, 3, 1, 4)
            q, k, v = (qkv[0], qkv[1], qkv[2])
            a = jnp.einsum('bhqd,bhkd->bhqk', q, k) * hd ** (-0.5)
            mask = jnp.triu(jnp.ones((s, s), dtype=bool), 1)
            a = jax.nn.softmax(jnp.where(mask, -1000000000.0, a), axis=-1)
            out = jnp.einsum('bhqk,bhkd->bhqd', a, v).transpose(0, 2, 1, 3).reshape(b, s, d)
            return out @ o_w.T

        def moe(x, gate_w, up_w, down_w):
            b, s, d = x.shape
            xf = x.reshape(b * s, d)
            gp = jax.nn.softmax(xf @ gate_w.T, axis=-1)
            ew, _ = jax.lax.top_k(gp, K)
            ew = ew / (jnp.sum(ew, axis=-1, keepdims=True) + 1e-09)
            ef = jax.nn.silu(xf @ up_w.T) @ down_w.T
            out = ef * jnp.sum(ew, axis=-1, keepdims=True)
            return out.reshape(b, s, d)
        x = x + attn(rmsnorm(x, n1_w), qkv_w, o_w)
        x = x + moe(rmsnorm(x, n2_w), gate_w, up_w, down_w)
        return x

    def _L3_xattn_ref(query, key, value, Wq, bq, Wk, bk, Wv, bv, Wo, bo):
        import jax, jax.numpy as jnp
        import numpy as np
        EMBED_DIM = 256
        Q_DIM = 256
        KV_DIM = 192
        NUM_HEADS = 16
        HEAD_DIM = EMBED_DIM // NUM_HEADS
        SCALE = NUM_HEADS ** (-0.5)

        def _linear_params(key, in_dim, out_dim):
            kw, kb = jax.random.split(key)
            bound = 1.0 / np.sqrt(in_dim)
            W = jax.random.uniform(kw, (in_dim, out_dim), minval=-bound, maxval=bound, dtype=jnp.float32)
            b = jax.random.uniform(kb, (out_dim,), minval=-bound, maxval=bound, dtype=jnp.float32)
            return (W, b)
        B, N1, _ = query.shape
        N2 = key.shape[1]
        Q = (query @ Wq + bq).reshape(B, N1, NUM_HEADS, HEAD_DIM).transpose(0, 2, 1, 3)
        K = (key @ Wk + bk).reshape(B, N2, NUM_HEADS, HEAD_DIM).transpose(0, 2, 1, 3)
        V = (value @ Wv + bv).reshape(B, N2, NUM_HEADS, HEAD_DIM).transpose(0, 2, 1, 3)
        att = jnp.einsum('bhqd,bhkd->bhqk', Q, K) * SCALE
        att = jax.nn.softmax(att, axis=-1)
        out = jnp.einsum('bhqk,bhkd->bhqd', att, V)
        out = out.transpose(0, 2, 1, 3).reshape(B, N1, EMBED_DIM)
        return out @ Wo + bo

    def _L3_ffn_ref(x, qweights, scales, biases, lora_a, lora_b, ln_gamma, ln_beta):
        import jax, jax.numpy as jnp
        import numpy as np
        GROUP = 16
        EPS = 1e-05

        def _dequant(q, scale):
            w = q.astype(jnp.float32) / 7.5 - 1.0
            return w * jnp.repeat(scale, GROUP, axis=1)

        def _qlora_linear(x, q, scale, bias, la, lb):
            w = _dequant(q, scale)
            base = jnp.einsum('btd,od->bto', x, w) + bias
            lora = jnp.einsum('btr,or->bto', jnp.einsum('btd,rd->btr', x, la), lb)
            return base + lora

        def _layernorm(x, g, b):
            mu = jnp.mean(x, axis=-1, keepdims=True)
            var = jnp.mean(jnp.square(x - mu), axis=-1, keepdims=True)
            return (x - mu) * jax.lax.rsqrt(var + EPS) * g + b
        h = x
        for blk in range(3):
            i0, i1 = (2 * blk, 2 * blk + 1)
            y = _qlora_linear(h, qweights[i0], scales[i0], biases[i0], lora_a[i0], lora_b[i0])
            y = _layernorm(y, ln_gamma[blk], ln_beta[blk])
            y = jax.nn.gelu(y, approximate=False)
            y = _qlora_linear(y, qweights[i1], scales[i1], biases[i1], lora_a[i1], lora_b[i1])
            h = y + h
        return h
    x = x + jnp.tanh(g_xattn[0]) * _L0_xattn_ref(_layernorm(x, axis=-1), ctx_768, L0_xattn_Wq, L0_xattn_bq, L0_xattn_Wkv, L0_xattn_bkv, L0_xattn_Wo, L0_xattn_bo)
    x = x + jnp.tanh(g_ffn[0]) * _L0_ffn_ref(_layernorm(x, axis=-1), L0_ffn_w1, L0_ffn_conv_w, L0_ffn_conv_b, L0_ffn_w2)
    x = x + jnp.tanh(g_xattn[1]) * _L1_xattn_ref(_layernorm(x, axis=-1), ctx_768, L1_xattn_w_q, L1_xattn_w_k, L1_xattn_w_v, L1_xattn_w_out, L1_xattn_b_out)
    x = x + jnp.tanh(g_ffn[1]) * _L1_ffn_ref(_layernorm(x, axis=-1), L1_ffn_router_w, L1_ffn_router_b, L1_ffn_expert_w, L1_ffn_expert_b)
    x = x + jnp.tanh(g_xattn[2]) * _L2_xattn_ref(_layernorm(x, axis=-1), ctx_768, L2_xattn_Wq, L2_xattn_bq, L2_xattn_Wk, L2_xattn_bk, L2_xattn_Wv, L2_xattn_bv, L2_xattn_Wo, L2_xattn_bo)
    x = x + jnp.tanh(g_ffn[2]) * _L2_ffn_ref(_layernorm(x, axis=-1), L2_ffn_n1_w, L2_ffn_qkv_w, L2_ffn_o_w, L2_ffn_n2_w, L2_ffn_gate_w, L2_ffn_up_w, L2_ffn_down_w)
    x = x + jnp.tanh(g_xattn[3]) * _L3_xattn_ref(_layernorm(x, axis=-1), ctx_768, ctx_768, L3_xattn_Wq, L3_xattn_bq, L3_xattn_Wk, L3_xattn_bk, L3_xattn_Wv, L3_xattn_bv, L3_xattn_Wo, L3_xattn_bo)
    x = x + jnp.tanh(g_ffn[3]) * _L3_ffn_ref(_layernorm(x, axis=-1), L3_ffn_qweights, L3_ffn_scales, L3_ffn_biases, L3_ffn_lora_a, L3_ffn_lora_b, L3_ffn_ln_gamma, L3_ffn_ln_beta)
    return x

_drawn_inputs = setup_inputs


def setup_inputs(seed=0):
    import zlib

    import numpy as np

    out = dict(_drawn_inputs(seed))
    spreads = {'L1_xattn_b_out': (0.0, 0.1),
     'L1_ffn_router_b': (0.0, 0.1),
     'L1_ffn_expert_b': (0.0, 0.285),
     'L2_xattn_bq': (0.0, 0.488),
     'L2_xattn_bk': (0.0, 0.8),
     'L2_xattn_bv': (0.0, 0.1),
     'L2_xattn_bo': (0.0, 0.1),
     'L2_ffn_n1_w': (1.0, 0.2),
     'L2_ffn_n2_w': (1.0, 0.2),
     'L3_ffn_ln_gamma': (1.0, 0.2),
     'L3_ffn_ln_beta': (0.0, 0.1)}
    factors = {'L0_xattn_bq': 8.0,
     'L0_xattn_bkv': 3.392,
     'L0_xattn_bo': 3.431,
     'L2_ffn_gate_w': 8.0,
     'L3_xattn_Wq': 2.963,
     'L3_xattn_bq': 8.0,
     'L3_xattn_Wk': 2.903,
     'L3_xattn_bk': 8.0,
     'L3_ffn_biases': 7.653,
     'L3_ffn_lora_a': 4.817,
     'L3_ffn_lora_b': 4.788}
    for name, (base, spread) in spreads.items():
        noise = np.random.default_rng([zlib.crc32(name.encode()), seed]).standard_normal(out[name].shape)
        drawn = base * np.exp(spread * noise) if base else spread * noise
        out[name] = jnp.asarray(drawn.astype(out[name].dtype))
    for name, factor in factors.items():
        out[name] = (out[name] * factor).astype(out[name].dtype)
    return out
```

```python
from contextlib import ExitStack

import numpy as np

import concourse.bass as bass
from concourse import mybir

F32 = mybir.dt.float32
BF16 = mybir.dt.bfloat16
I32 = mybir.dt.int32
ALU = mybir.AluOpType
ACT = mybir.ActivationFunctionType
AX = mybir.AxisListType

B, S, D, C = 32, 128, 256, 192
P = 128
KD = D // P
CC, KC = 96, 2
H = 16
CH = 4
BANK = 512
LANES_A, LANES_B = 4, 4
HID0, HID2, E1 = 1024, 1024, 8
LN_EPS, RMS_EPS = 1e-5, 1e-6
MAGIC = 1.5 * 2.0**23
MASKED = -1e9
GROUP, RANK, BLOCKS = 16, 32, 3

PAIRED = ["L0", "L2", "L3"]


class Mark:

    def __init__(self, engine, number):
        self.engine, self.number = engine, number


class Engine:

    def __init__(self, nc, queue, sem):
        self.nc, self.q, self.sem = nc, queue, sem
        self.count, self.loop, self.per_pass = 0, None, 0
        self.seen = {}

    def enter(self, sem, loop, per_pass):
        self.sem, self.loop, self.per_pass = sem, loop, per_pass
        self.count, self.seen = 0, {}

    def wait_apart(self, *marks):
        self.wait(*marks)
        self.q.sem_inc(self.passed, 1)

    def done(self, instruction):
        self.count += 1
        instruction.then_inc(self.sem, 1)
        return Mark(self, self.count)

    def wait(self, *marks):
        for m in marks:
            if m is None or self.seen.get(m.engine, -1) >= m.number:
                continue
            self.seen[m.engine] = m.number
            e = m.engine
            value = m.number if e.loop is None else e.loop * e.per_pass + m.number + 1
            self.q.wait_ge(e.sem, value)


def issue(lanes, hop=0.15):
    lanes = list(lanes)
    ends = {n: [0.0] for n in range(len(lanes))}
    ready = {n: 0.0 for n in range(len(lanes))}
    pe_free = dve_free = act_free = 0.0
    while ready:
        n = min(ready, key=lambda k: (max(ready[k], pe_free), ready[k], k))
        try:
            on_pe, on_dve, on_act, *back = next(lanes[n])
        except StopIteration:
            del ready[n]
            continue
        end = ready[n]
        if on_pe:
            end = pe_free = max(pe_free, end) + on_pe
        if on_dve:
            end = dve_free = max(dve_free, end + hop) + on_dve
        if on_act:
            end = act_free = max(act_free, end + hop) + on_act
        ends[n].append(end + hop)
        ready[n] = ends[n][-min(back[0] if back else 1, len(ends[n]))]


def build(nc, a, out, signals):
    ctx = ExitStack()
    with ctx:

        def sb(name, shape, dt=F32):
            return ctx.enter_context(nc.sbuf_tensor(name, shape, dt))

        def sem(name):
            return ctx.enter_context(nc.semaphore(name))

        scratch = nc.dram_tensor("after_L3_xattn", (B, S, D), F32, kind="Internal").ap()
        psum = ctx.enter_context(nc.psum_tensor("psum", [P, 8, BANK], F32))

        pe = Engine(nc, nc.tensor, sem("pe_setup"))
        dve = Engine(nc, nc.vector, sem("dve_setup"))
        act = Engine(nc, nc.scalar, sem("act_setup"))
        pool = Engine(nc, nc.gpsimd, sem("pool_setup"))
        engines = {"pe": pe, "dve": dve, "act": act, "pool": pool}
        for name, e in engines.items():
            e.passed = sem(name + "_passed")
        loop_sems = {(l, e): sem(f"{e}_{l}") for l in "ab" for e in engines}
        s_load = sem("s_load")
        loaded = [0]

        def load(dst, src):
            nc.sync.dma_start(dst, src).then_inc(s_load, 16)
            loaded[0] += 16

        ident = sb("ident", [P, P])
        ident_bf = sb("ident_bf", [P, P], BF16)
        ones = sb("ones", [P, P])
        head_rows = sb("head_rows", [P, 8])
        half_of = sb("half_of", [P, 2])
        causal = sb("causal", [P, P])
        minus_half = sb("minus_half", [P, 1])
        gates = sb("gates", [P, 8])
        first_of = sb("first_of", [P, E1])
        magic = sb("magic", [P, 2])

        load(gates[:, 0:4], a["g_xattn"].rearrange("(o n) -> o n", o=1).to_broadcast([P, 4]))
        load(gates[:, 4:8], a["g_ffn"].rearrange("(o n) -> o n", o=1).to_broadcast([P, 4]))

        w = {}

        def matrix(name, src, k, n, rows=P):
            w[name] = sb("w_" + name, [rows, k, n])
            load(w[name][:], src.rearrange("(k p) n -> p k n", k=k))

        def columns(name, src, n):
            w[name] = sb("w_" + name, [P, n])
            load(w[name][:], src)

        setup_ctx = ExitStack()

        def row(name, src, n):
            w[name] = setup_ctx.enter_context(nc.sbuf_tensor("w_" + name, [1, n], F32))
            load(w[name][:], src.rearrange("(o n) -> o n", o=1))

        for l in PAIRED:
            matrix(l + "q", a[l + "_wq"], KD, D)
            matrix(l + "k", a[l + "_wk"], KC, D, CC)
            matrix(l + "v", a[l + "_wv"], KC, D, CC)
            matrix(l + "o", a[l + "_wo"], KD, D)
            columns(l + "bq", a[l + "_bq"], KD)
            columns(l + "bk", a[l + "_bk"], KD)
        matrix("L1q", a["L1_wq"], KD, H * 64)
        matrix("L1k", a["L1_wk"], KC, H * 64, CC)
        matrix("L1v", a["L1_wv"], KC, H * 64, CC)
        matrix("L1o", a["L1_wo"], 8, D)
        matrix("router", a["L1_router"], KD, E1)
        matrix("experts", a["L1_experts"], KD, E1 * D)
        w["eb"] = sb("w_eb", [E1, D])
        load(w["eb"][:], a["L1_ffn_expert_b"])
        w["rb"] = sb("w_rb", [P, E1])
        load(w["rb"][:], a["L1_ffn_router_b"].rearrange("(o n) -> o n", o=1).to_broadcast([P, E1]))
        for n in "qkv":
            matrix("self" + n, a["L2s_w" + n], KD, D)
        matrix("selfo", a["L2s_wo"], KD, D)
        matrix("gate", a["L2s_gate"], KD, E1)
        matrix("up", a["L2s_up"], KD, HID2)
        matrix("down", a["L2s_down"], HID2 // P, D)
        w["conv"] = sb("w_conv", [P, HID0 // P, 3])
        load(w["conv"][:], a["L0_conv"].rearrange("(k p) t -> p k t", p=P))
        columns("convb", a["L0_convb"], HID0 // P)
        w["w1q"] = sb("w_w1q", [P, KD, HID0], BF16)
        w["w2q"] = sb("w_w2q", [P, HID0 // P, D], BF16)
        out_bias = {l: sb("out_bias_" + l, [P, D]) for l in ["L0", "L1", "L2", "L3"]}
        deq = sb("deq", [P, 2])

        for l in PAIRED:
            w[l + "bv"] = setup_ctx.enter_context(nc.sbuf_tensor(l + "bv", [P, KD], F32))
            load(w[l + "bv"][:], a[l + "_bv"])
        for l in PAIRED + ["L1"]:
            row(l + "bo", a[l + "_bo"], D)
        raw = [setup_ctx.enter_context(nc.sbuf_tensor(f"raw{n}", [P, HID0 * KD], F32)) for n in range(2)]
        load(raw[0][:].rearrange("p (k n) -> p k n", k=KD), a["L0_w1"].rearrange("(k p) n -> p k n", p=P))
        load(raw[1][:].rearrange("p (k n) -> p k n", n=D), a["L0_w2"].rearrange("(k p) n -> p k n", p=P))
        norms = setup_ctx.enter_context(nc.sbuf_tensor("norms", [P, 2, KD], F32))
        load(norms[:, 0, :], a["L2s_n1"])
        load(norms[:, 1, :], a["L2s_n2"])
        bvb = setup_ctx.enter_context(nc.sbuf_tensor("bvb", [P, len(PAIRED), KD, P], F32))
        absum = setup_ctx.enter_context(nc.sbuf_tensor("absum", [P, 4], F32))

        pool.q.memset(ident[:], 0.0)
        pool.q.memset(causal[:], 3.0e38)
        pool.q.memset(minus_half[:], -0.5)
        for r in range(2):
            dve.q.memset(half_of[0:64, r:r + 1], 1.0 - r)
            dve.q.memset(half_of[64:P, r:r + 1], 0.0 + r)
        pool.q.memset(magic[:, 0:1], MAGIC)
        pool.q.memset(magic[:, 1:2], -MAGIC)
        pool.q.memset(head_rows[:], 1.0)
        m = pool.done(pool.q.memset(ones[:], 1.0))
        pool.wait(m)
        pool.q.affine_select(out=ident[:], in_=ident[:], compare_op=ALU.not_equal, fill=1.0, base=0,
                             pattern=[[-1, P]], channel_multiplier=1)
        m = pool.done(pool.q.affine_select(out=causal[:], in_=causal[:], compare_op=ALU.is_ge, fill=4 * MASKED,
                                           base=0, pattern=[[-1, P]], channel_multiplier=1))
        pool.wait(m)
        m = pool.done(pool.q.affine_select(out=head_rows[:], in_=head_rows[:], compare_op=ALU.is_ge, fill=0.0, base=0,
                                           pattern=[[-16, 8]], channel_multiplier=1))
        pool.wait(m)
        consts_ready = pool.done(pool.q.affine_select(
            out=head_rows[:], in_=head_rows[:], compare_op=ALU.is_ge, fill=0.0, base=15, pattern=[[16, 8]],
            channel_multiplier=-1))
        dve.wait(consts_ready)
        dve_consts = dve.done(dve.q.tensor_copy(ident_bf[:], ident[:]))

        for e in (act, dve, pe):
            e.q.wait_ge(s_load, loaded[0])
        tanh_gates = act.done(act.q.activation(gates[:], gates[:], ACT.Tanh))
        dve.wait(tanh_gates)
        gx = {l: gates[:, n:n + 1] for n, l in enumerate(["L0", "L1", "L2", "L3"])}
        gf = {l: gates[:, 4 + n:5 + n] for n, l in enumerate(["L0", "L1", "L2", "L3"])}

        def scale(name, by):
            return dve.q.tensor_scalar(w[name][:], w[name][:], by, None, ALU.mult)

        for l in PAIRED + ["L1"]:
            scale(l + "o", gx[l])
            dve.q.tensor_scalar(w[l + "bo"][:], w[l + "bo"][:], gx[l][0:1], None, ALU.mult)
        scale("experts", gf["L1"])
        dve.q.tensor_scalar(w["eb"][:], w["eb"][:], gf["L1"][0:E1], None, ALU.mult)
        dve.q.tensor_scalar(w["down"][:], w["down"][:], gf["L2"], 0.5, ALU.mult, ALU.mult)
        for name, n in (("selfq", 0), ("selfk", 0), ("selfv", 0), ("gate", 1), ("up", 1)):
            for k in range(KD):
                dve.q.tensor_scalar(w[name][:, k, :], w[name][:, k, :], norms[:, n, k:k + 1], None, ALU.mult)
        for n, l in enumerate(PAIRED):
            for k in range(KD):
                last = dve.q.tensor_copy(bvb[:, n, k, :], w[l + "bv"][:, k:k + 1].to_broadcast([P, P]))
        for n in range(2):
            last = dve.q.tensor_reduce(absum[:, n:n + 1], raw[n][:], AX.X, ALU.add, apply_absolute_value=True)
        ready = dve.done(last)
        pe.wait(ready, consts_ready, dve_consts)
        for n, l in enumerate(PAIRED + ["L1"]):
            if l != "L1":
                for k in range(KD):
                    pe.q.matmul(psum[:, n, 0:D], bvb[:, n, k, :], w[l + "o"][:, k, :], start=k == 0, stop=False)
            last = pe.q.matmul(psum[:, n, 0:D], ones[0:1, :], w[l + "bo"][:], start=l == "L1", stop=True)
        last = pe.q.matmul(psum[:, 4, 0:2], ones[:], absum[:, 0:2], start=True, stop=True)
        ready = pe.done(last)
        dve.wait(ready)
        for n, l in enumerate(PAIRED + ["L1"]):
            dve.q.tensor_copy(out_bias[l][:], psum[:, n, 0:D])
        m = dve.done(dve.q.tensor_scalar(absum[:, 0:2], psum[:, 4, 0:2], 1.0 / (HID0 * D), 1e-5, ALU.mult, ALU.max))
        dve.wait(m)
        dve.q.tensor_scalar(deq[:, 0:1], absum[:, 0:1], 1.0 / 127.0, None, ALU.mult)
        dve.q.tensor_scalar(deq[:, 1:2], absum[:, 1:2], gf["L0"], 0.5 / 127.0, ALU.mult, ALU.mult)
        m = dve.done(dve.q.reciprocal(absum[:, 2:4], absum[:, 0:2]))
        dve.wait(m)
        for n in range(2):
            m = dve.done(dve.q.tensor_scalar(raw[n][:], raw[n][:], absum[:, 2 + n:3 + n], MAGIC, ALU.mult, ALU.add))
        dve.wait(m)
        for n in range(2):
            m = dve.done(dve.q.tensor_scalar(raw[n][:], raw[n][:], -MAGIC, 1.0, ALU.add, ALU.min))
        dve.wait(m)
        for n, name in enumerate(["w1q", "w2q"]):
            flat = w[name][:].rearrange("p k n -> p (k n)")
            weights_ready = dve.done(dve.q.tensor_scalar(flat, raw[n][:], -1.0, None, ALU.max))
        setup_ctx.close()

        class Lane:
            pass

        lane_ctx = ExitStack()

        def lane_buffers(n):
            t = Lane()

            def buf(name, shape, dt=F32):
                return lane_ctx.enter_context(nc.sbuf_tensor(f"{name}_{n}", shape, dt))

            t.n = n
            t.a, t.b = psum[:, 2 * n, :], psum[:, 2 * n + 1, :]
            t.x_in = buf("x_in", [P, D])
            t.ctxT = buf("ctxT", [CC, KC, S])
            t.x = buf("x", [P, D])
            t.xn = buf("xn", [P, D])
            t.xnT = buf("xnT", [P, KD, S])
            t.stats = buf("stats", [P, 6])
            t.mv = buf("mv", [P, 2])
            t.tiny = buf("tiny", [P, 64])
            big = buf("big", [P, 4 * BANK])
            t.e = [big[:, 0:BANK].rearrange("p (h s) -> p h s", h=CH), big[:, BANK:2 * BANK].rearrange("p (h s) -> p h s", h=CH)]
            t.eT = big[:, 2 * BANK:3 * BANK].rearrange("p (h s) -> p h s", h=CH)
            t.kT = big[:, 3 * BANK:4 * BANK].rearrange("p (k s) -> p k s", s=S)
            t.hid = big[:, 0:2 * BANK].rearrange("p (k s) -> p k s", s=S)
            t.act = big[:, 2 * BANK:4 * BANK].rearrange("p (k s) -> p k s", s=S)
            t.rounded = big[:, 0:2 * BANK]
            keys = buf("head_keys", [P, 2 * BANK])
            small = buf("small", [P, 2 * BANK + 32])
            t.qT = small[:, 0:D].rearrange("p (k s) -> p k s", s=S)
            t.o = t.un = small[:, D:2 * D]
            t.v = small[:, 2 * D:2 * D + H * 17]
            t.oT = small[:, 3 * D + 32:4 * D + 32].rearrange("p (k s) -> p k s", s=S)
            t.xi = small[:, 0:BANK].bitcast(BF16)
            t.xiT = small[:, BANK:2 * BANK].bitcast(BF16).rearrange("p (k s) -> p k s", s=S)
            t.diag, t.row_scale = t.act[:, 0, :], t.xnT[:, 0, :]
            t.wtT = t.un[0:E1, 0:S]
            t.head_keys = [keys[:, n * BANK:(n + 1) * BANK].rearrange("p (h s) -> p h s", h=CH) for n in range(2)]
            t.loaded_x, t.loaded_c = sem(f"loaded_x_{n}"), sem(f"loaded_c_{n}")
            t.stored = sem(f"stored_{n}")
            return t

        lanes = [lane_buffers(n) for n in range(LANES_A)]
        for t in lanes:
            nc.sync.wait_ge(dve.sem, weights_ready.number)
            nc.sync.dma_start(t.x_in[:], a["x"][t.n]).then_inc(t.loaded_x, 16)
            nc.sync.dma_start(t.ctxT[:], a["ctxT"][t.n].rearrange("(k p) s -> p k s", k=KC)).then_inc(t.loaded_c, 16)
        pe.wait(weights_ready)
        act.wait(weights_ready)
        pool.wait(weights_ready)

        def layernorm(t, src):
            m = dve.done(dve.q.bn_stats(t.stats[:], src))
            dve.wait_apart(m)
            m = dve.done(dve.q.bn_aggr(t.mv[:], t.stats[:]))
            dve.wait(m)
            m = dve.done(dve.q.tensor_scalar(t.tiny[:, 0:1], t.mv[:, 1:2], LN_EPS, None, ALU.add))
            pool.wait(m)
            m = pool.done(pool.q.tensor_tensor(t.tiny[:, 1:2], t.tiny[:, 0:1], minus_half[:], ALU.pow))
            dve.wait(m)
            return dve.done(dve.q.tensor_scalar(t.xn[:], src, t.mv[:, 0:1], t.tiny[:, 1:2],
                                                ALU.subtract, ALU.mult))

        def transposes(bank, src, chunks, identity=None):
            for k in range(chunks):
                last = pe.q.transpose(bank[:, k * P:(k + 1) * P], src[:, k * P:(k + 1) * P],
                                      ident[:] if identity is None else identity)
            return last

        def two_transposed(t, dst, src, src_ready):
            pe.wait(t.a_free, src_ready)
            m = pe.done(transposes(t.a, src, KD))
            act.wait(m)
            t.a_free = act.done(act.q.activation(dst[:], t.a[:, 0:D].rearrange("p (k s) -> p k s", s=S), ACT.Copy))
            return t.a_free

        def features_T(bank, wt, src, rows, outs):
            for j, n in enumerate(outs):
                for k in range(KD):
                    last = pe.q.matmul(bank[:, j * S:(j + 1) * S], wt[0:rows, k, n * P:(n + 1) * P],
                                       src[0:rows, k, :], start=k == 0, stop=k == KD - 1)
            return last

        def tokens(bank, srcT, wt, n, rows=P, chunks=KD, c0=0):
            for k in range(chunks):
                last = pe.q.matmul(bank[:, 0:n], srcT[0:rows, k, :], wt[0:rows, k, c0:c0 + n],
                                   start=k == 0, stop=k == chunks - 1)
            return last

        def softmax(t, c, scale, scores_ready, clip=None, masked=False):
            s4 = t.a.rearrange("p (h s) -> p h s", h=CH)
            dve.wait(scores_ready)
            if clip:
                dve.wait(dve.done(dve.q.tensor_scalar(t.a, t.a, clip / scale, -clip / scale, ALU.min, ALU.max)))
            if masked:
                dve.wait(dve.done(dve.q.tensor_tensor(s4, s4, causal[:].rearrange("p (o s) -> p o s", o=1)
                                                      .to_broadcast([P, CH, S]), ALU.min)))
            top = t.tiny[:, 8 + 4 * (c % 2):12 + 4 * (c % 2)]
            dve.wait(dve.done(dve.q.tensor_reduce(top, s4, AX.X, ALU.max)))
            t.a_free = dve.done(dve.q.tensor_tensor(t.e[c % 2], s4, top.rearrange("p (h o) -> p h o", o=1)
                                                    .to_broadcast([P, CH, S]), ALU.subtract))
            act.wait(t.a_free)
            flat = t.e[c % 2].rearrange("p h s -> p (h s)")
            return act.done(act.q.activation(flat, flat, ACT.Exp, scale=scale))

        def transposed_probabilities(t, c, e_ready):
            pe.wait(t.b_free, e_ready)
            m = pe.done(transposes(t.b, t.e[c % 2].rearrange("p h s -> p (h s)"), CH))
            act.wait(m)
            t.b_free = act.done(act.q.activation(t.eT.rearrange("p h s -> p (h s)"), t.b, ACT.Copy))
            return t.b_free

        def weighted_values(t, values, eT_ready):
            pe.wait(eT_ready)
            n = values[0].shape[-1]
            for j in range(CH):
                last = pe.q.matmul(t.b[:, j * n:(j + 1) * n], t.eT[:, j, :], values[j], start=True, stop=True)
            dve.wait(pe.done(last))
            got = t.b[:, 0:CH * n].rearrange("p (h d) -> p h d", h=CH)
            den = t.tiny[:, 32:32 + CH].rearrange("p (h o) -> p h o", o=1)
            dve.wait(dve.done(dve.q.reciprocal(den, got[:, :, n - 1:n])))
            return got[:, :, 0:n - 1], den

        def narrow_attention(t, l, x_ready, kv, kv_rows, clip=None, masked=False, kv_wait=None):
            dh = D // H
            v = t.v.rearrange("p (h d) -> p h d", h=H)
            pe.wait(t.a_free, x_ready)
            m = pe.done(features_T(t.a, w[l + "q"], t.xnT, P, range(KD)))
            act.wait(m)
            for k in range(KD):
                src = t.a[:, k * S:(k + 1) * S]
                if l == "self":
                    last = act.q.activation(t.qT[:, k, :], src, ACT.Copy)
                else:
                    last = act.q.activation(t.qT[:, k, :], src, ACT.Identity, bias=w[l + "bq"][:, k:k + 1])
            t.a_free = q_ready = act.done(last)
            yield 0.96, 0, 0.5
            if kv_wait:
                kv_wait()
            pe.wait(t.b_free)
            m = pe.done(features_T(t.b, w[l + "k"], kv, kv_rows, range(KD)))
            act.wait(m)
            for k in range(KD):
                src = t.b[:, k * S:(k + 1) * S]
                if l == "self":
                    last = act.q.activation(t.kT[:, k, :], src, ACT.Copy)
                else:
                    last = act.q.activation(t.kT[:, k, :], src, ACT.Identity, bias=w[l + "bk"][:, k:k + 1])
            t.b_free = k_ready = act.done(last)
            pool.wait_apart(q_ready)
            v_ones = pool.done(pool.q.memset(v[:, :, dh:dh + 1], 1.0))
            yield 0.96, 0, 0.5
            pe.wait(t.a_free)
            m = pe.done(tokens(t.a, kv, w[l + "v"], D, kv_rows))
            act.wait(m)
            t.a_free = v_ready = act.done(act.q.activation(
                v[:, :, 0:dh], t.a[:, 0:D].rearrange("p (h d) -> p h d", h=H), ACT.Copy))
            yield 0.9, 0, 0.35
            slot_read = [None, None]

            def keys_apart(c):
                pool.wait(k_ready, slot_read[c % 2])
                return pool.done(pool.q.tensor_tensor(
                    t.head_keys[c % 2], t.kT[:, c // 2:c // 2 + 1, :].to_broadcast([P, CH, S]),
                    head_rows[:, CH * (c % 2):CH * (c % 2 + 1)].rearrange("p (h o) -> p h o", o=1)
                    .to_broadcast([P, CH, S]), ALU.mult))

            def scores(c):
                pe.wait(t.a_free, q_ready, keys[c])
                slot_read[c % 2] = pe.done(pe.q.matmul(
                    t.a, t.qT[:, c // 2, :], t.head_keys[c % 2].rearrange("p h s -> p (h s)"), start=True, stop=True))
                return softmax(t, c, dh ** -0.5, slot_read[c % 2], clip, masked)

            keys = {0: keys_apart(0), 1: keys_apart(1)}
            e_ready = [scores(0), None]
            yield 0.9, 1.2, 0.5
            pe.wait(v_ready, v_ones)
            for c in range(4):
                if c + 1 < 4:
                    e_ready[(c + 1) % 2] = scores(c + 1)
                    if c + 2 < 4:
                        keys[c + 2] = keys_apart(c + 2)
                    yield 0.9, 1.2, 0.5, 2
                eT_ready = transposed_probabilities(t, c, e_ready[c % 2])
                yield 0.6, 0, 0.5
                got, den = weighted_values(t, [v[:, CH * c + j, :] for j in range(CH)], eT_ready)
                t.b_free = dve.done(dve.q.tensor_tensor(
                    t.o[:, CH * dh * c:CH * dh * (c + 1)].rearrange("p (h d) -> p h d", h=CH), got,
                    den.to_broadcast([P, CH, dh]), ALU.mult))
                yield 0.57, 0.4, 0, 3 if c < 2 else 1
            oT_ready = two_transposed(t, t.oT, t.o, t.b_free)
            yield 0.3, 0, 0.35
            pe.wait(t.b_free, oT_ready)
            t.result_ready = pe.done(tokens(t.b, t.oT, w[l + "o"], D))

        def wide_attention(t, x_ready, kv, kv_rows):
            dh = 64
            v = t.v[:, 0:CH * (dh + 1)].rearrange("p (h d) -> p h d", h=CH)
            o3 = t.o.rearrange("p (h d) -> p h d", h=CH)
            pool.wait_apart(x_ready)
            v_ones = pool.done(pool.q.memset(v[:, :, dh:dh + 1], 1.0))
            for g in range(4):
                pe.wait(t.a_free, x_ready)
                m = pe.done(features_T(t.a, w["L1q"], t.xnT, P, range(2 * g, 2 * g + 2)))
                act.wait(m)
                t.a_free = q_ready = act.done(act.q.activation(
                    t.qT, t.a[:, 0:D].rearrange("p (k s) -> p k s", s=S), ACT.Copy))
                yield 0.96, 0, 0.35
                pe.wait(t.b_free)
                m = pe.done(features_T(t.b, w["L1k"], kv, kv_rows, range(2 * g, 2 * g + 2)))
                dve.wait(m)
                kT4 = t.kT.rearrange("p (k r) s -> p k r s", r=2)
                for r in range(2):
                    last = dve.q.tensor_scalar(kT4[:, :, r, :], t.b[:, 0:D].rearrange("p (k s) -> p k s", s=S),
                                               half_of[:, r:r + 1], None, ALU.mult)
                t.b_free = k_ready = dve.done(last)
                yield 0.96, 0.6, 0
                pe.wait(t.a_free, q_ready, k_ready)
                for k in range(2):
                    last = pe.q.matmul(t.a[:, 2 * k * S:2 * (k + 1) * S], t.qT[:, k, :],
                                       t.kT[:, 2 * k:2 * k + 2, :].rearrange("p k s -> p (k s)"), start=True, stop=True)
                e_ready = softmax(t, g, dh ** -0.5, pe.done(last))
                yield 0.9, 1.2, 0.5
                pe.wait(t.b_free)
                m = pe.done(tokens(t.b, kv, w["L1v"], CH * dh, kv_rows, c0=g * CH * dh))
                act.wait(m)
                t.b_free = v_ready = act.done(act.q.activation(
                    v[:, :, 0:dh], t.b[:, 0:CH * dh].rearrange("p (h d) -> p h d", h=CH), ACT.Copy))
                yield 0.9, 0, 0.35, 2
                eT_ready = transposed_probabilities(t, g, e_ready)
                yield 0.6, 0, 0.5
                pe.wait(v_ready, v_ones)
                got, den = weighted_values(t, [v[:, j, :] for j in range(CH)], eT_ready)
                t.b_free = dve.done(dve.q.tensor_tensor(o3, got, den.to_broadcast([P, CH, dh]), ALU.mult))
                yield 0.6, 0.6, 0
                oT_ready = two_transposed(t, t.oT, t.o, t.b_free)
                yield 0.3, 0, 0.35
                pe.wait(t.b_free, oT_ready)
                for k in range(2):
                    last = pe.q.matmul(t.b[:, 0:D], t.oT[:, k, :], w["L1o"][:, 2 * g + k, :], start=k == 0, stop=k == 1)
                t.result_ready = pe.done(last)
                if g < 3:
                    dve.wait(t.result_ready, t.x_ready)
                    t.b_free = t.x_ready = dve.done(dve.q.tensor_tensor(t.x[:], t.b[:, 0:D], t.x[:], ALU.add))
                    yield 0.9, 0.35, 0

        def cross_attention(t, l, src, clip=None, kv_wait=None):
            m = layernorm(t, src)
            pool.wait(m)
            t.x_ready = t.x_in_free = pool.done(pool.q.tensor_tensor(t.x[:], src, out_bias[l][:], ALU.add))
            yield 0, 1.5, 0
            xnT_ready = two_transposed(t, t.xnT, t.xn, m)
            yield 0.3, 0, 0.35
            if l == "L1":
                yield from wide_attention(t, xnT_ready, t.ctxT, CC)
            else:
                yield from narrow_attention(t, l, xnT_ready, t.ctxT, CC, clip=clip, kv_wait=kv_wait)
            dve.wait(t.result_ready, t.x_ready)
            t.b_free = t.x_ready = dve.done(dve.q.tensor_tensor(t.x[:], t.b[:, 0:D], t.x[:], ALU.add))
            dve.wait(t.x_ready)
            yield 0.9, 0.35, 0

        def bitlinear_ffn(t):
            mx, rs, sc = t.tiny[:, 2:3], t.tiny[:, 3:4], t.tiny[:, 4:5]
            m = layernorm(t, t.x[:])
            dve.wait(m)
            dve.wait(dve.done(dve.q.tensor_reduce(mx, t.xn[:], AX.X, ALU.max, apply_absolute_value=True)))
            dve.wait(dve.done(dve.q.tensor_scalar(mx, mx, 1e-5, None, ALU.max)))
            dve.wait(dve.done(dve.q.reciprocal(rs, mx)))
            dve.wait(dve.done(dve.q.tensor_scalar(rs, rs, 127.0, None, ALU.mult)))
            dve.wait(dve.done(dve.q.tensor_scalar(t.rounded[:, 0:D], t.xn[:], rs, MAGIC, ALU.mult, ALU.add)))
            xi_ready = dve.done(dve.q.tensor_scalar(t.xi[:, 0:D], t.rounded[:, 0:D], -MAGIC, None, ALU.add))
            dve.wait(dve.done(dve.q.tensor_scalar(sc, mx, deq[:, 0:1], None, ALU.mult)))
            diag_ready = dve.done(dve.q.tensor_scalar(t.diag, ident[:], sc, None, ALU.mult))
            yield 0, 3.0, 0
            bf = t.a[:, 0:P].bitcast(BF16)
            pe.wait(t.a_free, xi_ready)
            m = pe.done(transposes(bf, t.xi, KD, ident_bf[:]))
            act.wait(m)
            t.a_free = xiT_ready = act.done(act.q.activation(t.xiT[:, 0:KD, :], bf.rearrange("p (k s) -> p k s", k=KD),
                                                             ACT.Copy))
            pe.wait(t.b_free, diag_ready)
            m = pe.done(pe.q.matmul(t.b[:, 0:S], ones[:], t.diag, start=True, stop=True))
            act.wait(m)
            t.b_free = rows_ready = act.done(act.q.activation(t.row_scale, t.b[:, 0:S], ACT.Copy))
            yield 0.35, 0, 0.6
            centre = []
            for half, bank in enumerate((t.a, t.b)):
                ks = range(4 * half, 4 * half + 4)
                pe.wait(xiT_ready, (t.a_free, t.b_free)[half])
                m = pe.done(features_T(bank, w["w1q"], t.xiT, P, ks))
                dve.wait(m, rows_ready)
                m = dve.done(dve.q.tensor_tensor(
                    t.hid[:, 4 * half:4 * half + 4, :], bank.rearrange("p (k s) -> p k s", s=S),
                    t.row_scale.rearrange("p (o s) -> p o s", o=1).to_broadcast([P, 4, S]), ALU.mult))
                if half == 0:
                    t.a_free = m
                else:
                    t.b_free = m
                act.wait(m)
                for k in ks:
                    m = act.q.activation(t.act[:, k, :], t.hid[:, k, :], ACT.Identity,
                                         bias=w["convb"][:, k:k + 1], scale=w["conv"][:, k, 1:2])
                centre.append(act.done(m))
                yield 0.65, 0.6, 1.2
            silu_ready = []
            for half in range(2):
                ks = range(4 * half, 4 * half + 4)
                sl = slice(4 * half, 4 * half + 4)
                dve.wait(centre[half])
                for k in ks:
                    m = dve.done(dve.q.scalar_tensor_tensor(
                        t.act[:, k, 1:S], t.hid[:, k, 0:S - 1], w["conv"][:, k, 0:1], t.act[:, k, 1:S],
                        ALU.mult, ALU.add))
                dve.wait(m)
                for k in ks:
                    m = dve.q.scalar_tensor_tensor(
                        t.act[:, k, 0:S - 1], t.hid[:, k, 1:S], w["conv"][:, k, 2:3], t.act[:, k, 0:S - 1],
                        ALU.mult, ALU.add)
                conv_ready = dve.done(m)
                act.wait(conv_ready)
                m = act.done(act.q.activation(t.hid[:, sl, :], t.act[:, sl, :], ACT.Tanh, scale=0.5))
                dve.wait(m, conv_ready)
                silu_ready.append(dve.done(dve.q.scalar_tensor_tensor(
                    t.act[:, sl, :], t.hid[:, sl, :], 1.0, t.act[:, sl, :], ALU.add, ALU.mult)))
                yield 0, 2.3, 0.5
            for half, bank in enumerate((t.a, t.b)):
                pe.wait(silu_ready[half], (t.a_free, t.b_free)[half])
                m = pe.done(transposes(bank, t.act[:, 4 * half:4 * half + 4, :].rearrange("p k s -> p (k s)"), 4))
                dve.wait(m)
                m = dve.done(dve.q.tensor_reduce(t.tiny[:, 5 + half:6 + half], bank, AX.X, ALU.max,
                                                 apply_absolute_value=True))
                yield 0.6, 0.6, 0
            dve.wait(m)
            dve.wait(dve.done(dve.q.tensor_tensor(mx, t.tiny[:, 5:6], t.tiny[:, 6:7], ALU.max)))
            dve.wait(dve.done(dve.q.tensor_scalar(mx, mx, 2e-5, None, ALU.max)))
            dve.wait(dve.done(dve.q.reciprocal(rs, mx)))
            rs_ready = dve.done(dve.q.tensor_scalar(rs, rs, 127.0, None, ALU.mult))
            sc_ready = dve.done(dve.q.tensor_scalar(sc, mx, deq[:, 1:2], None, ALU.mult))
            yield 0, 0.8, 0
            for half, bank in enumerate((t.a, t.b)):
                cols = slice(half * BANK, (half + 1) * BANK)
                act.wait(rs_ready)
                m = act.done(act.q.activation(t.rounded[:, cols], bank, ACT.Identity, bias=magic[:, 0:1], scale=rs))
                dve.wait(m)
                xi_ready = dve.done(dve.q.tensor_scalar(t.xi[:, cols], t.rounded[:, cols], -MAGIC, None, ALU.add))
                bf = bank[:, 0:2 * P].bitcast(BF16)
                pe.wait(m, xi_ready)
                m = pe.done(transposes(bf, t.xi[:, cols], 4, ident_bf[:]))
                act.wait(m)
                xiT_ready = act.done(act.q.activation(t.xiT[:, 4 * half:4 * half + 4, :],
                                                      bf.rearrange("p (k s) -> p k s", k=4), ACT.Copy))
                if half == 0:
                    t.a_free = xiT_ready
                else:
                    t.b_free = xiT_ready
                yield 0.3, 0.35, 0.9
            pe.wait(xiT_ready)
            m = pe.done(tokens(t.a, t.xiT, w["w2q"], D, chunks=HID0 // P))
            dve.wait(m, sc_ready)
            t.a_free = t.x_ready = dve.done(dve.q.scalar_tensor_tensor(t.x[:], t.a[:, 0:D], sc, t.x[:],
                                                                       ALU.mult, ALU.add))
            dve.wait(t.x_ready)
            yield 1.0, 0.35, 0

        def moe_ffn(t):
            xn_ready = layernorm(t, t.x[:])
            yield 0, 1.5, 0
            xnT_ready = two_transposed(t, t.xnT, t.xn, xn_ready)
            yield 0.3, 0, 0.35
            pe.wait(t.b_free, xnT_ready)
            m = pe.done(tokens(t.b, t.xnT, w["router"], E1))
            lg, ex, wt, mx, sm = t.tiny[:, 8:16], t.tiny[:, 16:24], t.tiny[:, 24:32], t.tiny[:, 2:3], t.tiny[:, 3:4]
            dve.wait(m)
            t.b_free = m = dve.done(dve.q.tensor_tensor(lg, t.b[:, 0:E1], w["rb"][:], ALU.add))
            dve.wait(m)
            dve.wait(dve.done(dve.q.tensor_reduce(mx, lg, AX.X, ALU.max)))
            m = dve.done(dve.q.tensor_scalar(lg, lg, mx, None, ALU.subtract))
            act.wait(m)
            exp_ready = act.done(act.q.activation(ex, lg, ACT.Exp, accum_out=sm))
            dve.wait(m)
            dve.wait(dve.done(dve.q.scalar_tensor_tensor(wt, lg, 0.0, first_of[:], ALU.is_equal, ALU.mult)))
            dve.wait(dve.done(dve.q.tensor_reduce(mx, wt, AX.X, ALU.max)))
            dve.wait(exp_ready)
            dve.wait(dve.done(dve.q.reciprocal(sm, sm)))
            wt_ready = dve.done(dve.q.tensor_scalar(wt, wt, mx, sm, ALU.is_equal, ALU.mult))
            yield 0.3, 1.2, 0.3
            pe.wait(t.b_free, wt_ready)
            m = pe.done(pe.q.transpose(t.b[0:E1, 0:P], wt, ident[:]))
            act.wait(m)
            t.b_free = wtT_ready = act.done(act.q.activation(t.wtT, t.b[0:E1, 0:P], ACT.Copy))
            yield 0.15, 0, 0.2
            for pair in range(E1 // 2):
                bank = (t.a, t.b)[pair % 2]
                pe.wait((t.a_free, t.b_free)[pair % 2])
                m = pe.done(tokens(bank, t.xnT, w["experts"], BANK, c0=pair * BANK))
                dve.wait(m, wt_ready)
                for j in range(2):
                    e = 2 * pair + j
                    m = dve.done(dve.q.scalar_tensor_tensor(t.x[:], bank[:, j * D:(j + 1) * D], wt[:, e:e + 1], t.x[:],
                                                            ALU.mult, ALU.add))
                    dve.wait(m)
                if pair % 2 == 0:
                    t.a_free = m
                else:
                    t.b_free = m
                yield 1.8, 0.7, 0, 2
            pe.wait(t.a_free, wtT_ready)
            m = pe.done(pe.q.matmul(t.a[:, 0:D], t.wtT, w["eb"][:], start=True, stop=True))
            dve.wait(m)
            t.a_free = t.x_ready = dve.done(dve.q.tensor_tensor(t.x[:], t.a[:, 0:D], t.x[:], ALU.add))
            dve.wait(t.x_ready)
            yield 0.45, 0.35, 0

        def transformer_ffn(t):
            u_ready = layernorm(t, t.x[:])
            ms, rr, f1, f2 = t.tiny[:, 2:3], t.tiny[:, 3:4], t.tiny[:, 4:5], t.tiny[:, 5:6]
            u, un = t.xn, t.un
            dve.wait(u_ready)

            def rms(ready):
                act.wait(ready)
                m = act.done(act.q.activation(un, u[:], ACT.Square, accum_out=ms))
                pool.wait_apart(m)
                m = pool.done(pool.q.tensor_scalar(rr, ms, 1.0 / D, RMS_EPS, ALU.mult, ALU.add))
                pool.wait(m)
                m = pool.done(pool.q.tensor_tensor(f1, rr, minus_half[:], ALU.pow))
                dve.wait(m)
                return dve.done(dve.q.tensor_scalar(un, u[:], f1, None, ALU.mult))

            un_ready = rms(u_ready)
            yield 0, 2.5, 0.3
            unT_ready = two_transposed(t, t.xnT, un, un_ready)
            yield 0.3, 0, 0.35
            yield from narrow_attention(t, "self", unT_ready, t.xnT, P, masked=True)
            dve.wait(t.result_ready)
            t.b_free = u_ready = dve.done(dve.q.tensor_tensor(u[:], t.b[:, 0:D], u[:], ALU.add))
            un_ready = rms(u_ready)
            dve.wait(u_ready)
            x_u = dve.done(dve.q.scalar_tensor_tensor(t.x[:], u[:], gf["L2"], t.x[:], ALU.mult, ALU.add))
            yield 0.9, 1.0, 0.4
            unT_ready = two_transposed(t, t.xnT, un, un_ready)
            yield 0.3, 0, 0.35
            pe.wait(t.b_free, unT_ready)
            m = pe.done(tokens(t.b, t.xnT, w["gate"], E1))
            lg, top, sm = t.tiny[:, 8:16], t.tiny[:, 16:24], t.tiny[:, 6:7]
            dve.wait(m)
            dve.wait(dve.done(dve.q.tensor_reduce(sm, t.b[:, 0:E1], AX.X, ALU.max)))
            t.b_free = m = dve.done(dve.q.tensor_scalar(lg, t.b[:, 0:E1], sm, None, ALU.subtract))
            act.wait(m)
            m = act.done(act.q.activation(lg, lg, ACT.Exp, accum_out=sm))
            dve.wait_apart(m)
            dve.wait(dve.done(dve.q.max(top, lg)))
            dve.wait(dve.done(dve.q.reciprocal(sm, sm)))
            dve.wait(dve.done(dve.q.tensor_scalar(top[:, 0:2], top[:, 0:2], sm, None, ALU.mult)))
            dve.wait(dve.done(dve.q.tensor_tensor(rr, top[:, 0:1], top[:, 1:2], ALU.add)))
            dve.wait(dve.done(dve.q.tensor_scalar(f1, rr, 1e-9, None, ALU.add)))
            dve.wait(dve.done(dve.q.reciprocal(f2, f1)))
            f_ready = dve.done(dve.q.tensor_scalar(f2, f2, rr, None, ALU.mult))
            yield 0.3, 1.6, 0.3, 2
            silu_ready = []
            for half, bank in enumerate((t.a, t.b)):
                pe.wait(unT_ready, (t.a_free, t.b_free)[half])
                m = pe.done(features_T(bank, w["up"], t.xnT, P, range(4 * half, 4 * half + 4)))
                act.wait(m)
                view = bank.rearrange("p (k s) -> p k s", s=S)
                sl = slice(4 * half, 4 * half + 4)
                m = act.done(act.q.activation(t.hid[:, sl, :], view, ACT.Tanh, scale=0.5))
                dve.wait(m)
                m = dve.done(dve.q.scalar_tensor_tensor(t.act[:, sl, :], t.hid[:, sl, :], 1.0, view, ALU.add, ALU.mult))
                silu_ready.append(m)
                yield 1.9, 0.6, 0.5
            t.a_free, t.b_free = silu_ready
            pe.wait(*silu_ready)
            m = pe.done(tokens(t.a, t.act, w["down"], D, chunks=HID2 // P))
            dve.wait(m, f_ready, x_u)
            t.a_free = t.x_ready = dve.done(dve.q.scalar_tensor_tensor(t.x[:], t.a[:, 0:D], f2, t.x[:],
                                                                       ALU.mult, ALU.add))
            dve.wait(t.x_ready)
            yield 3.6, 0.35, 0

        for e in range(E1):
            m = pool.q.memset(first_of[:, e:e + 1], float(E1 - e))
        first_ready = pool.done(m)
        dve.wait(first_ready)
        pe.wait(consts_ready, dve_consts)
        act.wait(consts_ready)

        passes_a = B // LANES_A
        for name, e in engines.items():
            e.q.sem_inc(loop_sems["a", name], 1)
        for t in lanes:
            nc.sync.sem_inc(t.stored, 1)
        with nc.Fori(0, passes_a) as i:
            for name, e in engines.items():
                e.enter(loop_sems["a", name], i, signals.get(("a", name), 1))

            def lane_a(t):
                t.a_free = t.b_free = None
                for e in (dve, pool):
                    e.q.wait_ge(t.loaded_x, 16 * i + 16)
                    e.q.wait_ge(t.stored, 16 * i + 1)

                def context_loaded():
                    pe.q.wait_ge(t.loaded_c, 16 * i + 16)

                yield from cross_attention(t, "L0", t.x_in[:], kv_wait=context_loaded)
                nc.sync.wait_ge(pool.sem, i * pool.per_pass + t.x_in_free.number + 1)
                nc.sync.dma_start(t.x_in[:], a["x"][(i + 1) % passes_a * LANES_A + t.n]).then_inc(t.loaded_x, 16)
                yield from bitlinear_ffn(t)
                yield from cross_attention(t, "L1", t.x[:])
                yield from moe_ffn(t)
                yield from cross_attention(t, "L2", t.x[:], clip=10000.0)
                yield from transformer_ffn(t)
                yield from cross_attention(t, "L3", t.x[:])
                nc.sync.wait_ge(dve.sem, i * dve.per_pass + t.x_ready.number + 1)
                nc.sync.dma_start(scratch[i * LANES_A + t.n], t.x[:]).then_inc(t.stored, 16)
                nc.sync.dma_start(t.ctxT[:], a["ctxT"][(i + 1) % passes_a * LANES_A + t.n]
                                  .rearrange("(k p) s -> p k s", k=KC)).then_inc(t.loaded_c, 16)

            issue(lane_a(t) for t in lanes)
            for name, e in engines.items():
                signals["a", name] = e.count

        for t in lanes:
            for q in (nc.sync, nc.vector):
                q.wait_ge(t.loaded_x, 16 * (passes_a + 1))
                q.wait_ge(t.loaded_c, 16 * (passes_a + 1))
                q.wait_ge(t.stored, 16 * passes_a + 1)
        a_done = {name: (loop_sems["a", name], passes_a * signals["a", name] + 1) for name in engines}
        for e in list(engines.values()):
            for s, v in a_done.values():
                e.q.wait_ge(s, v)
        for s, v in a_done.values():
            nc.sync.wait_ge(s, v)
        lane_ctx.close()

        bctx = ExitStack()
        lane_ctx = bctx

        def sb2(name, shape, dt=F32):
            return bctx.enter_context(nc.sbuf_tensor(name, shape, dt))

        NL = 2 * BLOCKS
        s_load_b = sem("s_load_b")
        wl = sb2("wl", [P, NL, KD, D])
        qw = sb2("qw", [P, NL, KD, D], I32)
        sct = sb2("sct", [P, NL, KD, D])
        la = sb2("la", [RANK, NL, D])
        lb = sb2("lb", [RANK, NL, D])
        bias = sb2("bias", [1, NL, D])
        gamma = sb2("gamma", [P, BLOCKS, KD])
        beta = sb2("beta", [P, BLOCKS, KD])
        nb = [0]

        def load_b(dst, src):
            nc.sync.dma_start(dst, src).then_inc(s_load_b, 16)
            nb[0] += 16

        for n in range(NL):
            load_b(qw[:, n], a["L3_q"][n].rearrange("(k p) o -> p k o", p=P))
            for k in range(KD):
                for g in range(P // GROUP):
                    load_b(sct[g * GROUP:(g + 1) * GROUP, n, k, :],
                           a["L3_s"][n, k * (P // GROUP) + g:k * (P // GROUP) + g + 1, :].to_broadcast([GROUP, D]))
        load_b(la[:], a["L3_la"].rearrange("n r d -> r n d"))
        load_b(lb[:], a["L3_lb"].rearrange("n r o -> r n o"))
        load_b(bias[:], a["L3_ffn_biases"].rearrange("(u n) o -> u n o", u=1))
        load_b(gamma[:], a["L3_gamma"])
        load_b(beta[:], a["L3_beta"])
        for e in (pe, dve, act):
            e.q.wait_ge(s_load_b, nb[0])
        setup_b = {name: sem(f"{name}_setup_b") for name in engines}
        for name, e in engines.items():
            e.enter(setup_b[name], None, 0)
        m = dve.done(dve.q.tensor_scalar(wl[:], qw[:], 1.0 / 7.5, -1.0, ALU.mult, ALU.add))
        dve.wait(m)
        base_ready = dve.done(dve.q.tensor_tensor(wl[:], wl[:], sct[:], ALU.mult))
        for n in range(NL):
            for k in range(KD):
                last = pe.q.matmul(psum[:, n, k * D:(k + 1) * D], la[:, n, k * P:(k + 1) * P], lb[:, n, :],
                                   start=True, stop=True)
        m = pe.done(last)
        dve.wait(m, base_ready)
        for n in range(NL):
            flat = wl[:, n].rearrange("p k o -> p (k o)")
            wl_ready = dve.done(dve.q.tensor_tensor(flat, flat, psum[:, n, :], ALU.add))

        lanes_b = []
        for n in range(LANES_B):
            t = Lane()
            t.n = n
            t.x_in = sb2(f"bx_in_{n}", [P, D])
            t.x = sb2(f"bx_{n}", [P, D])
            t.h = sb2(f"bh_{n}", [P, D])
            t.out = sb2(f"bout_{n}", [P, D])
            t.xn = sb2(f"bxn_{n}", [P, D])
            t.hT = sb2(f"bhT_{n}", [P, KD, S])
            t.yT = sb2(f"byT_{n}", [P, KD, S])
            t.stats = sb2(f"bstats_{n}", [P, 6])
            t.mv = sb2(f"bmv_{n}", [P, 2])
            t.tiny = sb2(f"btiny_{n}", [P, 4])
            t.a, t.b = psum[:, 2 * n, :], psum[:, 2 * n + 1, :]
            t.loaded, t.stored = sem(f"b_loaded_{n}"), sem(f"b_stored_{n}")
            nc.sync.dma_start(t.x_in[:], scratch[n]).then_inc(t.loaded, 16)
            lanes_b.append(t)
        pe.wait(wl_ready)
        act.wait(wl_ready)
        pool.wait(wl_ready)
        passes_b = B // LANES_B
        for name, e in engines.items():
            e.q.sem_inc(loop_sems["b", name], 1)
        for t in lanes_b:
            nc.sync.sem_inc(t.stored, 1)
        with nc.Fori(0, passes_b) as i:
            for name, e in engines.items():
                e.enter(loop_sems["b", name], i, signals.get(("b", name), 1))

            def linear(t, n, srcT, ready):
                pe.wait(t.b_free, ready)
                pe.q.matmul(t.b[:, 0:D], ones[0:1, :], bias[:, n, :], start=True, stop=False)
                for k in range(KD):
                    last = pe.q.matmul(t.b[:, 0:D], srcT[:, k, :], wl[:, n, k, :], start=False, stop=k == KD - 1)
                return pe.done(last)

            def lane_b(t):
                t.a_free = t.b_free = None
                dve.q.wait_ge(t.loaded, 16 * i + 16)
                m = dve.done(dve.q.tensor_copy(t.x[:], t.x_in[:]))
                dve.wait(m)
                xn_free = layernorm(t, t.x_in[:])
                nc.sync.wait_ge(dve.sem, i * dve.per_pass + xn_free.number + 1)
                nc.sync.dma_start(t.x_in[:], scratch[(i + 1) % passes_b * LANES_B + t.n]).then_inc(t.loaded, 16)
                dve.wait(xn_free)
                h_ready = dve.done(dve.q.tensor_copy(t.h[:], t.xn[:]))
                yield 0, 2, 0
                for blk in range(BLOCKS):
                    hT_ready = two_transposed(t, t.hT, t.h, h_ready)
                    yield 0.3, 0, 0.35
                    y = linear(t, 2 * blk, t.hT, hT_ready)
                    dve.wait(y)
                    t.b_free = m = layernorm(t, t.b[:, 0:D])
                    yield 1.2, 1.5, 0
                    pe.wait(t.a_free, m)
                    m = pe.done(transposes(t.a, t.xn, KD))
                    act.wait(m)
                    for k in range(KD):
                        m = act.q.activation(t.yT[:, k, :], t.a[:, k * P:(k + 1) * P], ACT.Gelu,
                                             scale=gamma[:, blk, k:k + 1], bias=beta[:, blk, k:k + 1])
                    t.a_free = m = act.done(m)
                    yield 0.3, 0, 0.6
                    y = linear(t, 2 * blk + 1, t.yT, m)
                    dve.wait(y, h_ready)
                    t.b_free = h_ready = dve.done(dve.q.tensor_tensor(t.h[:], t.b[:, 0:D], t.h[:], ALU.add))
                    yield 1.2, 0.35, 0
                dve.wait(h_ready)
                dve.q.wait_ge(t.stored, 16 * i + 1)
                m = dve.done(dve.q.scalar_tensor_tensor(t.out[:], t.h[:], gf["L3"], t.x[:], ALU.mult, ALU.add))
                nc.sync.wait_ge(dve.sem, i * dve.per_pass + m.number + 1)
                nc.sync.dma_start(out[i * LANES_B + t.n], t.out[:]).then_inc(t.stored, 16)

            issue(lane_b(t) for t in lanes_b)
            for name, e in engines.items():
                signals["b", name] = e.count
        for t in lanes_b:
            nc.sync.wait_ge(t.loaded, 16 * (passes_b + 1))
            nc.sync.wait_ge(t.stored, 16 * passes_b + 1)
        bctx.close()


_OUT = (B, S, D)


def kernel(**inputs):
    import concourse.bacc as bacc
    from concourse.bass_utils import run_bass_kernel_spmd

    x = {n: np.asarray(v) for n, v in inputs.items()}
    c = np.ascontiguousarray
    arrays = {n: c(x[n]) for n in (
        "x", "g_xattn", "g_ffn", "L1_ffn_router_b", "L1_ffn_expert_b", "L3_ffn_biases")}

    def columns(v):
        v = v.reshape(*v.shape[:-1], -1, P)
        return c(np.moveaxis(v, -1, 0))

    arrays["ctxT"] = c(x["ctx_768"].transpose(0, 2, 1))
    kv = x["L0_xattn_Wkv"].reshape(H, 2, D // H, C)
    bkv = x["L0_xattn_bkv"].reshape(H, 2, D // H)
    arrays["L0_wq"] = c(x["L0_xattn_Wq"].T)
    arrays["L0_bq"] = columns(x["L0_xattn_bq"])
    arrays["L0_wk"], arrays["L0_wv"] = (c(kv[:, n].reshape(D, C).T) for n in range(2))
    arrays["L0_bk"], arrays["L0_bv"] = (columns(bkv[:, n].reshape(D)) for n in range(2))
    arrays["L0_wo"] = c(x["L0_xattn_Wo"].T)
    arrays["L0_bo"] = c(x["L0_xattn_bo"])
    for l in ("L2", "L3"):
        for n in "qkvo":
            arrays[f"{l}_w{n}"] = c(x[f"{l}_xattn_W{n}"])
            arrays[f"{l}_b{n}"] = (c if n == "o" else columns)(x[f"{l}_xattn_b{n}"])
    arrays["L1_wq"], arrays["L1_wk"], arrays["L1_wv"] = (c(x["L1_xattn_w_" + n]) for n in "qkv")
    arrays["L1_wo"], arrays["L1_bo"] = c(x["L1_xattn_w_out"]), c(x["L1_xattn_b_out"])
    arrays["L1_router"] = c(x["L1_ffn_router_w"])
    arrays["L1_experts"] = c(x["L1_ffn_expert_w"].transpose(1, 0, 2).reshape(D, E1 * D))
    arrays["L0_w1"], arrays["L0_w2"] = c(x["L0_ffn_w1"].T), c(x["L0_ffn_w2"].T)
    arrays["L0_convb"] = columns(x["L0_ffn_conv_b"])
    arrays["L2s_n1"], arrays["L2s_n2"] = columns(x["L2_ffn_n1_w"]), columns(x["L2_ffn_n2_w"])
    arrays["L3_gamma"], arrays["L3_beta"] = columns(x["L3_ffn_ln_gamma"]), columns(x["L3_ffn_ln_beta"])
    arrays["L0_conv"] = c(x["L0_ffn_conv_w"][:, 0, :])
    qkv = x["L2_ffn_qkv_w"].reshape(3, D, D)
    for n, name in enumerate("qkv"):
        arrays["L2s_w" + name] = c(qkv[n].T)
    arrays["L2s_wo"] = c(x["L2_ffn_o_w"].T)
    arrays["L2s_gate"], arrays["L2s_up"], arrays["L2s_down"] = (c(x[f"L2_ffn_{n}_w"].T) for n in ("gate", "up", "down"))
    arrays["L3_q"] = c(x["L3_ffn_qweights"].transpose(0, 2, 1))
    arrays["L3_s"] = c(x["L3_ffn_scales"].transpose(0, 2, 1))
    arrays["L3_la"] = c(x["L3_ffn_lora_a"])
    arrays["L3_lb"] = c(x["L3_ffn_lora_b"].transpose(0, 2, 1))
    signals = {}
    for _ in range(2):
        nc = bacc.Bacc("TRN2", target_bir_lowering=False, num_devices=1)
        a = {n: nc.dram_tensor("in_" + n, v.shape, mybir.dt.from_np(v.dtype), kind="ExternalInput").ap()
             for n, v in arrays.items()}
        out = nc.dram_tensor("out", _OUT, F32, kind="ExternalOutput").ap()
        build(nc, a, out, signals)
    r = run_bass_kernel_spmd(nc, [{"in_" + n: v for n, v in arrays.items()}], core_ids=[0])
    return r.results[0]["out"]
```

```python
from contextlib import ExitStack

import numpy as np

import concourse.bass as bass
from concourse import mybir

F32 = mybir.dt.float32
BF16 = mybir.dt.bfloat16
I32 = mybir.dt.int32
ALU = mybir.AluOpType
ACT = mybir.ActivationFunctionType
AX = mybir.AxisListType

B, S, D, C = 32, 128, 256, 192
P = 128
KD = D // P
CC, KC = 96, 2
H = 16
CH = 4
BANK = 512
LANES_A, LANES_B = 4, 4
HID0, HID2, E1 = 1024, 1024, 8
LN_EPS, RMS_EPS = 1e-5, 1e-6
MAGIC = 1.5 * 2.0**23
MASKED = -1e9
GROUP, RANK, BLOCKS = 16, 32, 3

PAIRED = ["L0", "L2", "L3"]

ORDER_A = (
    "323233232212203103311233022013101030320302031131033202013212032312010132020111203020033122"
    "002333113103300301103100311133011121303231012321031310101030212102321021022323123101233121"
    "311330211130000230323232210233213112020201321221100303333010131213133110103320113003130201"
    "012102310010210223120302120310132033220312120102312002321211301213231220330313021001202021"
    "203203022120031232111331122333010221132012001300232101200231120200012131013220013023302013"
    "102001213022213033220310221321030201102012223330221120313213023122322212111232222001020312"
    "312102221311030230023210301202330313002310330221231023201333122300211331231001200203021302"
    "100302132213033022031002303203013012323300320330222003110232220030321220130001103303001031"
    "303031332003211232101121322130312100133112100232111002313212210313231002133132003030122130"
    "022120103232232310301323110333112120121311023200132311221221031301210212032100311213232330"
    "030102112230022313020210112202203133120313210131220113201320331122212301120303230303033112"
    "310030230121032311202102311100321231032102110013320221003112213032302211313010203131201230"
    "012311310022021002123113031123213032302023302302303320230133312213301031302330201032031311"
    "00"
)
ORDER_B = (
    "323233120231032121013301021032301322031112331023100103231323101202231032013212013002310130"
    "220301112310233210202013221000"
)


class Mark:

    def __init__(self, engine, number):
        self.engine, self.number = engine, number


class Engine:

    def __init__(self, nc, queue, sem):
        self.nc, self.q, self.sem = nc, queue, sem
        self.count, self.loop, self.per_pass = 0, None, 0
        self.seen = {}

    def enter(self, sem, loop, per_pass):
        self.sem, self.loop, self.per_pass = sem, loop, per_pass
        self.count, self.seen = 0, {}

    def wait_apart(self, *marks):
        self.wait(*marks)
        self.q.sem_inc(self.passed, 1)

    def done(self, instruction):
        self.count += 1
        instruction.then_inc(self.sem, 1)
        return Mark(self, self.count)

    def wait(self, *marks):
        for m in marks:
            if m is None or self.seen.get(m.engine, -1) >= m.number:
                continue
            self.seen[m.engine] = m.number
            e = m.engine
            value = m.number if e.loop is None else e.loop * e.per_pass + m.number + 1
            self.q.wait_ge(e.sem, value)


def issue(lanes, order):
    lanes = [iter(lane) for lane in lanes]
    for n in order:
        next(lanes[int(n)], None)
    assert all(next(lane, order) is order for lane in lanes)


def build(nc, a, out, signals):
    ctx = ExitStack()
    with ctx:

        def sb(name, shape, dt=F32):
            return ctx.enter_context(nc.sbuf_tensor(name, shape, dt))

        def sem(name):
            return ctx.enter_context(nc.semaphore(name))

        scratch = nc.dram_tensor("after_L3_xattn", (B, S, D), F32, kind="Internal").ap()
        psum = ctx.enter_context(nc.psum_tensor("psum", [P, 8, BANK], F32))

        pe = Engine(nc, nc.tensor, sem("pe_setup"))
        dve = Engine(nc, nc.vector, sem("dve_setup"))
        act = Engine(nc, nc.scalar, sem("act_setup"))
        pool = Engine(nc, nc.gpsimd, sem("pool_setup"))
        engines = {"pe": pe, "dve": dve, "act": act, "pool": pool}
        for name, e in engines.items():
            e.passed = sem(name + "_passed")
        loop_sems = {(l, e): sem(f"{e}_{l}") for l in "ab" for e in engines}
        s_load = sem("s_load")
        loaded = [0]

        def load(dst, src):
            nc.sync.dma_start(dst, src).then_inc(s_load, 16)
            loaded[0] += 16

        ident = sb("ident", [P, P])
        ident_bf = sb("ident_bf", [P, P], BF16)
        ones = sb("ones", [P, P])
        head_rows = sb("head_rows", [P, 8])
        half_of = sb("half_of", [P, 2])
        causal = sb("causal", [P, P])
        minus_half = sb("minus_half", [P, 1])
        gates = sb("gates", [P, 8])
        first_of = sb("first_of", [P, E1])
        magic = sb("magic", [P, 2])

        load(gates[:, 0:4], a["g_xattn"].rearrange("(o n) -> o n", o=1).to_broadcast([P, 4]))
        load(gates[:, 4:8], a["g_ffn"].rearrange("(o n) -> o n", o=1).to_broadcast([P, 4]))

        w = {}

        def matrix(name, src, k, n, rows=P):
            w[name] = sb("w_" + name, [rows, k, n])
            load(w[name][:], src.rearrange("(k p) n -> p k n", k=k))

        def columns(name, src, n):
            w[name] = sb("w_" + name, [P, n])
            load(w[name][:], src)

        setup_ctx = ExitStack()

        def row(name, src, n):
            w[name] = setup_ctx.enter_context(nc.sbuf_tensor("w_" + name, [1, n], F32))
            load(w[name][:], src.rearrange("(o n) -> o n", o=1))

        for l in PAIRED:
            matrix(l + "q", a[l + "_wq"], KD, D)
            matrix(l + "k", a[l + "_wk"], KC, D, CC)
            matrix(l + "v", a[l + "_wv"], KC, D, CC)
            matrix(l + "o", a[l + "_wo"], KD, D)
            columns(l + "bq", a[l + "_bq"], KD)
            columns(l + "bk", a[l + "_bk"], KD)
        matrix("L1q", a["L1_wq"], KD, H * 64)
        matrix("L1k", a["L1_wk"], KC, H * 64, CC)
        matrix("L1v", a["L1_wv"], KC, H * 64, CC)
        matrix("L1o", a["L1_wo"], 8, D)
        matrix("router", a["L1_router"], KD, E1)
        matrix("experts", a["L1_experts"], KD, E1 * D)
        w["eb"] = sb("w_eb", [E1, D])
        load(w["eb"][:], a["L1_ffn_expert_b"])
        w["rb"] = sb("w_rb", [P, E1])
        load(w["rb"][:], a["L1_ffn_router_b"].rearrange("(o n) -> o n", o=1).to_broadcast([P, E1]))
        for n in "qkv":
            matrix("self" + n, a["L2s_w" + n], KD, D)
        matrix("selfo", a["L2s_wo"], KD, D)
        matrix("gate", a["L2s_gate"], KD, E1)
        matrix("up", a["L2s_up"], KD, HID2)
        matrix("down", a["L2s_down"], HID2 // P, D)
        w["conv"] = sb("w_conv", [P, HID0 // P, 3])
        load(w["conv"][:], a["L0_conv"].rearrange("(k p) t -> p k t", p=P))
        columns("convb", a["L0_convb"], HID0 // P)
        w["w1q"] = sb("w_w1q", [P, KD, HID0], BF16)
        w["w2q"] = sb("w_w2q", [P, HID0 // P, D], BF16)
        out_bias = {l: sb("out_bias_" + l, [P, D]) for l in ["L0", "L1", "L2", "L3"]}
        deq = sb("deq", [P, 2])

        for l in PAIRED:
            w[l + "bv"] = setup_ctx.enter_context(nc.sbuf_tensor(l + "bv", [P, KD], F32))
            load(w[l + "bv"][:], a[l + "_bv"])
        for l in PAIRED + ["L1"]:
            row(l + "bo", a[l + "_bo"], D)
        raw = [setup_ctx.enter_context(nc.sbuf_tensor(f"raw{n}", [P, HID0 * KD], F32)) for n in range(2)]
        load(raw[0][:].rearrange("p (k n) -> p k n", k=KD), a["L0_w1"].rearrange("(k p) n -> p k n", p=P))
        load(raw[1][:].rearrange("p (k n) -> p k n", n=D), a["L0_w2"].rearrange("(k p) n -> p k n", p=P))
        norms = setup_ctx.enter_context(nc.sbuf_tensor("norms", [P, 2, KD], F32))
        load(norms[:, 0, :], a["L2s_n1"])
        load(norms[:, 1, :], a["L2s_n2"])
        bvb = setup_ctx.enter_context(nc.sbuf_tensor("bvb", [P, len(PAIRED), KD, P], F32))
        absum = setup_ctx.enter_context(nc.sbuf_tensor("absum", [P, 4], F32))

        pool.q.memset(ident[:], 0.0)
        pool.q.memset(causal[:], 3.0e38)
        pool.q.memset(minus_half[:], -0.5)
        for r in range(2):
            dve.q.memset(half_of[0:64, r:r + 1], 1.0 - r)
            dve.q.memset(half_of[64:P, r:r + 1], 0.0 + r)
        pool.q.memset(magic[:, 0:1], MAGIC)
        pool.q.memset(magic[:, 1:2], -MAGIC)
        pool.q.memset(head_rows[:], 1.0)
        m = pool.done(pool.q.memset(ones[:], 1.0))
        pool.wait(m)
        pool.q.affine_select(out=ident[:], in_=ident[:], compare_op=ALU.not_equal, fill=1.0, base=0,
                             pattern=[[-1, P]], channel_multiplier=1)
        m = pool.done(pool.q.affine_select(out=causal[:], in_=causal[:], compare_op=ALU.is_ge, fill=4 * MASKED,
                                           base=0, pattern=[[-1, P]], channel_multiplier=1))
        pool.wait(m)
        m = pool.done(pool.q.affine_select(out=head_rows[:], in_=head_rows[:], compare_op=ALU.is_ge, fill=0.0, base=0,
                                           pattern=[[-16, 8]], channel_multiplier=1))
        pool.wait(m)
        consts_ready = pool.done(pool.q.affine_select(
            out=head_rows[:], in_=head_rows[:], compare_op=ALU.is_ge, fill=0.0, base=15, pattern=[[16, 8]],
            channel_multiplier=-1))
        dve.wait(consts_ready)
        dve_consts = dve.done(dve.q.tensor_copy(ident_bf[:], ident[:]))

        for e in (act, dve, pe):
            e.q.wait_ge(s_load, loaded[0])
        tanh_gates = act.done(act.q.activation(gates[:], gates[:], ACT.Tanh))
        dve.wait(tanh_gates)
        gx = {l: gates[:, n:n + 1] for n, l in enumerate(["L0", "L1", "L2", "L3"])}
        gf = {l: gates[:, 4 + n:5 + n] for n, l in enumerate(["L0", "L1", "L2", "L3"])}

        def scale(name, by):
            return dve.q.tensor_scalar(w[name][:], w[name][:], by, None, ALU.mult)

        for l in PAIRED + ["L1"]:
            scale(l + "o", gx[l])
            dve.q.tensor_scalar(w[l + "bo"][:], w[l + "bo"][:], gx[l][0:1], None, ALU.mult)
        scale("experts", gf["L1"])
        dve.q.tensor_scalar(w["eb"][:], w["eb"][:], gf["L1"][0:E1], None, ALU.mult)
        dve.q.tensor_scalar(w["down"][:], w["down"][:], gf["L2"], 0.5, ALU.mult, ALU.mult)
        for name, n in (("selfq", 0), ("selfk", 0), ("selfv", 0), ("gate", 1), ("up", 1)):
            for k in range(KD):
                dve.q.tensor_scalar(w[name][:, k, :], w[name][:, k, :], norms[:, n, k:k + 1], None, ALU.mult)
        for n, l in enumerate(PAIRED):
            for k in range(KD):
                last = dve.q.tensor_copy(bvb[:, n, k, :], w[l + "bv"][:, k:k + 1].to_broadcast([P, P]))
        for n in range(2):
            last = dve.q.tensor_reduce(absum[:, n:n + 1], raw[n][:], AX.X, ALU.add, apply_absolute_value=True)
        ready = dve.done(last)
        pe.wait(ready, consts_ready, dve_consts)
        for n, l in enumerate(PAIRED + ["L1"]):
            if l != "L1":
                for k in range(KD):
                    pe.q.matmul(psum[:, n, 0:D], bvb[:, n, k, :], w[l + "o"][:, k, :], start=k == 0, stop=False)
            last = pe.q.matmul(psum[:, n, 0:D], ones[0:1, :], w[l + "bo"][:], start=l == "L1", stop=True)
        last = pe.q.matmul(psum[:, 4, 0:2], ones[:], absum[:, 0:2], start=True, stop=True)
        ready = pe.done(last)
        dve.wait(ready)
        for n, l in enumerate(PAIRED + ["L1"]):
            dve.q.tensor_copy(out_bias[l][:], psum[:, n, 0:D])
        m = dve.done(dve.q.tensor_scalar(absum[:, 0:2], psum[:, 4, 0:2], 1.0 / (HID0 * D), 1e-5, ALU.mult, ALU.max))
        dve.wait(m)
        dve.q.tensor_scalar(deq[:, 0:1], absum[:, 0:1], 1.0 / 127.0, None, ALU.mult)
        dve.q.tensor_scalar(deq[:, 1:2], absum[:, 1:2], gf["L0"], 0.5 / 127.0, ALU.mult, ALU.mult)
        m = dve.done(dve.q.reciprocal(absum[:, 2:4], absum[:, 0:2]))
        dve.wait(m)
        for n in range(2):
            m = dve.done(dve.q.tensor_scalar(raw[n][:], raw[n][:], absum[:, 2 + n:3 + n], MAGIC, ALU.mult, ALU.add))
        dve.wait(m)
        for n in range(2):
            m = dve.done(dve.q.tensor_scalar(raw[n][:], raw[n][:], -MAGIC, 1.0, ALU.add, ALU.min))
        dve.wait(m)
        for n, name in enumerate(["w1q", "w2q"]):
            flat = w[name][:].rearrange("p k n -> p (k n)")
            weights_ready = dve.done(dve.q.tensor_scalar(flat, raw[n][:], -1.0, None, ALU.max))
        setup_ctx.close()

        class Lane:
            pass

        lane_ctx = ExitStack()

        def lane_buffers(n):
            t = Lane()

            def buf(name, shape, dt=F32):
                return lane_ctx.enter_context(nc.sbuf_tensor(f"{name}_{n}", shape, dt))

            t.n = n
            t.a, t.b = psum[:, 2 * n, :], psum[:, 2 * n + 1, :]
            t.x_in = buf("x_in", [P, D])
            t.ctxT = buf("ctxT", [CC, KC, S])
            t.x = buf("x", [P, D])
            t.xn = buf("xn", [P, D])
            t.xnT = buf("xnT", [P, KD, S])
            t.stats = buf("stats", [P, 6])
            t.mv = buf("mv", [P, 2])
            t.tiny = buf("tiny", [P, 64])
            big = buf("big", [P, 4 * BANK])
            t.e = [big[:, 0:BANK].rearrange("p (h s) -> p h s", h=CH), big[:, BANK:2 * BANK].rearrange("p (h s) -> p h s", h=CH)]
            t.eT = big[:, 2 * BANK:3 * BANK].rearrange("p (h s) -> p h s", h=CH)
            t.kT = big[:, 3 * BANK:4 * BANK].rearrange("p (k s) -> p k s", s=S)
            t.hid = big[:, 0:2 * BANK].rearrange("p (k s) -> p k s", s=S)
            t.act = big[:, 2 * BANK:4 * BANK].rearrange("p (k s) -> p k s", s=S)
            t.rounded = big[:, 0:2 * BANK]
            keys = buf("head_keys", [P, 2 * BANK])
            small = buf("small", [P, 2 * BANK + 32])
            t.qT = small[:, 0:D].rearrange("p (k s) -> p k s", s=S)
            t.o = t.un = small[:, D:2 * D]
            t.v = small[:, 2 * D:2 * D + H * 17]
            t.oT = small[:, 3 * D + 32:4 * D + 32].rearrange("p (k s) -> p k s", s=S)
            t.xi = small[:, 0:BANK].bitcast(BF16)
            t.xiT = small[:, BANK:2 * BANK].bitcast(BF16).rearrange("p (k s) -> p k s", s=S)
            t.diag, t.row_scale = t.act[:, 0, :], t.xnT[:, 0, :]
            t.wtT = t.un[0:E1, 0:S]
            t.head_keys = [keys[:, n * BANK:(n + 1) * BANK].rearrange("p (h s) -> p h s", h=CH) for n in range(2)]
            t.loaded_x, t.loaded_c = sem(f"loaded_x_{n}"), sem(f"loaded_c_{n}")
            t.stored = sem(f"stored_{n}")
            return t

        lanes = [lane_buffers(n) for n in range(LANES_A)]
        for t in lanes:
            nc.sync.wait_ge(dve.sem, weights_ready.number)
            nc.sync.dma_start(t.x_in[:], a["x"][t.n]).then_inc(t.loaded_x, 16)
            nc.sync.dma_start(t.ctxT[:], a["ctxT"][t.n].rearrange("(k p) s -> p k s", k=KC)).then_inc(t.loaded_c, 16)
        pe.wait(weights_ready)
        act.wait(weights_ready)
        pool.wait(weights_ready)

        def layernorm(t, src, src_ready=None):
            dve.wait(src_ready)
            m = dve.done(dve.q.bn_stats(t.stats[:], src))
            dve.wait_apart(m)
            m = dve.done(dve.q.bn_aggr(t.mv[:], t.stats[:]))
            dve.wait(m)
            m = dve.done(dve.q.tensor_scalar(t.tiny[:, 0:1], t.mv[:, 1:2], LN_EPS, None, ALU.add))
            pool.wait(m)
            m = pool.done(pool.q.tensor_tensor(t.tiny[:, 1:2], t.tiny[:, 0:1], minus_half[:], ALU.pow))
            yield
            dve.wait(m)
            return dve.done(dve.q.tensor_scalar(t.xn[:], src, t.mv[:, 0:1], t.tiny[:, 1:2],
                                                ALU.subtract, ALU.mult))

        def transposes(bank, src, chunks, identity=None):
            for k in range(chunks):
                last = pe.q.transpose(bank[:, k * P:(k + 1) * P], src[:, k * P:(k + 1) * P],
                                      ident[:] if identity is None else identity)
            return last

        def two_transposed(t, dst, src, src_ready):
            pe.wait(t.a_free, src_ready)
            m = pe.done(transposes(t.a, src, KD))
            yield
            act.wait(m)
            t.a_free = act.done(act.q.activation(dst[:], t.a[:, 0:D].rearrange("p (k s) -> p k s", s=S), ACT.Copy))
            return t.a_free

        def features_T(bank, wt, src, rows, outs):
            for j, n in enumerate(outs):
                for k in range(KD):
                    last = pe.q.matmul(bank[:, j * S:(j + 1) * S], wt[0:rows, k, n * P:(n + 1) * P],
                                       src[0:rows, k, :], start=k == 0, stop=k == KD - 1)
            return last

        def tokens(bank, srcT, wt, n, rows=P, chunks=KD, c0=0):
            for k in range(chunks):
                last = pe.q.matmul(bank[:, 0:n], srcT[0:rows, k, :], wt[0:rows, k, c0:c0 + n],
                                   start=k == 0, stop=k == chunks - 1)
            return last

        def softmax(t, c, scale, scores_ready, clip=None, masked=False):
            s4 = t.a.rearrange("p (h s) -> p h s", h=CH)
            yield
            dve.wait(scores_ready)
            if clip:
                dve.wait(dve.done(dve.q.tensor_scalar(t.a, t.a, clip / scale, -clip / scale, ALU.min, ALU.max)))
            if masked:
                dve.wait(dve.done(dve.q.tensor_tensor(s4, s4, causal[:].rearrange("p (o s) -> p o s", o=1)
                                                      .to_broadcast([P, CH, S]), ALU.min)))
            top = t.tiny[:, 8 + 4 * (c % 2):12 + 4 * (c % 2)]
            dve.wait(dve.done(dve.q.tensor_reduce(top, s4, AX.X, ALU.max)))
            t.a_free = dve.done(dve.q.tensor_tensor(t.e[c % 2], s4, top.rearrange("p (h o) -> p h o", o=1)
                                                    .to_broadcast([P, CH, S]), ALU.subtract))
            yield
            act.wait(t.a_free)
            flat = t.e[c % 2].rearrange("p h s -> p (h s)")
            return act.done(act.q.activation(flat, flat, ACT.Exp, scale=scale))

        def transposed_probabilities(t, c, e_ready):
            pe.wait(t.b_free, e_ready)
            m = pe.done(transposes(t.b, t.e[c % 2].rearrange("p h s -> p (h s)"), CH))
            yield
            act.wait(m)
            t.b_free = act.done(act.q.activation(t.eT.rearrange("p h s -> p (h s)"), t.b, ACT.Copy))
            return t.b_free

        def weighted_values(t, values, eT_ready):
            pe.wait(eT_ready)
            n = values[0].shape[-1]
            for j in range(CH):
                last = pe.q.matmul(t.b[:, j * n:(j + 1) * n], t.eT[:, j, :], values[j], start=True, stop=True)
            m = pe.done(last)
            yield
            dve.wait(m)
            got = t.b[:, 0:CH * n].rearrange("p (h d) -> p h d", h=CH)
            den = t.tiny[:, 32:32 + CH].rearrange("p (h o) -> p h o", o=1)
            dve.wait(dve.done(dve.q.reciprocal(den, got[:, :, n - 1:n])))
            return got[:, :, 0:n - 1], den

        def narrow_attention(t, l, x_ready, kv, kv_rows, clip=None, masked=False, kv_wait=None):
            dh = D // H
            v = t.v.rearrange("p (h d) -> p h d", h=H)
            pe.wait(t.a_free, x_ready)
            m = pe.done(features_T(t.a, w[l + "q"], t.xnT, P, range(KD)))
            yield
            act.wait(m)
            for k in range(KD):
                src = t.a[:, k * S:(k + 1) * S]
                if l == "self":
                    last = act.q.activation(t.qT[:, k, :], src, ACT.Copy)
                else:
                    last = act.q.activation(t.qT[:, k, :], src, ACT.Identity, bias=w[l + "bq"][:, k:k + 1])
            t.a_free = q_ready = act.done(last)
            yield
            if kv_wait:
                kv_wait()
            pe.wait(t.b_free)
            m = pe.done(features_T(t.b, w[l + "k"], kv, kv_rows, range(KD)))
            yield
            act.wait(m)
            for k in range(KD):
                src = t.b[:, k * S:(k + 1) * S]
                if l == "self":
                    last = act.q.activation(t.kT[:, k, :], src, ACT.Copy)
                else:
                    last = act.q.activation(t.kT[:, k, :], src, ACT.Identity, bias=w[l + "bk"][:, k:k + 1])
            t.b_free = k_ready = act.done(last)
            pool.wait_apart(q_ready)
            v_ones = pool.done(pool.q.memset(v[:, :, dh:dh + 1], 1.0))
            yield
            pe.wait(t.a_free)
            m = pe.done(tokens(t.a, kv, w[l + "v"], D, kv_rows))
            yield
            act.wait(m)
            t.a_free = v_ready = act.done(act.q.activation(
                v[:, :, 0:dh], t.a[:, 0:D].rearrange("p (h d) -> p h d", h=H), ACT.Copy))
            yield
            slot_read = [None, None]

            def keys_apart(c):
                pool.wait(k_ready, slot_read[c % 2])
                return pool.done(pool.q.tensor_tensor(
                    t.head_keys[c % 2], t.kT[:, c // 2:c // 2 + 1, :].to_broadcast([P, CH, S]),
                    head_rows[:, CH * (c % 2):CH * (c % 2 + 1)].rearrange("p (h o) -> p h o", o=1)
                    .to_broadcast([P, CH, S]), ALU.mult))

            def scores(c):
                pe.wait(t.a_free, q_ready, keys[c])
                slot_read[c % 2] = pe.done(pe.q.matmul(
                    t.a, t.qT[:, c // 2, :], t.head_keys[c % 2].rearrange("p h s -> p (h s)"), start=True, stop=True))
                return (yield from softmax(t, c, dh ** -0.5, slot_read[c % 2], clip, masked))

            keys = {0: keys_apart(0), 1: keys_apart(1)}
            e_ready = [(yield from scores(0)), None]
            yield
            for c in range(4):
                if c + 1 < 4:
                    e_ready[(c + 1) % 2] = yield from scores(c + 1)
                    if c + 2 < 4:
                        keys[c + 2] = keys_apart(c + 2)
                    yield
                eT_ready = yield from transposed_probabilities(t, c, e_ready[c % 2])
                yield
                pe.wait(v_ready, v_ones)
                got, den = yield from weighted_values(t, [v[:, CH * c + j, :] for j in range(CH)], eT_ready)
                t.b_free = dve.done(dve.q.tensor_tensor(
                    t.o[:, CH * dh * c:CH * dh * (c + 1)].rearrange("p (h d) -> p h d", h=CH), got,
                    den.to_broadcast([P, CH, dh]), ALU.mult))
                yield
            oT_ready = yield from two_transposed(t, t.oT, t.o, t.b_free)
            yield
            pe.wait(t.b_free, oT_ready)
            t.result_ready = pe.done(tokens(t.b, t.oT, w[l + "o"], D))

        def wide_attention(t, x_ready, kv, kv_rows):
            dh = 64
            v = t.v[:, 0:CH * (dh + 1)].rearrange("p (h d) -> p h d", h=CH)
            o3 = t.o.rearrange("p (h d) -> p h d", h=CH)
            pool.wait_apart(x_ready)
            v_ones = pool.done(pool.q.memset(v[:, :, dh:dh + 1], 1.0))
            for g in range(4):
                pe.wait(t.a_free, x_ready)
                m = pe.done(features_T(t.a, w["L1q"], t.xnT, P, range(2 * g, 2 * g + 2)))
                yield
                act.wait(m)
                t.a_free = q_ready = act.done(act.q.activation(
                    t.qT, t.a[:, 0:D].rearrange("p (k s) -> p k s", s=S), ACT.Copy))
                yield
                pe.wait(t.b_free)
                m = pe.done(features_T(t.b, w["L1k"], kv, kv_rows, range(2 * g, 2 * g + 2)))
                yield
                dve.wait(m)
                kT4 = t.kT.rearrange("p (k r) s -> p k r s", r=2)
                for r in range(2):
                    last = dve.q.tensor_scalar(kT4[:, :, r, :], t.b[:, 0:D].rearrange("p (k s) -> p k s", s=S),
                                               half_of[:, r:r + 1], None, ALU.mult)
                t.b_free = k_ready = dve.done(last)
                yield
                pe.wait(t.a_free, q_ready, k_ready)
                for k in range(2):
                    last = pe.q.matmul(t.a[:, 2 * k * S:2 * (k + 1) * S], t.qT[:, k, :],
                                       t.kT[:, 2 * k:2 * k + 2, :].rearrange("p k s -> p (k s)"), start=True, stop=True)
                e_ready = yield from softmax(t, g, dh ** -0.5, pe.done(last))
                yield
                pe.wait(t.b_free)
                m = pe.done(tokens(t.b, kv, w["L1v"], CH * dh, kv_rows, c0=g * CH * dh))
                yield
                act.wait(m)
                t.b_free = v_ready = act.done(act.q.activation(
                    v[:, :, 0:dh], t.b[:, 0:CH * dh].rearrange("p (h d) -> p h d", h=CH), ACT.Copy))
                yield
                eT_ready = yield from transposed_probabilities(t, g, e_ready)
                yield
                pe.wait(v_ready, v_ones)
                got, den = yield from weighted_values(t, [v[:, j, :] for j in range(CH)], eT_ready)
                t.b_free = dve.done(dve.q.tensor_tensor(o3, got, den.to_broadcast([P, CH, dh]), ALU.mult))
                yield
                oT_ready = yield from two_transposed(t, t.oT, t.o, t.b_free)
                yield
                pe.wait(t.b_free, oT_ready)
                for k in range(2):
                    last = pe.q.matmul(t.b[:, 0:D], t.oT[:, k, :], w["L1o"][:, 2 * g + k, :], start=k == 0, stop=k == 1)
                t.result_ready = pe.done(last)
                if g < 3:
                    dve.wait(t.result_ready, t.x_ready)
                    t.b_free = t.x_ready = dve.done(dve.q.tensor_tensor(t.x[:], t.b[:, 0:D], t.x[:], ALU.add))
                    yield

        def cross_attention(t, l, src, clip=None, kv_wait=None):
            m = yield from layernorm(t, src, t.x_ready)
            pool.wait(m)
            t.x_ready = t.x_in_free = pool.done(pool.q.tensor_tensor(t.x[:], src, out_bias[l][:], ALU.add))
            yield
            xnT_ready = yield from two_transposed(t, t.xnT, t.xn, m)
            yield
            if l == "L1":
                yield from wide_attention(t, xnT_ready, t.ctxT, CC)
            else:
                yield from narrow_attention(t, l, xnT_ready, t.ctxT, CC, clip=clip, kv_wait=kv_wait)
            dve.wait(t.result_ready, t.x_ready)
            t.b_free = t.x_ready = dve.done(dve.q.tensor_tensor(t.x[:], t.b[:, 0:D], t.x[:], ALU.add))
            yield

        def bitlinear_ffn(t):
            mx, rs, sc = t.tiny[:, 2:3], t.tiny[:, 3:4], t.tiny[:, 4:5]
            m = yield from layernorm(t, t.x[:], t.x_ready)
            dve.wait(m)
            dve.wait(dve.done(dve.q.tensor_reduce(mx, t.xn[:], AX.X, ALU.max, apply_absolute_value=True)))
            dve.wait(dve.done(dve.q.tensor_scalar(mx, mx, 1e-5, None, ALU.max)))
            dve.wait(dve.done(dve.q.reciprocal(rs, mx)))
            dve.wait(dve.done(dve.q.tensor_scalar(rs, rs, 127.0, None, ALU.mult)))
            dve.wait(dve.done(dve.q.tensor_scalar(t.rounded[:, 0:D], t.xn[:], rs, MAGIC, ALU.mult, ALU.add)))
            xi_ready = dve.done(dve.q.tensor_scalar(t.xi[:, 0:D], t.rounded[:, 0:D], -MAGIC, None, ALU.add))
            yield
            dve.wait(dve.done(dve.q.tensor_scalar(sc, mx, deq[:, 0:1], None, ALU.mult)))
            diag_ready = dve.done(dve.q.tensor_scalar(t.diag, ident[:], sc, None, ALU.mult))
            yield
            bf = t.a[:, 0:P].bitcast(BF16)
            pe.wait(t.a_free, xi_ready)
            m = pe.done(transposes(bf, t.xi, KD, ident_bf[:]))
            yield
            act.wait(m)
            t.a_free = xiT_ready = act.done(act.q.activation(t.xiT[:, 0:KD, :], bf.rearrange("p (k s) -> p k s", k=KD),
                                                             ACT.Copy))
            yield
            pe.wait(t.b_free, diag_ready)
            m = pe.done(pe.q.matmul(t.b[:, 0:S], ones[:], t.diag, start=True, stop=True))
            yield
            act.wait(m)
            t.b_free = rows_ready = act.done(act.q.activation(t.row_scale, t.b[:, 0:S], ACT.Copy))
            yield
            centre = []
            for half, bank in enumerate((t.a, t.b)):
                ks = range(4 * half, 4 * half + 4)
                pe.wait(xiT_ready, (t.a_free, t.b_free)[half])
                m = pe.done(features_T(bank, w["w1q"], t.xiT, P, ks))
                yield
                dve.wait(m, rows_ready)
                m = dve.done(dve.q.tensor_tensor(
                    t.hid[:, 4 * half:4 * half + 4, :], bank.rearrange("p (k s) -> p k s", s=S),
                    t.row_scale.rearrange("p (o s) -> p o s", o=1).to_broadcast([P, 4, S]), ALU.mult))
                if half == 0:
                    t.a_free = m
                else:
                    t.b_free = m
                yield
                act.wait(m)
                for k in ks:
                    m = act.q.activation(t.act[:, k, :], t.hid[:, k, :], ACT.Identity,
                                         bias=w["convb"][:, k:k + 1], scale=w["conv"][:, k, 1:2])
                centre.append(act.done(m))
                yield
            silu_ready = []
            for half in range(2):
                ks = range(4 * half, 4 * half + 4)
                sl = slice(4 * half, 4 * half + 4)
                dve.wait(centre[half])
                for k in ks:
                    m = dve.done(dve.q.scalar_tensor_tensor(
                        t.act[:, k, 1:S], t.hid[:, k, 0:S - 1], w["conv"][:, k, 0:1], t.act[:, k, 1:S],
                        ALU.mult, ALU.add))
                yield
                dve.wait(m)
                for k in ks:
                    m = dve.q.scalar_tensor_tensor(
                        t.act[:, k, 0:S - 1], t.hid[:, k, 1:S], w["conv"][:, k, 2:3], t.act[:, k, 0:S - 1],
                        ALU.mult, ALU.add)
                conv_ready = dve.done(m)
                yield
                act.wait(conv_ready)
                m = act.done(act.q.activation(t.hid[:, sl, :], t.act[:, sl, :], ACT.Tanh, scale=0.5))
                yield
                dve.wait(m, conv_ready)
                silu_ready.append(dve.done(dve.q.scalar_tensor_tensor(
                    t.act[:, sl, :], t.hid[:, sl, :], 1.0, t.act[:, sl, :], ALU.add, ALU.mult)))
                yield
            for half, bank in enumerate((t.a, t.b)):
                pe.wait(silu_ready[half], (t.a_free, t.b_free)[half])
                m = pe.done(transposes(bank, t.act[:, 4 * half:4 * half + 4, :].rearrange("p k s -> p (k s)"), 4))
                yield
                dve.wait(m)
                m = dve.done(dve.q.tensor_reduce(t.tiny[:, 5 + half:6 + half], bank, AX.X, ALU.max,
                                                 apply_absolute_value=True))
                yield
            dve.wait(m)
            dve.wait(dve.done(dve.q.tensor_tensor(mx, t.tiny[:, 5:6], t.tiny[:, 6:7], ALU.max)))
            dve.wait(dve.done(dve.q.tensor_scalar(mx, mx, 2e-5, None, ALU.max)))
            dve.wait(dve.done(dve.q.reciprocal(rs, mx)))
            rs_ready = dve.done(dve.q.tensor_scalar(rs, rs, 127.0, None, ALU.mult))
            sc_ready = dve.done(dve.q.tensor_scalar(sc, mx, deq[:, 1:2], None, ALU.mult))
            yield
            for half, bank in enumerate((t.a, t.b)):
                cols = slice(half * BANK, (half + 1) * BANK)
                act.wait(rs_ready)
                m = act.done(act.q.activation(t.rounded[:, cols], bank, ACT.Identity, bias=magic[:, 0:1], scale=rs))
                yield
                dve.wait(m)
                xi_ready = dve.done(dve.q.tensor_scalar(t.xi[:, cols], t.rounded[:, cols], -MAGIC, None, ALU.add))
                yield
                bf = bank[:, 0:2 * P].bitcast(BF16)
                pe.wait(m, xi_ready)
                m = pe.done(transposes(bf, t.xi[:, cols], 4, ident_bf[:]))
                yield
                act.wait(m)
                xiT_ready = act.done(act.q.activation(t.xiT[:, 4 * half:4 * half + 4, :],
                                                      bf.rearrange("p (k s) -> p k s", k=4), ACT.Copy))
                if half == 0:
                    t.a_free = xiT_ready
                else:
                    t.b_free = xiT_ready
                yield
            pe.wait(xiT_ready)
            m = pe.done(tokens(t.a, t.xiT, w["w2q"], D, chunks=HID0 // P))
            yield
            dve.wait(m, sc_ready)
            t.a_free = t.x_ready = dve.done(dve.q.scalar_tensor_tensor(t.x[:], t.a[:, 0:D], sc, t.x[:],
                                                                       ALU.mult, ALU.add))
            yield

        def moe_ffn(t):
            xn_ready = yield from layernorm(t, t.x[:], t.x_ready)
            yield
            xnT_ready = yield from two_transposed(t, t.xnT, t.xn, xn_ready)
            yield
            pe.wait(t.b_free, xnT_ready)
            m = pe.done(tokens(t.b, t.xnT, w["router"], E1))
            lg, ex, wt, mx, sm = t.tiny[:, 8:16], t.tiny[:, 16:24], t.tiny[:, 24:32], t.tiny[:, 2:3], t.tiny[:, 3:4]
            dve.wait(m)
            t.b_free = m = dve.done(dve.q.tensor_tensor(lg, t.b[:, 0:E1], w["rb"][:], ALU.add))
            dve.wait(m)
            dve.wait(dve.done(dve.q.tensor_reduce(mx, lg, AX.X, ALU.max)))
            m = dve.done(dve.q.tensor_scalar(lg, lg, mx, None, ALU.subtract))
            act.wait(m)
            exp_ready = act.done(act.q.activation(ex, lg, ACT.Exp, accum_out=sm))
            dve.wait(m)
            dve.wait(dve.done(dve.q.scalar_tensor_tensor(wt, lg, 0.0, first_of[:], ALU.is_equal, ALU.mult)))
            dve.wait(dve.done(dve.q.tensor_reduce(mx, wt, AX.X, ALU.max)))
            dve.wait(exp_ready)
            dve.wait(dve.done(dve.q.reciprocal(sm, sm)))
            wt_ready = dve.done(dve.q.tensor_scalar(wt, wt, mx, sm, ALU.is_equal, ALU.mult))
            yield
            pe.wait(t.b_free, wt_ready)
            m = pe.done(pe.q.transpose(t.b[0:E1, 0:P], wt, ident[:]))
            yield
            act.wait(m)
            t.b_free = wtT_ready = act.done(act.q.activation(t.wtT, t.b[0:E1, 0:P], ACT.Copy))
            yield
            for pair in range(E1 // 2):
                bank = (t.a, t.b)[pair % 2]
                pe.wait((t.a_free, t.b_free)[pair % 2])
                m = pe.done(tokens(bank, t.xnT, w["experts"], BANK, c0=pair * BANK))
                for j in range(2):
                    e = 2 * pair + j
                    dve.wait(m, wt_ready, t.x_ready)
                    m = t.x_ready = dve.done(dve.q.scalar_tensor_tensor(t.x[:], bank[:, j * D:(j + 1) * D], wt[:, e:e + 1], t.x[:],
                                                            ALU.mult, ALU.add))
                if pair % 2 == 0:
                    t.a_free = m
                else:
                    t.b_free = m
                yield
            pe.wait(t.a_free, wtT_ready)
            m = pe.done(pe.q.matmul(t.a[:, 0:D], t.wtT, w["eb"][:], start=True, stop=True))
            yield
            dve.wait(m, t.x_ready)
            t.a_free = t.x_ready = dve.done(dve.q.tensor_tensor(t.x[:], t.a[:, 0:D], t.x[:], ALU.add))
            yield

        def transformer_ffn(t):
            u_ready = yield from layernorm(t, t.x[:], t.x_ready)
            ms, rr, f1, f2 = t.tiny[:, 2:3], t.tiny[:, 3:4], t.tiny[:, 4:5], t.tiny[:, 5:6]
            u, un = t.xn, t.un
            dve.wait(u_ready)

            def rms(ready):
                act.wait(ready)
                m = act.done(act.q.activation(un, u[:], ACT.Square, accum_out=ms))
                pool.wait_apart(m)
                m = pool.done(pool.q.tensor_scalar(rr, ms, 1.0 / D, RMS_EPS, ALU.mult, ALU.add))
                pool.wait(m)
                m = pool.done(pool.q.tensor_tensor(f1, rr, minus_half[:], ALU.pow))
                dve.wait(m)
                return dve.done(dve.q.tensor_scalar(un, u[:], f1, None, ALU.mult))

            un_ready = rms(u_ready)
            yield
            unT_ready = yield from two_transposed(t, t.xnT, un, un_ready)
            yield
            yield from narrow_attention(t, "self", unT_ready, t.xnT, P, masked=True)
            dve.wait(t.result_ready)
            t.b_free = u_ready = dve.done(dve.q.tensor_tensor(u[:], t.b[:, 0:D], u[:], ALU.add))
            un_ready = rms(u_ready)
            dve.wait(u_ready)
            x_u = dve.done(dve.q.scalar_tensor_tensor(t.x[:], u[:], gf["L2"], t.x[:], ALU.mult, ALU.add))
            yield
            unT_ready = yield from two_transposed(t, t.xnT, un, un_ready)
            yield
            pe.wait(t.b_free, unT_ready)
            m = pe.done(tokens(t.b, t.xnT, w["gate"], E1))
            lg, top, sm = t.tiny[:, 8:16], t.tiny[:, 16:24], t.tiny[:, 6:7]
            dve.wait(m)
            dve.wait(dve.done(dve.q.tensor_reduce(sm, t.b[:, 0:E1], AX.X, ALU.max)))
            t.b_free = m = dve.done(dve.q.tensor_scalar(lg, t.b[:, 0:E1], sm, None, ALU.subtract))
            act.wait(m)
            m = act.done(act.q.activation(lg, lg, ACT.Exp, accum_out=sm))
            yield
            dve.wait_apart(m)
            dve.wait(dve.done(dve.q.max(top, lg)))
            dve.wait(dve.done(dve.q.reciprocal(sm, sm)))
            dve.wait(dve.done(dve.q.tensor_scalar(top[:, 0:2], top[:, 0:2], sm, None, ALU.mult)))
            dve.wait(dve.done(dve.q.tensor_tensor(rr, top[:, 0:1], top[:, 1:2], ALU.add)))
            dve.wait(dve.done(dve.q.tensor_scalar(f1, rr, 1e-9, None, ALU.add)))
            dve.wait(dve.done(dve.q.reciprocal(f2, f1)))
            f_ready = dve.done(dve.q.tensor_scalar(f2, f2, rr, None, ALU.mult))
            yield
            silu_ready = []
            for half, bank in enumerate((t.a, t.b)):
                pe.wait(unT_ready, (t.a_free, t.b_free)[half])
                m = pe.done(features_T(bank, w["up"], t.xnT, P, range(4 * half, 4 * half + 4)))
                yield
                act.wait(m)
                view = bank.rearrange("p (k s) -> p k s", s=S)
                sl = slice(4 * half, 4 * half + 4)
                m = act.done(act.q.activation(t.hid[:, sl, :], view, ACT.Tanh, scale=0.5))
                yield
                dve.wait(m)
                m = dve.done(dve.q.scalar_tensor_tensor(t.act[:, sl, :], t.hid[:, sl, :], 1.0, view, ALU.add, ALU.mult))
                silu_ready.append(m)
                yield
            t.a_free, t.b_free = silu_ready
            pe.wait(*silu_ready)
            m = pe.done(tokens(t.a, t.act, w["down"], D, chunks=HID2 // P))
            yield
            dve.wait(m, f_ready, x_u)
            t.a_free = t.x_ready = dve.done(dve.q.scalar_tensor_tensor(t.x[:], t.a[:, 0:D], f2, t.x[:],
                                                                       ALU.mult, ALU.add))
            yield

        for e in range(E1):
            m = pool.q.memset(first_of[:, e:e + 1], float(E1 - e))
        first_ready = pool.done(m)
        dve.wait(first_ready)
        pe.wait(consts_ready, dve_consts)
        act.wait(consts_ready)

        passes_a = B // LANES_A
        for name, e in engines.items():
            e.q.sem_inc(loop_sems["a", name], 1)
        for t in lanes:
            nc.sync.sem_inc(t.stored, 1)
        with nc.Fori(0, passes_a) as i:
            for name, e in engines.items():
                e.enter(loop_sems["a", name], i, signals.get(("a", name), 1))

            dve.q.wait_ge(dve.sem, i * dve.per_pass + 1)

            def lane_a(t):
                t.a_free = t.b_free = t.x_ready = None
                for e in (dve, pool):
                    e.q.wait_ge(t.loaded_x, 16 * i + 16)
                    e.q.wait_ge(t.stored, 16 * i + 1)

                def context_loaded():
                    pe.q.wait_ge(t.loaded_c, 16 * i + 16)

                yield from cross_attention(t, "L0", t.x_in[:], kv_wait=context_loaded)
                nc.sync.wait_ge(pool.sem, i * pool.per_pass + t.x_in_free.number + 1)
                nc.sync.dma_start(t.x_in[:], a["x"][(i + 1) % passes_a * LANES_A + t.n]).then_inc(t.loaded_x, 16)
                yield from bitlinear_ffn(t)
                yield from cross_attention(t, "L1", t.x[:])
                yield from moe_ffn(t)
                yield from cross_attention(t, "L2", t.x[:], clip=10000.0)
                yield from transformer_ffn(t)
                yield from cross_attention(t, "L3", t.x[:])
                nc.sync.wait_ge(dve.sem, i * dve.per_pass + t.x_ready.number + 1)
                nc.sync.dma_start(scratch[i * LANES_A + t.n], t.x[:]).then_inc(t.stored, 16)
                nc.sync.dma_start(t.ctxT[:], a["ctxT"][(i + 1) % passes_a * LANES_A + t.n]
                                  .rearrange("(k p) s -> p k s", k=KC)).then_inc(t.loaded_c, 16)

            issue([lane_a(t) for t in lanes], ORDER_A)
            for name, e in engines.items():
                signals["a", name] = e.count

        for t in lanes:
            for q in (nc.sync, nc.vector):
                q.wait_ge(t.loaded_x, 16 * (passes_a + 1))
                q.wait_ge(t.loaded_c, 16 * (passes_a + 1))
                q.wait_ge(t.stored, 16 * passes_a + 1)
        a_done = {name: (loop_sems["a", name], passes_a * signals["a", name] + 1) for name in engines}
        for e in list(engines.values()):
            for s, v in a_done.values():
                e.q.wait_ge(s, v)
        for s, v in a_done.values():
            nc.sync.wait_ge(s, v)
        lane_ctx.close()

        bctx = ExitStack()
        lane_ctx = bctx

        def sb2(name, shape, dt=F32):
            return bctx.enter_context(nc.sbuf_tensor(name, shape, dt))

        NL = 2 * BLOCKS
        s_load_b = sem("s_load_b")
        wl = sb2("wl", [P, NL, KD, D])
        qw = sb2("qw", [P, NL, KD, D], I32)
        sct = sb2("sct", [P, NL, KD, D])
        la = sb2("la", [RANK, NL, D])
        lb = sb2("lb", [RANK, NL, D])
        bias = sb2("bias", [1, NL, D])
        gamma = sb2("gamma", [P, BLOCKS, KD])
        beta = sb2("beta", [P, BLOCKS, KD])
        nb = [0]

        def load_b(dst, src):
            nc.sync.dma_start(dst, src).then_inc(s_load_b, 16)
            nb[0] += 16

        for n in range(NL):
            load_b(qw[:, n], a["L3_q"][n].rearrange("(k p) o -> p k o", p=P))
            for k in range(KD):
                for g in range(P // GROUP):
                    load_b(sct[g * GROUP:(g + 1) * GROUP, n, k, :],
                           a["L3_s"][n, k * (P // GROUP) + g:k * (P // GROUP) + g + 1, :].to_broadcast([GROUP, D]))
        load_b(la[:], a["L3_la"].rearrange("n r d -> r n d"))
        load_b(lb[:], a["L3_lb"].rearrange("n r o -> r n o"))
        load_b(bias[:], a["L3_ffn_biases"].rearrange("(u n) o -> u n o", u=1))
        load_b(gamma[:], a["L3_gamma"])
        load_b(beta[:], a["L3_beta"])
        for e in (pe, dve, act):
            e.q.wait_ge(s_load_b, nb[0])
        setup_b = {name: sem(f"{name}_setup_b") for name in engines}
        for name, e in engines.items():
            e.enter(setup_b[name], None, 0)
        m = dve.done(dve.q.tensor_scalar(wl[:], qw[:], 1.0 / 7.5, -1.0, ALU.mult, ALU.add))
        dve.wait(m)
        base_ready = dve.done(dve.q.tensor_tensor(wl[:], wl[:], sct[:], ALU.mult))
        for n in range(NL):
            for k in range(KD):
                last = pe.q.matmul(psum[:, n, k * D:(k + 1) * D], la[:, n, k * P:(k + 1) * P], lb[:, n, :],
                                   start=True, stop=True)
        m = pe.done(last)
        dve.wait(m, base_ready)
        for n in range(NL):
            flat = wl[:, n].rearrange("p k o -> p (k o)")
            wl_ready = dve.done(dve.q.tensor_tensor(flat, flat, psum[:, n, :], ALU.add))

        lanes_b = []
        for n in range(LANES_B):
            t = Lane()
            t.n = n
            t.x_in = sb2(f"bx_in_{n}", [P, D])
            t.x = sb2(f"bx_{n}", [P, D])
            t.h = sb2(f"bh_{n}", [P, D])
            t.out = sb2(f"bout_{n}", [P, D])
            t.xn = sb2(f"bxn_{n}", [P, D])
            t.hT = sb2(f"bhT_{n}", [P, KD, S])
            t.yT = sb2(f"byT_{n}", [P, KD, S])
            t.stats = sb2(f"bstats_{n}", [P, 6])
            t.mv = sb2(f"bmv_{n}", [P, 2])
            t.tiny = sb2(f"btiny_{n}", [P, 4])
            t.a, t.b = psum[:, 2 * n, :], psum[:, 2 * n + 1, :]
            t.loaded, t.stored = sem(f"b_loaded_{n}"), sem(f"b_stored_{n}")
            nc.sync.dma_start(t.x_in[:], scratch[n]).then_inc(t.loaded, 16)
            lanes_b.append(t)
        pe.wait(wl_ready)
        act.wait(wl_ready)
        pool.wait(wl_ready)
        passes_b = B // LANES_B
        for name, e in engines.items():
            e.q.sem_inc(loop_sems["b", name], 1)
        for t in lanes_b:
            nc.sync.sem_inc(t.stored, 1)
        with nc.Fori(0, passes_b) as i:
            for name, e in engines.items():
                e.enter(loop_sems["b", name], i, signals.get(("b", name), 1))

            dve.q.wait_ge(dve.sem, i * dve.per_pass + 1)

            def linear(t, n, srcT, ready):
                pe.wait(t.b_free, ready)
                pe.q.matmul(t.b[:, 0:D], ones[0:1, :], bias[:, n, :], start=True, stop=False)
                for k in range(KD):
                    last = pe.q.matmul(t.b[:, 0:D], srcT[:, k, :], wl[:, n, k, :], start=False, stop=k == KD - 1)
                return pe.done(last)

            def lane_b(t):
                t.a_free = t.b_free = None
                dve.q.wait_ge(t.loaded, 16 * i + 16)
                m = dve.done(dve.q.tensor_copy(t.x[:], t.x_in[:]))
                dve.wait(m)
                xn_free = yield from layernorm(t, t.x_in[:])
                nc.sync.wait_ge(dve.sem, i * dve.per_pass + xn_free.number + 1)
                nc.sync.dma_start(t.x_in[:], scratch[(i + 1) % passes_b * LANES_B + t.n]).then_inc(t.loaded, 16)
                dve.wait(xn_free)
                h_ready = dve.done(dve.q.tensor_copy(t.h[:], t.xn[:]))
                yield
                for blk in range(BLOCKS):
                    hT_ready = yield from two_transposed(t, t.hT, t.h, h_ready)
                    yield
                    y = linear(t, 2 * blk, t.hT, hT_ready)
                    yield
                    dve.wait(y)
                    t.b_free = m = yield from layernorm(t, t.b[:, 0:D])
                    yield
                    pe.wait(t.a_free, m)
                    m = pe.done(transposes(t.a, t.xn, KD))
                    yield
                    act.wait(m)
                    for k in range(KD):
                        m = act.q.activation(t.yT[:, k, :], t.a[:, k * P:(k + 1) * P], ACT.Gelu,
                                             scale=gamma[:, blk, k:k + 1], bias=beta[:, blk, k:k + 1])
                    t.a_free = m = act.done(m)
                    yield
                    y = linear(t, 2 * blk + 1, t.yT, m)
                    yield
                    dve.wait(y, h_ready)
                    t.b_free = h_ready = dve.done(dve.q.tensor_tensor(t.h[:], t.b[:, 0:D], t.h[:], ALU.add))
                    yield
                dve.wait(h_ready)
                dve.q.wait_ge(t.stored, 16 * i + 1)
                m = dve.done(dve.q.scalar_tensor_tensor(t.out[:], t.h[:], gf["L3"], t.x[:], ALU.mult, ALU.add))
                nc.sync.wait_ge(dve.sem, i * dve.per_pass + m.number + 1)
                nc.sync.dma_start(out[i * LANES_B + t.n], t.out[:]).then_inc(t.stored, 16)

            issue([lane_b(t) for t in lanes_b], ORDER_B)
            for name, e in engines.items():
                signals["b", name] = e.count
        for t in lanes_b:
            nc.sync.wait_ge(t.loaded, 16 * (passes_b + 1))
            nc.sync.wait_ge(t.stored, 16 * passes_b + 1)
        bctx.close()


_OUT = (B, S, D)


def kernel(**inputs):
    import concourse.bacc as bacc
    from concourse.bass_utils import run_bass_kernel_spmd

    x = {n: np.asarray(v) for n, v in inputs.items()}
    c = np.ascontiguousarray
    arrays = {n: c(x[n]) for n in (
        "x", "g_xattn", "g_ffn", "L1_ffn_router_b", "L1_ffn_expert_b", "L3_ffn_biases")}

    def columns(v):
        v = v.reshape(*v.shape[:-1], -1, P)
        return c(np.moveaxis(v, -1, 0))

    arrays["ctxT"] = c(x["ctx_768"].transpose(0, 2, 1))
    kv = x["L0_xattn_Wkv"].reshape(H, 2, D // H, C)
    bkv = x["L0_xattn_bkv"].reshape(H, 2, D // H)
    arrays["L0_wq"] = c(x["L0_xattn_Wq"].T)
    arrays["L0_bq"] = columns(x["L0_xattn_bq"])
    arrays["L0_wk"], arrays["L0_wv"] = (c(kv[:, n].reshape(D, C).T) for n in range(2))
    arrays["L0_bk"], arrays["L0_bv"] = (columns(bkv[:, n].reshape(D)) for n in range(2))
    arrays["L0_wo"] = c(x["L0_xattn_Wo"].T)
    arrays["L0_bo"] = c(x["L0_xattn_bo"])
    for l in ("L2", "L3"):
        for n in "qkvo":
            arrays[f"{l}_w{n}"] = c(x[f"{l}_xattn_W{n}"])
            arrays[f"{l}_b{n}"] = (c if n == "o" else columns)(x[f"{l}_xattn_b{n}"])
    arrays["L1_wq"], arrays["L1_wk"], arrays["L1_wv"] = (c(x["L1_xattn_w_" + n]) for n in "qkv")
    arrays["L1_wo"], arrays["L1_bo"] = c(x["L1_xattn_w_out"]), c(x["L1_xattn_b_out"])
    arrays["L1_router"] = c(x["L1_ffn_router_w"])
    arrays["L1_experts"] = c(x["L1_ffn_expert_w"].transpose(1, 0, 2).reshape(D, E1 * D))
    arrays["L0_w1"], arrays["L0_w2"] = c(x["L0_ffn_w1"].T), c(x["L0_ffn_w2"].T)
    arrays["L0_convb"] = columns(x["L0_ffn_conv_b"])
    arrays["L2s_n1"], arrays["L2s_n2"] = columns(x["L2_ffn_n1_w"]), columns(x["L2_ffn_n2_w"])
    arrays["L3_gamma"], arrays["L3_beta"] = columns(x["L3_ffn_ln_gamma"]), columns(x["L3_ffn_ln_beta"])
    arrays["L0_conv"] = c(x["L0_ffn_conv_w"][:, 0, :])
    qkv = x["L2_ffn_qkv_w"].reshape(3, D, D)
    for n, name in enumerate("qkv"):
        arrays["L2s_w" + name] = c(qkv[n].T)
    arrays["L2s_wo"] = c(x["L2_ffn_o_w"].T)
    arrays["L2s_gate"], arrays["L2s_up"], arrays["L2s_down"] = (c(x[f"L2_ffn_{n}_w"].T) for n in ("gate", "up", "down"))
    arrays["L3_q"] = c(x["L3_ffn_qweights"].transpose(0, 2, 1))
    arrays["L3_s"] = c(x["L3_ffn_scales"].transpose(0, 2, 1))
    arrays["L3_la"] = c(x["L3_ffn_lora_a"])
    arrays["L3_lb"] = c(x["L3_ffn_lora_b"].transpose(0, 2, 1))
    signals = {}
    for _ in range(2):
        nc = bacc.Bacc("TRN2", target_bir_lowering=False, num_devices=1)
        a = {n: nc.dram_tensor("in_" + n, v.shape, mybir.dt.from_np(v.dtype), kind="ExternalInput").ap()
             for n, v in arrays.items()}
        out = nc.dram_tensor("out", _OUT, F32, kind="ExternalOutput").ap()
        build(nc, a, out, signals)
    r = run_bass_kernel_spmd(nc, [{"in_" + n: v for n, v in arrays.items()}], core_ids=[0])
    return r.results[0]["out"]
```

```python
from contextlib import ExitStack

import numpy as np

import concourse.bass as bass
from concourse import mybir

F32 = mybir.dt.float32
BF16 = mybir.dt.bfloat16
I32 = mybir.dt.int32
ALU = mybir.AluOpType
ACT = mybir.ActivationFunctionType
AX = mybir.AxisListType

B, S, D, C = 32, 128, 256, 192
P = 128
KD = D // P
CC, KC = 96, 2
H = 16
CH = 4
BANK = 512
LANES_A, LANES_B = 4, 8
HID0, HID2, E1 = 1024, 1024, 8
LN_EPS, RMS_EPS = 1e-5, 1e-6
MAGIC = 1.5 * 2.0**23
MASKED = -1e9
GROUP, RANK, BLOCKS = 16, 32, 3

ORDER_A = (
    "202020231310200322203100312211021203130131021011103220013021213230233220223121330013331201"
    "323032110122312022323010220312032020112123031201023130321112321201201211003132102301213122"
    "021103112002103100022133101202102231213001232113023211102121310213321213033213011023202302"
    "000203321123023301320033011132201021102312102101030221231110320011202303101210311123020301"
    "201230302103122033002211233030112100233233012302112322110132213232131202311302023011220130"
    "301121113332310222123201221111223103132122221113233300112223230023311212110013100231221011"
    "203011202313200130110320210002231133211112010100121002303203031123102203113323201220213312"
    "103020111313220231112030020123013120203110103201312223133121100231220032031120011113121023"
    "012332303230120200132321013203212023202102313330012213311131301023011003032000113213310310"
    "331011213320032102020131031232103212031223223022030230103121220010032213121330033232330210"
    "010121032312301330102210323211010102320321200103103032330132002313022330311230130130031132"
    "320231333003300033003303301210231133032021320123302333220103202031333023030032022331320023"
    "131333001030303233001032013202032320223230201303230320013213103120203313201231003300203302"
    "33"
)
ORDER_AHEAD = (
    "333323333322331322220323212133303232323323032322233130323332022123233323321233333323333323"
    "033333223133233123233233310321232311223323321130331333111233333213230112233333222322333130"
    "123233312302323133212133133233131333233122132331332113232311331333232323232232231332133132"
    "3333012301230123"
)
ORDER_LAST = (
    "020031030200032032131021221023031111122121103221001132201032213020132010020322002113203010"
    "103323011331023012321202310113201201330210122312130021122203120323012213201223302021102200"
    "011210223122100331213032331312212301231102302132103221011223113130210310020321312313000221"
    "123211022323202131023033033112033021101220310223112312313320211303213210301330232101103033"
    "213120102311223120013012002213310311032122033121133221222301121112302323020102130122111301"
    "221201221123032001202120111120320123131112011303003130012102121310010002211201331203221012"
    "102211012010302331001110212210101202312012300210321231021012030021201222104222200120320100"
    "300101013130010413120012330000110130201121200110011020010000211320001121001000210310310003"
    "000020102001100300112000021011101010300020103000210002114100020202201030010014130003003123"
    "100000004100022111220002221024003310000023300010214002030011121020010114320002100100010201"
    "234021120401000240000123012344444"
)
ORDER_B = (
    "743454434327472773502343225735405447433201274737700314265720756047311322317551605265020762"
    "057015163016235016177436616233740315662714672264023537464022173662516006521605346610127045"
    "223647517546051725136134051076434660153075421142300461015515"
)


class Mark:

    def __init__(self, engine, number):
        self.engine, self.number = engine, number


class Engine:

    def __init__(self, nc, queue, sem):
        self.nc, self.q, self.sem = nc, queue, sem
        self.count, self.loop, self.per_pass = 0, None, 0
        self.seen = {}

    def enter(self, sem, loop, per_pass):
        self.sem, self.loop, self.per_pass = sem, loop, per_pass
        self.count, self.seen = 0, {}

    def wait_apart(self, *marks):
        self.wait(*marks)
        self.q.sem_inc(self.passed, 1)

    def done(self, instruction):
        self.count += 1
        instruction.then_inc(self.sem, 1)
        return Mark(self, self.count)

    def wait(self, *marks):
        for m in marks:
            if m is None or self.seen.get(m.engine, -1) >= m.number:
                continue
            self.seen[m.engine] = m.number
            e = m.engine
            value = m.number if e.loop is None else e.loop * e.per_pass + m.number + 1
            self.q.wait_ge(e.sem, value)


def issue(lanes, order):
    lanes = [iter(lane) for lane in lanes]
    for n in order:
        next(lanes[int(n)], None)
    for lane in lanes:
        for _ in lane:
            raise ValueError("the order has too few steps")


def build(nc, a, out, signals):
    ctx = ExitStack()
    with ctx:

        def sb(name, shape, dt=F32):
            return ctx.enter_context(nc.sbuf_tensor(name, shape, dt))

        def sem(name):
            return ctx.enter_context(nc.semaphore(name))

        scratch = nc.dram_tensor("after_L3_xattn", (B, S, D), F32, kind="Internal").ap()
        psum = ctx.enter_context(nc.psum_tensor("psum", [P, 8, BANK], F32))

        pe = Engine(nc, nc.tensor, sem("pe_setup"))
        dve = Engine(nc, nc.vector, sem("dve_setup"))
        act = Engine(nc, nc.scalar, sem("act_setup"))
        pool = Engine(nc, nc.gpsimd, sem("pool_setup"))
        engines = {"pe": pe, "dve": dve, "act": act, "pool": pool}
        for name, e in engines.items():
            e.passed = sem(name + "_passed")
        ahead_sems = {e: sem(f"{e}_ahead") for e in engines}
        last_sems = {e: sem(f"{e}_last") for e in engines}
        loop_sems = {(l, e): sem(f"{e}_{l}") for l in "ab" for e in engines}
        s_load = {l: sem("loads_" + l.replace(" ", "_")) for l in ("L0", "L0 ffn", "L1", "MoE", "L2", "L3")}
        loaded = {l: 0 for l in s_load}
        group = "L0"

        planned = {l: [] for l in s_load}

        def load(dst, src):
            planned[group].append((dst, src))

        def start_loads(l):
            for dst, src in planned[l]:
                nc.sync.dma_start(dst, src).then_inc(s_load[l], 16)
                loaded[l] += 16
            planned[l] = []

        def wait_loads(l, *queues):
            for e in queues:
                e.q.wait_ge(s_load[l], loaded[l])

        ident = sb("ident", [P, P])
        ident_bf = sb("ident_bf", [P, P], BF16)
        ones = sb("ones", [P, P])
        head_rows = sb("head_rows", [P, 8])
        half_of = sb("half_of", [P, 2])
        causal = sb("causal", [P, P])
        minus_half = sb("minus_half", [P, 1])
        gates = sb("gates", [P, 8])
        first_of = sb("first_of", [P, E1])
        magic = sb("magic", [P, 1])

        load(gates[:, 0:4], a["g_xattn"].rearrange("(o n) -> o n", o=1).to_broadcast([P, 4]))
        load(gates[:, 4:8], a["g_ffn"].rearrange("(o n) -> o n", o=1).to_broadcast([P, 4]))

        w = {}

        def matrix(name, src, k, n, rows=P):
            w[name] = sb("w_" + name, [rows, k, n])
            load(w[name][:], src.rearrange("(k p) n -> p k n", k=k))

        def columns(name, src, n):
            w[name] = sb("w_" + name, [P, n])
            load(w[name][:], src)

        def row(name, src, n):
            w[name] = sb("w_" + name, [1, n])
            load(w[name][:], src.rearrange("(o n) -> o n", o=1))

        L1_SIZE = KD * H * 64
        wide_memory = sb("w_L1", [P, 4 * L1_SIZE])

        def attention_constants(l):
            if l == "L1":
                for n, (name, rows) in enumerate((("q", P), ("k", CC), ("v", CC), ("o", P))):
                    piece = wide_memory[0:rows, n * L1_SIZE:(n + 1) * L1_SIZE]
                    w["L1" + name] = piece.rearrange("p (k n) -> p k n", k=8 if name == "o" else 2)
                    load(w["L1" + name], a["L1_w" + name].rearrange("(k p) n -> p k n", p=rows))
            else:
                matrix(l + "q", a[l + "_wq"], KD, D)
                matrix(l + "k", a[l + "_wk"], KC, D, CC)
                matrix(l + "v", a[l + "_wv"], KC, D, CC)
                matrix(l + "o", a[l + "_wo"], KD, D)
                for n in ("bq", "bk", "bv"):
                    columns(l + n, a[l + "_" + n], KD)
            row(l + "bo", a[l + "_bo"], D)
            out_bias[l] = sb("out_bias_" + l, [P, D])

        out_bias = {}
        attention_constants("L0")
        group = "L0 ffn"
        w["conv"] = sb("w_conv", [P, HID0 // P, 3])
        load(w["conv"][:], a["L0_conv"].rearrange("(k p) t -> p k t", p=P))
        columns("convb", a["L0_convb"], HID0 // P)
        w["w1q"] = sb("w_w1q", [P, KD, HID0], BF16)
        w["w2q"] = sb("w_w2q", [P, HID0 // P, D], BF16)
        deq = sb("deq", [P, 2])
        bvb = sb("bvb", [P, KD, P])
        absum = sb("absum", [P, 4])
        group = "L1"
        attention_constants("L1")
        group = "MoE"
        matrix("router", a["L1_router"], KD, E1)
        matrix("experts", a["L1_experts"], KD, E1 * D)
        w["eb"] = sb("w_eb", [E1, D])
        load(w["eb"][:], a["L1_ffn_expert_b"])
        w["rb"] = sb("w_rb", [P, E1])
        load(w["rb"][:], a["L1_ffn_router_b"].rearrange("(o n) -> o n", o=1).to_broadcast([P, E1]))
        group = "L2"
        attention_constants("L2")
        for n in "qkv":
            matrix("self" + n, a["L2s_w" + n], KD, D)
        matrix("selfo", a["L2s_wo"], KD, D)
        matrix("gate", a["L2s_gate"], KD, E1)
        matrix("up", a["L2s_up"], KD, HID2)
        matrix("down", a["L2s_down"], HID2 // P, D)
        norms = sb("norms", [P, 2, KD])
        load(norms[:, 0, :], a["L2s_n1"])
        load(norms[:, 1, :], a["L2s_n2"])
        group = "L3"
        attention_constants("L3")
        gamma = sb("gamma", [P, BLOCKS, KD])
        beta = sb("beta", [P, BLOCKS, KD])
        load(gamma[:], a["L3_gamma"])
        load(beta[:], a["L3_beta"])

        class Lane:
            pass

        lane_ctx = ExitStack()

        def lane_buffers(n):
            t = Lane()

            def buf(name, shape, dt=F32):
                return lane_ctx.enter_context(nc.sbuf_tensor(f"{name}_{n}", shape, dt))

            t.n = n
            t.a, t.b = psum[:, 2 * n, :], psum[:, 2 * n + 1, :]
            t.x_in = buf("x_in", [P, D])
            t.ctxT = buf("ctxT", [CC, KC, S])
            t.x = buf("x", [P, D])
            t.xn = buf("xn", [P, D])
            t.xnT = buf("xnT", [P, KD, S])
            t.stats = buf("stats", [P, 6])
            t.mv = buf("mv", [P, 2])
            t.tiny = buf("tiny", [P, 64])
            big = buf("big", [P, 4 * BANK])
            t.e = [big[:, n * BANK:(n + 1) * BANK].rearrange("p (h s) -> p h s", h=CH) for n in range(2)]
            t.eT = big[:, 2 * BANK:3 * BANK].rearrange("p (h s) -> p h s", h=CH)
            t.kT = big[:, 3 * BANK:4 * BANK].rearrange("p (k s) -> p k s", s=S)
            t.hid = big[:, 0:2 * BANK].rearrange("p (k s) -> p k s", s=S)
            t.act = big[:, 2 * BANK:4 * BANK].rearrange("p (k s) -> p k s", s=S)
            t.rounded = big[:, 0:2 * BANK]
            keys = buf("head_keys", [P, 2 * BANK])
            small = buf("small", [P, 2 * BANK + 32])
            t.qT = small[:, 0:D].rearrange("p (k s) -> p k s", s=S)
            t.o = t.un = small[:, D:2 * D]
            t.v = small[:, 2 * D:2 * D + H * 17]
            t.oT = small[:, 3 * D + 32:4 * D + 32].rearrange("p (k s) -> p k s", s=S)
            t.xi = small[:, 0:BANK].bitcast(BF16)
            t.xiT = small[:, BANK:2 * BANK].bitcast(BF16).rearrange("p (k s) -> p k s", s=S)
            t.diag, t.row_scale = t.act[:, 0, :], t.xnT[:, 0, :]
            t.wtT = t.un[0:E1, 0:S]
            t.head_keys = [keys[:, n * BANK:(n + 1) * BANK].rearrange("p (h s) -> p h s", h=CH) for n in range(2)]
            t.loaded_x, t.loaded_c = sem(f"loaded_x_{n}"), sem(f"loaded_c_{n}")
            t.stored = sem(f"stored_{n}")
            return t

        lanes = [lane_buffers(n) for n in range(LANES_A)]
        group = "L0 ffn"
        start_loads("L0")
        for t in reversed(lanes):
            nc.sync.dma_start(t.x_in[:], a["x"][t.n]).then_inc(t.loaded_x, 16)
            nc.sync.dma_start(t.ctxT[:], a["ctxT"][t.n].rearrange("(k p) s -> p k s", k=KC)).then_inc(t.loaded_c, 16)
        experts_memory = w["experts"][:].rearrange("p k n -> p (k n)")
        raw = [experts_memory[:, n * KD * HID0:(n + 1) * KD * HID0] for n in range(2)]
        load(raw[0][:].rearrange("p (k n) -> p k n", k=KD), a["L0_w1"].rearrange("(k p) n -> p k n", p=P))
        load(raw[1][:].rearrange("p (k n) -> p k n", n=D), a["L0_w2"].rearrange("(k p) n -> p k n", p=P))
        for l in ("L0 ffn", "L1", "L2", "L3"):
            start_loads(l)

        pool.q.memset(ident[:], 0.0)
        pool.q.memset(causal[:], 3.0e38)
        pool.q.memset(minus_half[:], -0.5)
        for r in range(2):
            dve.q.memset(half_of[0:64, r:r + 1], 1.0 - r)
            dve.q.memset(half_of[64:P, r:r + 1], 0.0 + r)
        pool.q.memset(magic[:, 0:1], MAGIC)
        pool.q.memset(head_rows[:], 1.0)
        m = pool.done(pool.q.memset(ones[:], 1.0))
        pool.wait(m)
        pool.q.affine_select(out=ident[:], in_=ident[:], compare_op=ALU.not_equal, fill=1.0, base=0,
                             pattern=[[-1, P]], channel_multiplier=1)
        m = pool.done(pool.q.affine_select(out=causal[:], in_=causal[:], compare_op=ALU.is_ge, fill=4 * MASKED,
                                           base=0, pattern=[[-1, P]], channel_multiplier=1))
        pool.wait(m)
        m = pool.done(pool.q.affine_select(out=head_rows[:], in_=head_rows[:], compare_op=ALU.is_ge, fill=0.0, base=0,
                                           pattern=[[-16, 8]], channel_multiplier=1))
        pool.wait(m)
        consts_ready = pool.done(pool.q.affine_select(
            out=head_rows[:], in_=head_rows[:], compare_op=ALU.is_ge, fill=0.0, base=15, pattern=[[16, 8]],
            channel_multiplier=-1))
        dve.wait(consts_ready)
        dve_consts = dve.done(dve.q.tensor_copy(ident_bf[:], ident[:]))

        wait_loads("L0", act, dve, pe)
        tanh_gates = act.done(act.q.activation(gates[:], gates[:], ACT.Tanh))
        dve.wait(tanh_gates)
        gx = {l: gates[:, n:n + 1] for n, l in enumerate(["L0", "L1", "L2", "L3"])}
        gf = {l: gates[:, 4 + n:5 + n] for n, l in enumerate(["L0", "L1", "L2", "L3"])}

        def scale(name, by):
            return dve.q.tensor_scalar(w[name][:], w[name][:], by, None, ALU.mult)

        def fold_output(l, bank):
            scale(l + "o", gx[l])
            last = dve.q.tensor_scalar(w[l + "bo"][:], w[l + "bo"][:], gx[l][0:1], None, ALU.mult)
            if l != "L1":
                for k in range(KD):
                    last = dve.q.tensor_copy(bvb[:, k, :], w[l + "bv"][:, k:k + 1].to_broadcast([P, P]))
            pe.wait(dve.done(last))
            if l != "L1":
                for k in range(KD):
                    pe.q.matmul(bank[:, 0:D], bvb[:, k, :], w[l + "o"][:, k, :], start=k == 0, stop=False)
            m = pe.done(pe.q.matmul(bank[:, 0:D], ones[0:1, :], w[l + "bo"][:], start=l == "L1", stop=True))
            dve.wait(m)
            return dve.done(dve.q.tensor_copy(out_bias[l][:], bank[:, 0:D]))

        pe.wait(consts_ready, dve_consts)
        first_ready = fold_output("L0", psum[:, 0, :])
        for e in (pe, act, pool):
            e.wait(first_ready)

        constants_of = {}

        def quantised():
            for n in range(2):
                last = dve.q.tensor_reduce(absum[:, n:n + 1], raw[n][:], AX.X, ALU.add, apply_absolute_value=True)
            pe.wait(dve.done(last))
            m = pe.done(pe.q.matmul(lanes[0].b[:, 0:2], ones[:], absum[:, 0:2], start=True, stop=True))
            yield
            dve.wait(m)
            m = dve.done(dve.q.tensor_scalar(absum[:, 0:2], lanes[0].b[:, 0:2], 1.0 / (HID0 * D), 1e-5,
                                             ALU.mult, ALU.max))
            dve.wait(m)
            dve.q.tensor_scalar(deq[:, 0:1], absum[:, 0:1], 1.0 / 127.0, None, ALU.mult)
            dve.q.tensor_scalar(deq[:, 1:2], absum[:, 1:2], gf["L0"], 0.5 / 127.0, ALU.mult, ALU.mult)
            m = dve.done(dve.q.reciprocal(absum[:, 2:4], absum[:, 0:2]))
            yield
            for n, name in enumerate(["w1q", "w2q"]):
                dve.wait(m)
                m = dve.done(dve.q.tensor_scalar(raw[n][:], raw[n][:], absum[:, 2 + n:3 + n], MAGIC, ALU.mult, ALU.add))
                dve.wait(m)
                m = dve.done(dve.q.tensor_scalar(raw[n][:], raw[n][:], -MAGIC, 1.0, ALU.add, ALU.min))
                dve.wait(m)
                flat = w[name][:].rearrange("p k n -> p (k n)")
                m = dve.done(dve.q.tensor_scalar(flat, raw[n][:], -1.0, None, ALU.max))
                constants_of[name] = m
                yield

        def sync_wait(m):
            e = m.engine
            nc.sync.wait_ge(e.sem, m.number if e.loop is None else e.loop * e.per_pass + m.number + 1)

        def later_constants():
            bank = lanes[0].a
            wait_loads("L0 ffn", dve, pe, act)
            yield from quantised()
            sync_wait(constants_of["w2q"])
            start_loads("MoE")
            wait_loads("L1", dve, pe)
            constants_of["L1"] = fold_output("L1", bank)
            yield
            wait_loads("MoE", dve)
            scale("experts", gf["L1"])
            last = dve.q.tensor_scalar(w["eb"][:], w["eb"][:], gf["L1"][0:E1], None, ALU.mult)
            yield
            wait_loads("L2", dve, pe)
            dve.wait(constants_of["L1"])
            constants_of["L2"] = fold_output("L2", bank)
            dve.q.tensor_scalar(w["down"][:], w["down"][:], gf["L2"], 0.5, ALU.mult, ALU.mult)
            yield
            for name, n in (("selfq", 0), ("selfk", 0), ("selfv", 0), ("gate", 1), ("up", 1)):
                for k in range(KD):
                    dve.q.tensor_scalar(w[name][:, k, :], w[name][:, k, :], norms[:, n, k:k + 1], None, ALU.mult)
            yield
            wait_loads("L3", dve, pe)
            dve.wait(constants_of["L2"])
            constants_of["L3"] = fold_output("L3", bank)

        def layernorm(t, src, src_ready=None):
            dve.wait(src_ready)
            m = dve.done(dve.q.bn_stats(t.stats[:], src))
            dve.wait_apart(m)
            m = dve.done(dve.q.bn_aggr(t.mv[:], t.stats[:]))
            dve.wait(m)
            m = dve.done(dve.q.tensor_scalar(t.tiny[:, 0:1], t.mv[:, 1:2], LN_EPS, None, ALU.add))
            pool.wait(m)
            m = pool.done(pool.q.tensor_tensor(t.tiny[:, 1:2], t.tiny[:, 0:1], minus_half[:], ALU.pow))
            yield
            dve.wait(m)
            return dve.done(dve.q.tensor_scalar(t.xn[:], src, t.mv[:, 0:1], t.tiny[:, 1:2],
                                                ALU.subtract, ALU.mult))

        def transposes(bank, src, chunks, identity=None):
            for k in range(chunks):
                last = pe.q.transpose(bank[:, k * P:(k + 1) * P], src[:, k * P:(k + 1) * P],
                                      ident[:] if identity is None else identity)
            return last

        def two_transposed(t, dst, src, src_ready):
            pe.wait(t.a_free, src_ready)
            m = pe.done(transposes(t.a, src, KD))
            yield
            act.wait(m)
            t.a_free = act.done(act.q.activation(dst[:], t.a[:, 0:D].rearrange("p (k s) -> p k s", s=S), ACT.Copy))
            return t.a_free

        def features_T(bank, wt, src, rows, outs):
            for j, n in enumerate(outs):
                for k in range(KD):
                    last = pe.q.matmul(bank[:, j * S:(j + 1) * S], wt[0:rows, k, n * P:(n + 1) * P],
                                       src[0:rows, k, :], start=k == 0, stop=k == KD - 1)
            return last

        def tokens(bank, srcT, wt, n, rows=P, chunks=KD, c0=0):
            for k in range(chunks):
                last = pe.q.matmul(bank[:, 0:n], srcT[0:rows, k, :], wt[0:rows, k, c0:c0 + n],
                                   start=k == 0, stop=k == chunks - 1)
            return last

        def softmax(t, c, scale, scores_ready, clip=None, masked=False):
            s4 = t.a.rearrange("p (h s) -> p h s", h=CH)
            yield
            dve.wait(scores_ready)
            if clip:
                dve.wait(dve.done(dve.q.tensor_scalar(t.a, t.a, clip / scale, -clip / scale, ALU.min, ALU.max)))
            if masked:
                dve.wait(dve.done(dve.q.tensor_tensor(s4, s4, causal[:].rearrange("p (o s) -> p o s", o=1)
                                                      .to_broadcast([P, CH, S]), ALU.min)))
            top = t.tiny[:, 8 + 4 * (c % 2):12 + 4 * (c % 2)]
            dve.wait(dve.done(dve.q.tensor_reduce(top, s4, AX.X, ALU.max)))
            t.a_free = dve.done(dve.q.tensor_tensor(t.e[c % 2], s4, top.rearrange("p (h o) -> p h o", o=1)
                                                    .to_broadcast([P, CH, S]), ALU.subtract))
            yield
            act.wait(t.a_free)
            flat = t.e[c % 2].rearrange("p h s -> p (h s)")
            return act.done(act.q.activation(flat, flat, ACT.Exp, scale=scale))

        def transposed_probabilities(t, c, e_ready):
            pe.wait(t.b_free, e_ready)
            m = pe.done(transposes(t.b, t.e[c % 2].rearrange("p h s -> p (h s)"), CH))
            yield
            act.wait(m)
            t.b_free = act.done(act.q.activation(t.eT.rearrange("p h s -> p (h s)"), t.b, ACT.Copy))
            return t.b_free

        def weighted_values(t, values, eT_ready):
            pe.wait(eT_ready)
            n = values[0].shape[-1]
            for j in range(CH):
                last = pe.q.matmul(t.b[:, j * n:(j + 1) * n], t.eT[:, j, :], values[j], start=True, stop=True)
            m = pe.done(last)
            yield
            dve.wait(m)
            got = t.b[:, 0:CH * n].rearrange("p (h d) -> p h d", h=CH)
            den = t.tiny[:, 32:32 + CH].rearrange("p (h o) -> p h o", o=1)
            dve.wait(dve.done(dve.q.reciprocal(den, got[:, :, n - 1:n])))
            return got[:, :, 0:n - 1], den

        def narrow_attention(t, l, x_ready, kv, kv_rows, clip=None, masked=False, kv_wait=None, kv_done=None):
            dh = D // H
            v = t.v.rearrange("p (h d) -> p h d", h=H)
            pe.wait(t.a_free, x_ready)
            m = pe.done(features_T(t.a, w[l + "q"], t.xnT, P, range(KD)))
            yield
            act.wait(m)
            for k in range(KD):
                src = t.a[:, k * S:(k + 1) * S]
                if l == "self":
                    last = act.q.activation(t.qT[:, k, :], src, ACT.Copy)
                else:
                    last = act.q.activation(t.qT[:, k, :], src, ACT.Identity, bias=w[l + "bq"][:, k:k + 1])
            t.a_free = q_ready = act.done(last)
            yield
            if kv_wait:
                kv_wait()
            pe.wait(t.b_free)
            m = pe.done(features_T(t.b, w[l + "k"], kv, kv_rows, range(KD)))
            yield
            act.wait(m)
            for k in range(KD):
                src = t.b[:, k * S:(k + 1) * S]
                if l == "self":
                    last = act.q.activation(t.kT[:, k, :], src, ACT.Copy)
                else:
                    last = act.q.activation(t.kT[:, k, :], src, ACT.Identity, bias=w[l + "bk"][:, k:k + 1])
            t.b_free = k_ready = act.done(last)
            pool.wait_apart(q_ready)
            v_ones = pool.done(pool.q.memset(v[:, :, dh:dh + 1], 1.0))
            yield
            pe.wait(t.a_free)
            m = pe.done(tokens(t.a, kv, w[l + "v"], D, kv_rows))
            if kv_done:
                kv_done(m)
            yield
            act.wait(m)
            t.a_free = v_ready = act.done(act.q.activation(
                v[:, :, 0:dh], t.a[:, 0:D].rearrange("p (h d) -> p h d", h=H), ACT.Copy))
            yield
            slot_read = [None, None]

            def keys_apart(c):
                pool.wait(k_ready, slot_read[c % 2])
                return pool.done(pool.q.tensor_tensor(
                    t.head_keys[c % 2], t.kT[:, c // 2:c // 2 + 1, :].to_broadcast([P, CH, S]),
                    head_rows[:, CH * (c % 2):CH * (c % 2 + 1)].rearrange("p (h o) -> p h o", o=1)
                    .to_broadcast([P, CH, S]), ALU.mult))

            def scores(c):
                pe.wait(t.a_free, q_ready, keys[c])
                slot_read[c % 2] = pe.done(pe.q.matmul(
                    t.a, t.qT[:, c // 2, :], t.head_keys[c % 2].rearrange("p h s -> p (h s)"), start=True, stop=True))
                return (yield from softmax(t, c, dh ** -0.5, slot_read[c % 2], clip, masked))

            keys = {0: keys_apart(0), 1: keys_apart(1)}
            e_ready = [(yield from scores(0)), None]
            yield
            for c in range(4):
                if c + 1 < 4:
                    e_ready[(c + 1) % 2] = yield from scores(c + 1)
                    if c + 2 < 4:
                        keys[c + 2] = keys_apart(c + 2)
                    yield
                eT_ready = yield from transposed_probabilities(t, c, e_ready[c % 2])
                yield
                pe.wait(v_ready, v_ones)
                got, den = yield from weighted_values(t, [v[:, CH * c + j, :] for j in range(CH)], eT_ready)
                t.b_free = dve.done(dve.q.tensor_tensor(
                    t.o[:, CH * dh * c:CH * dh * (c + 1)].rearrange("p (h d) -> p h d", h=CH), got,
                    den.to_broadcast([P, CH, dh]), ALU.mult))
                yield
            oT_ready = yield from two_transposed(t, t.oT, t.o, t.b_free)
            yield
            pe.wait(t.b_free, oT_ready)
            t.result_ready = pe.done(tokens(t.b, t.oT, w[l + "o"], D))

        def wide_attention(t, x_ready, kv, kv_rows):
            dh = 64
            v = t.v[:, 0:CH * (dh + 1)].rearrange("p (h d) -> p h d", h=CH)
            o3 = t.o.rearrange("p (h d) -> p h d", h=CH)
            pool.wait_apart(x_ready)
            v_ones = pool.done(pool.q.memset(v[:, :, dh:dh + 1], 1.0))
            for g in range(4):
                pe.wait(t.a_free, x_ready)
                m = pe.done(features_T(t.a, w["L1q"], t.xnT, P, range(2 * g, 2 * g + 2)))
                yield
                act.wait(m)
                t.a_free = q_ready = act.done(act.q.activation(
                    t.qT, t.a[:, 0:D].rearrange("p (k s) -> p k s", s=S), ACT.Copy))
                yield
                pe.wait(t.b_free)
                m = pe.done(features_T(t.b, w["L1k"], kv, kv_rows, range(2 * g, 2 * g + 2)))
                yield
                dve.wait(m)
                kT4 = t.kT.rearrange("p (k r) s -> p k r s", r=2)
                for r in range(2):
                    last = dve.q.tensor_scalar(kT4[:, :, r, :], t.b[:, 0:D].rearrange("p (k s) -> p k s", s=S),
                                               half_of[:, r:r + 1], None, ALU.mult)
                t.b_free = k_ready = dve.done(last)
                yield
                pe.wait(t.a_free, q_ready, k_ready)
                for k in range(2):
                    last = pe.q.matmul(t.a[:, 2 * k * S:2 * (k + 1) * S], t.qT[:, k, :],
                                       t.kT[:, 2 * k:2 * k + 2, :].rearrange("p k s -> p (k s)"), start=True, stop=True)
                e_ready = yield from softmax(t, g, dh ** -0.5, pe.done(last))
                yield
                pe.wait(t.b_free)
                m = pe.done(tokens(t.b, kv, w["L1v"], CH * dh, kv_rows, c0=g * CH * dh))
                yield
                act.wait(m)
                t.b_free = v_ready = act.done(act.q.activation(
                    v[:, :, 0:dh], t.b[:, 0:CH * dh].rearrange("p (h d) -> p h d", h=CH), ACT.Copy))
                yield
                eT_ready = yield from transposed_probabilities(t, g, e_ready)
                yield
                pe.wait(v_ready, v_ones)
                got, den = yield from weighted_values(t, [v[:, j, :] for j in range(CH)], eT_ready)
                t.b_free = dve.done(dve.q.tensor_tensor(o3, got, den.to_broadcast([P, CH, dh]), ALU.mult))
                yield
                oT_ready = yield from two_transposed(t, t.oT, t.o, t.b_free)
                yield
                pe.wait(t.b_free, oT_ready)
                for k in range(2):
                    last = pe.q.matmul(t.b[:, 0:D], t.oT[:, k, :], w["L1o"][:, 2 * g + k, :], start=k == 0, stop=k == 1)
                t.result_ready = pe.done(last)
                if g < 3:
                    dve.wait(t.result_ready, t.x_ready)
                    t.b_free = t.x_ready = dve.done(dve.q.tensor_tensor(t.x[:], t.b[:, 0:D], t.x[:], ALU.add))
                    yield

        def cross_attention(t, l, src, clip=None, x_wait=None, kv_wait=None, kv_done=None):
            m = yield from layernorm(t, src, t.x_ready)
            yield
            xnT_ready = yield from two_transposed(t, t.xnT, t.xn, m)
            if x_wait:
                x_wait()
            pool.wait(m)
            t.x_ready = t.x_in_free = pool.done(pool.q.tensor_tensor(t.x[:], src, out_bias[l][:], ALU.add))
            yield
            if l == "L1":
                yield from wide_attention(t, xnT_ready, t.ctxT, CC)
            else:
                yield from narrow_attention(t, l, xnT_ready, t.ctxT, CC, clip=clip, kv_wait=kv_wait, kv_done=kv_done)
            dve.wait(t.result_ready, t.x_ready)
            t.b_free = t.x_ready = dve.done(dve.q.tensor_tensor(t.x[:], t.b[:, 0:D], t.x[:], ALU.add))
            yield

        def bitlinear_ffn(t):
            mx, rs, sc = t.tiny[:, 2:3], t.tiny[:, 3:4], t.tiny[:, 4:5]
            m = yield from layernorm(t, t.x[:], t.x_ready)
            dve.wait(m)
            dve.wait(dve.done(dve.q.tensor_reduce(mx, t.xn[:], AX.X, ALU.max, apply_absolute_value=True)))
            dve.wait(dve.done(dve.q.tensor_scalar(mx, mx, 1e-5, None, ALU.max)))
            dve.wait(dve.done(dve.q.reciprocal(rs, mx)))
            dve.wait(dve.done(dve.q.tensor_scalar(rs, rs, 127.0, None, ALU.mult)))
            dve.wait(dve.done(dve.q.tensor_scalar(t.rounded[:, 0:D], t.xn[:], rs, MAGIC, ALU.mult, ALU.add)))
            xi_ready = dve.done(dve.q.tensor_scalar(t.xi[:, 0:D], t.rounded[:, 0:D], -MAGIC, None, ALU.add))
            yield
            dve.wait(dve.done(dve.q.tensor_scalar(sc, mx, deq[:, 0:1], None, ALU.mult)))
            diag_ready = dve.done(dve.q.tensor_scalar(t.diag, ident[:], sc, None, ALU.mult))
            yield
            bf = t.a[:, 0:P].bitcast(BF16)
            pe.wait(t.a_free, xi_ready)
            m = pe.done(transposes(bf, t.xi, KD, ident_bf[:]))
            yield
            act.wait(m)
            t.a_free = xiT_ready = act.done(act.q.activation(t.xiT[:, 0:KD, :], bf.rearrange("p (k s) -> p k s", k=KD),
                                                             ACT.Copy))
            yield
            pe.wait(t.b_free, diag_ready)
            m = pe.done(pe.q.matmul(t.b[:, 0:S], ones[:], t.diag, start=True, stop=True))
            yield
            act.wait(m)
            t.b_free = rows_ready = act.done(act.q.activation(t.row_scale, t.b[:, 0:S], ACT.Copy))
            yield
            centre = []
            for half, bank in enumerate((t.a, t.b)):
                ks = range(4 * half, 4 * half + 4)
                pe.wait(xiT_ready, (t.a_free, t.b_free)[half])
                m = pe.done(features_T(bank, w["w1q"], t.xiT, P, ks))
                yield
                dve.wait(m, rows_ready)
                m = dve.done(dve.q.tensor_tensor(
                    t.hid[:, 4 * half:4 * half + 4, :], bank.rearrange("p (k s) -> p k s", s=S),
                    t.row_scale.rearrange("p (o s) -> p o s", o=1).to_broadcast([P, 4, S]), ALU.mult))
                if half == 0:
                    t.a_free = m
                else:
                    t.b_free = m
                yield
                act.wait(m)
                for k in ks:
                    m = act.q.activation(t.act[:, k, :], t.hid[:, k, :], ACT.Identity,
                                         bias=w["convb"][:, k:k + 1], scale=w["conv"][:, k, 1:2])
                centre.append(act.done(m))
                yield
            silu_ready = []
            for half in range(2):
                ks = range(4 * half, 4 * half + 4)
                sl = slice(4 * half, 4 * half + 4)
                dve.wait(centre[half])
                for k in ks:
                    m = dve.done(dve.q.scalar_tensor_tensor(
                        t.act[:, k, 1:S], t.hid[:, k, 0:S - 1], w["conv"][:, k, 0:1], t.act[:, k, 1:S],
                        ALU.mult, ALU.add))
                yield
                dve.wait(m)
                for k in ks:
                    m = dve.q.scalar_tensor_tensor(
                        t.act[:, k, 0:S - 1], t.hid[:, k, 1:S], w["conv"][:, k, 2:3], t.act[:, k, 0:S - 1],
                        ALU.mult, ALU.add)
                conv_ready = dve.done(m)
                yield
                act.wait(conv_ready)
                m = act.done(act.q.activation(t.hid[:, sl, :], t.act[:, sl, :], ACT.Tanh, scale=0.5))
                yield
                dve.wait(m, conv_ready)
                silu_ready.append(dve.done(dve.q.scalar_tensor_tensor(
                    t.act[:, sl, :], t.hid[:, sl, :], 1.0, t.act[:, sl, :], ALU.add, ALU.mult)))
                yield
            for half, bank in enumerate((t.a, t.b)):
                pe.wait(silu_ready[half], (t.a_free, t.b_free)[half])
                m = pe.done(transposes(bank, t.act[:, 4 * half:4 * half + 4, :].rearrange("p k s -> p (k s)"), 4))
                yield
                dve.wait(m)
                m = dve.done(dve.q.tensor_reduce(t.tiny[:, 5 + half:6 + half], bank, AX.X, ALU.max,
                                                 apply_absolute_value=True))
                yield
            dve.wait(m)
            dve.wait(dve.done(dve.q.tensor_tensor(mx, t.tiny[:, 5:6], t.tiny[:, 6:7], ALU.max)))
            dve.wait(dve.done(dve.q.tensor_scalar(mx, mx, 2e-5, None, ALU.max)))
            dve.wait(dve.done(dve.q.reciprocal(rs, mx)))
            rs_ready = dve.done(dve.q.tensor_scalar(rs, rs, 127.0, None, ALU.mult))
            sc_ready = dve.done(dve.q.tensor_scalar(sc, mx, deq[:, 1:2], None, ALU.mult))
            yield
            for half, bank in enumerate((t.a, t.b)):
                cols = slice(half * BANK, (half + 1) * BANK)
                act.wait(rs_ready)
                m = act.done(act.q.activation(t.rounded[:, cols], bank, ACT.Identity, bias=magic[:, 0:1], scale=rs))
                yield
                dve.wait(m)
                xi_ready = dve.done(dve.q.tensor_scalar(t.xi[:, cols], t.rounded[:, cols], -MAGIC, None, ALU.add))
                yield
                bf = bank[:, 0:2 * P].bitcast(BF16)
                pe.wait(m, xi_ready)
                m = pe.done(transposes(bf, t.xi[:, cols], 4, ident_bf[:]))
                yield
                act.wait(m)
                xiT_ready = act.done(act.q.activation(t.xiT[:, 4 * half:4 * half + 4, :],
                                                      bf.rearrange("p (k s) -> p k s", k=4), ACT.Copy))
                if half == 0:
                    t.a_free = xiT_ready
                else:
                    t.b_free = xiT_ready
                yield
            pe.wait(xiT_ready)
            m = pe.done(tokens(t.a, t.xiT, w["w2q"], D, chunks=HID0 // P))
            yield
            dve.wait(m, sc_ready)
            t.a_free = t.x_ready = dve.done(dve.q.scalar_tensor_tensor(t.x[:], t.a[:, 0:D], sc, t.x[:],
                                                                       ALU.mult, ALU.add))
            yield

        def moe_ffn(t):
            xn_ready = yield from layernorm(t, t.x[:], t.x_ready)
            yield
            xnT_ready = yield from two_transposed(t, t.xnT, t.xn, xn_ready)
            yield
            pe.wait(t.b_free, xnT_ready)
            m = pe.done(tokens(t.b, t.xnT, w["router"], E1))
            lg, ex, wt, mx, sm = t.tiny[:, 8:16], t.tiny[:, 16:24], t.tiny[:, 24:32], t.tiny[:, 2:3], t.tiny[:, 3:4]
            dve.wait(m)
            t.b_free = m = dve.done(dve.q.tensor_tensor(lg, t.b[:, 0:E1], w["rb"][:], ALU.add))
            dve.wait(m)
            dve.wait(dve.done(dve.q.tensor_reduce(mx, lg, AX.X, ALU.max)))
            m = dve.done(dve.q.tensor_scalar(lg, lg, mx, None, ALU.subtract))
            act.wait(m)
            exp_ready = act.done(act.q.activation(ex, lg, ACT.Exp, accum_out=sm))
            dve.wait(m)
            dve.wait(dve.done(dve.q.scalar_tensor_tensor(wt, lg, 0.0, first_of[:], ALU.is_equal, ALU.mult)))
            dve.wait(dve.done(dve.q.tensor_reduce(mx, wt, AX.X, ALU.max)))
            dve.wait(exp_ready)
            dve.wait(dve.done(dve.q.reciprocal(sm, sm)))
            wt_ready = dve.done(dve.q.tensor_scalar(wt, wt, mx, sm, ALU.is_equal, ALU.mult))
            yield
            pe.wait(t.b_free, wt_ready)
            m = pe.done(pe.q.transpose(t.b[0:E1, 0:P], wt, ident[:]))
            yield
            act.wait(m)
            t.b_free = wtT_ready = act.done(act.q.activation(t.wtT, t.b[0:E1, 0:P], ACT.Copy))
            yield
            for pair in range(E1 // 2):
                bank = (t.a, t.b)[pair % 2]
                pe.wait((t.a_free, t.b_free)[pair % 2])
                m = pe.done(tokens(bank, t.xnT, w["experts"], BANK, c0=pair * BANK))
                for j in range(2):
                    e = 2 * pair + j
                    dve.wait(m, wt_ready, t.x_ready)
                    m = t.x_ready = dve.done(dve.q.scalar_tensor_tensor(
                        t.x[:], bank[:, j * D:(j + 1) * D], wt[:, e:e + 1], t.x[:], ALU.mult, ALU.add))
                if pair % 2 == 0:
                    t.a_free = m
                else:
                    t.b_free = m
                yield
            pe.wait(t.a_free, wtT_ready)
            m = pe.done(pe.q.matmul(t.a[:, 0:D], t.wtT, w["eb"][:], start=True, stop=True))
            yield
            dve.wait(m, t.x_ready)
            t.a_free = t.x_ready = dve.done(dve.q.tensor_tensor(t.x[:], t.a[:, 0:D], t.x[:], ALU.add))
            yield

        def transformer_ffn(t):
            u_ready = yield from layernorm(t, t.x[:], t.x_ready)
            ms, rr, f1, f2 = t.tiny[:, 2:3], t.tiny[:, 3:4], t.tiny[:, 4:5], t.tiny[:, 5:6]
            u, un = t.xn, t.un
            dve.wait(u_ready)

            def rms(ready):
                act.wait(ready)
                m = act.done(act.q.activation(un, u[:], ACT.Square, accum_out=ms))
                pool.wait_apart(m)
                m = pool.done(pool.q.tensor_scalar(rr, ms, 1.0 / D, RMS_EPS, ALU.mult, ALU.add))
                pool.wait(m)
                m = pool.done(pool.q.tensor_tensor(f1, rr, minus_half[:], ALU.pow))
                dve.wait(m)
                return dve.done(dve.q.tensor_scalar(un, u[:], f1, None, ALU.mult))

            un_ready = rms(u_ready)
            yield
            unT_ready = yield from two_transposed(t, t.xnT, un, un_ready)
            yield
            yield from narrow_attention(t, "self", unT_ready, t.xnT, P, masked=True)
            dve.wait(t.result_ready)
            t.b_free = u_ready = dve.done(dve.q.tensor_tensor(u[:], t.b[:, 0:D], u[:], ALU.add))
            un_ready = rms(u_ready)
            dve.wait(u_ready)
            x_u = dve.done(dve.q.scalar_tensor_tensor(t.x[:], u[:], gf["L2"], t.x[:], ALU.mult, ALU.add))
            yield
            unT_ready = yield from two_transposed(t, t.xnT, un, un_ready)
            yield
            pe.wait(t.b_free, unT_ready)
            m = pe.done(tokens(t.b, t.xnT, w["gate"], E1))
            lg, top, sm = t.tiny[:, 8:16], t.tiny[:, 16:24], t.tiny[:, 6:7]
            dve.wait(m)
            dve.wait(dve.done(dve.q.tensor_reduce(sm, t.b[:, 0:E1], AX.X, ALU.max)))
            t.b_free = m = dve.done(dve.q.tensor_scalar(lg, t.b[:, 0:E1], sm, None, ALU.subtract))
            act.wait(m)
            m = act.done(act.q.activation(lg, lg, ACT.Exp, accum_out=sm))
            yield
            dve.wait_apart(m)
            dve.wait(dve.done(dve.q.max(top, lg)))
            dve.wait(dve.done(dve.q.reciprocal(sm, sm)))
            dve.wait(dve.done(dve.q.tensor_scalar(top[:, 0:2], top[:, 0:2], sm, None, ALU.mult)))
            dve.wait(dve.done(dve.q.tensor_tensor(rr, top[:, 0:1], top[:, 1:2], ALU.add)))
            dve.wait(dve.done(dve.q.tensor_scalar(f1, rr, 1e-9, None, ALU.add)))
            dve.wait(dve.done(dve.q.reciprocal(f2, f1)))
            f_ready = dve.done(dve.q.tensor_scalar(f2, f2, rr, None, ALU.mult))
            yield
            silu_ready = []
            for half, bank in enumerate((t.a, t.b)):
                pe.wait(unT_ready, (t.a_free, t.b_free)[half])
                m = pe.done(features_T(bank, w["up"], t.xnT, P, range(4 * half, 4 * half + 4)))
                yield
                act.wait(m)
                view = bank.rearrange("p (k s) -> p k s", s=S)
                sl = slice(4 * half, 4 * half + 4)
                m = act.done(act.q.activation(t.hid[:, sl, :], view, ACT.Tanh, scale=0.5))
                yield
                dve.wait(m)
                m = dve.done(dve.q.scalar_tensor_tensor(t.act[:, sl, :], t.hid[:, sl, :], 1.0, view, ALU.add, ALU.mult))
                silu_ready.append(m)
                yield
            t.a_free, t.b_free = silu_ready
            pe.wait(*silu_ready)
            m = pe.done(tokens(t.a, t.act, w["down"], D, chunks=HID2 // P))
            yield
            dve.wait(m, f_ready, x_u)
            t.a_free = t.x_ready = dve.done(dve.q.scalar_tensor_tensor(t.x[:], t.a[:, 0:D], f2, t.x[:],
                                                                       ALU.mult, ALU.add))
            yield

        STAGES = 7

        def sequence(t, first, end, batch):
            def x_left():
                for e in (dve, pool):
                    e.q.wait_ge(t.stored, 16 * batch + 1)

            def context_loaded():
                pe.q.wait_ge(t.loaded_c, 16 * batch + 16)

            def next_context(m):
                sync_wait(m)
                nc.sync.dma_start(t.ctxT[:], a["ctxT"][(batch + 1) % passes_a * LANES_A + t.n]
                                  .rearrange("(k p) s -> p k s", k=KC)).then_inc(t.loaded_c, 16)

            for n in range(first, end):
                if n == 0:
                    for e in (dve, pool):
                        e.q.wait_ge(t.loaded_x, 16 * batch + 16)
                    yield from cross_attention(t, "L0", t.x_in[:], x_wait=x_left, kv_wait=context_loaded)
                    sync_wait(t.x_in_free)
                    nc.sync.dma_start(t.x_in[:], a["x"][(batch + 1) % passes_a * LANES_A + t.n]
                                      ).then_inc(t.loaded_x, 16)
                elif n == 1:
                    yield from bitlinear_ffn(t)
                elif n == 2:
                    yield from cross_attention(t, "L1", t.x[:])
                elif n == 3:
                    yield from moe_ffn(t)
                elif n == 4:
                    yield from cross_attention(t, "L2", t.x[:], clip=10000.0)
                elif n == 5:
                    yield from transformer_ffn(t)
                else:
                    yield from cross_attention(t, "L3", t.x[:], kv_done=next_context)
                    sync_wait(t.x_ready)
                    nc.sync.dma_start(scratch[batch * LANES_A + t.n], t.x[:]).then_inc(t.stored, 16)
                t.x_after[n] = t.x_ready

        def forget(t):
            t.a_free = t.b_free = t.x_ready = None
            t.x_after = {}

        def a_pass(t, batch):
            forget(t)
            yield from sequence(t, t.n, STAGES, batch)
            yield from sequence(t, 0, t.n, batch + 1)

        def ahead(t):
            forget(t)
            yield from sequence(t, 0, 1, 0)
            if t.n > 1:
                for e in (pe, act, pool):
                    e.wait(constants_of["w2q"])
                yield from sequence(t, 1, 2, 0)
            if t.n == 3:
                for e in (pe, act, pool):
                    e.wait(constants_of["L1"])
                yield from sequence(t, 2, 3, 0)

        def last_pass(t):
            forget(t)
            yield from sequence(t, t.n, STAGES, passes_a - 1)

        NL = 2 * BLOCKS
        s_loads_b = sem("loads_b")
        WL_SIZE = NL * KD * D
        wl_memory = w["experts"][:].rearrange("p k n -> p (k n)")
        wl = wl_memory[:, 0:WL_SIZE].rearrange("p (n k o) -> p n k o", n=NL, k=KD)
        qw = wide_memory[:, 0:WL_SIZE].bitcast(I32).rearrange("p (n k o) -> p n k o", n=NL, k=KD)
        group_scale = wide_memory[:, WL_SIZE:2 * WL_SIZE].rearrange("p (n k o) -> p n k o", n=NL, k=KD)
        la = wide_memory[0:RANK, 2 * WL_SIZE:2 * WL_SIZE + NL * D].rearrange("p (n d) -> p n d", n=NL)
        lb = [w[("L0q", "L0k", "L0v")[n // 2]][0:RANK, n % 2, :] for n in range(NL)]
        biases = ([wl_memory[:, WL_SIZE + n * D:WL_SIZE + (n + 1) * D] for n in range(4)]
                  + [wide_memory[:, 4 * L1_SIZE - (n + 1) * D:4 * L1_SIZE - n * D] for n in range(2)])

        def loop_b_constants():
            loads = [0]

            def load_b(dst, src):
                nc.sync.dma_start(dst, src).then_inc(s_loads_b, 16)
                loads[0] += 16

            for t in lanes[0:3]:
                sync_wait(t.x_after[2])
            for n in range(NL):
                load_b(qw[:, n], a["L3_q"][n].rearrange("(k p) o -> p k o", p=P))
                for k in range(KD):
                    for g in range(P // GROUP):
                        load_b(group_scale[g * GROUP:(g + 1) * GROUP, n, k, :],
                               a["L3_s"][n, k * (P // GROUP) + g:k * (P // GROUP) + g + 1, :].to_broadcast([GROUP, D]))
                load_b(lb[n], a["L3_lb"][n])
            load_b(la, a["L3_la"].rearrange("n r d -> r n d"))
            for n in (4, 5):
                load_b(biases[n], a["L3_ffn_biases"][n:n + 1, :].to_broadcast([P, D]))
            yield
            for t in lanes:
                sync_wait(t.x_after[3])
            for n in range(4):
                load_b(biases[n], a["L3_ffn_biases"][n:n + 1, :].to_broadcast([P, D]))
            yield
            dve.wait(*(t.x_after[3] for t in lanes))
            dve.q.wait_ge(s_loads_b, loads[0])
            pe.q.wait_ge(s_loads_b, loads[0])
            base_ready = []
            for n in range(NL):
                dve.wait(dve.done(dve.q.tensor_scalar(wl[:, n], qw[:, n], 1.0 / 7.5, -1.0, ALU.mult, ALU.add)))
                base_ready.append(dve.done(dve.q.tensor_tensor(wl[:, n], wl[:, n], group_scale[:, n], ALU.mult)))
                yield
            t = lanes[3]
            pe.wait(t.x_ready)
            bank_free = [None, None]
            for n in range(NL):
                bank = (t.a, t.b)[n % 2]
                pe.wait(bank_free[n % 2])
                for k in range(KD):
                    last = pe.q.matmul(bank[:, k * D:(k + 1) * D], la[:, n, k * P:(k + 1) * P], lb[n],
                                       start=True, stop=True)
                dve.wait(pe.done(last), base_ready[n])
                flat = wl[:, n].rearrange("p k o -> p (k o)")
                bank_free[n % 2] = dve.done(dve.q.tensor_tensor(flat, flat, bank[:, :], ALU.add))
                yield

        for e in range(E1):
            m = pool.q.memset(first_of[:, e:e + 1], float(E1 - e))
        first_ready = pool.done(m)
        dve.wait(first_ready)
        pe.wait(consts_ready, dve_consts)
        act.wait(consts_ready)

        passes_a = B // LANES_A
        for t in lanes:
            nc.sync.sem_inc(t.stored, 1)
        for name, e in engines.items():
            e.enter(ahead_sems[name], None, 0)
        issue([later_constants()] + [ahead(t) for t in lanes[1:]], ORDER_AHEAD)
        for e in engines.values():
            e.wait(constants_of["L3"], *(t.x_ready for t in lanes[1:]))
        for name, e in engines.items():
            e.q.sem_inc(loop_sems["a", name], 1)
        with nc.Fori(0, passes_a - 1) as i:
            for name, e in engines.items():
                e.enter(loop_sems["a", name], i, signals.get(("a", name), 1))
            dve.q.wait_ge(dve.sem, i * dve.per_pass + 1)
            issue([a_pass(t, i) for t in lanes], ORDER_A)
            for name, e in engines.items():
                signals["a", name] = e.count
        dve.q.wait_ge(dve.sem, (passes_a - 1) * signals["a", "dve"] + 1)
        for name, e in engines.items():
            e.enter(last_sems[name], None, 0)
        issue([last_pass(t) for t in lanes] + [loop_b_constants()], ORDER_LAST)

        for t in lanes:
            for q in (nc.sync, nc.vector):
                q.wait_ge(t.loaded_x, 16 * (passes_a + 1))
                q.wait_ge(t.loaded_c, 16 * (passes_a + 1))
                q.wait_ge(t.stored, 16 * passes_a + 1)
        a_done = {name: (last_sems[name], engines[name].count) for name in engines}
        for e in list(engines.values()):
            for s, v in a_done.values():
                e.q.wait_ge(s, v)
        for s, v in a_done.values():
            nc.sync.wait_ge(s, v)
        lane_ctx.close()

        bctx = ExitStack()

        def sb2(name, shape, dt=F32):
            return bctx.enter_context(nc.sbuf_tensor(name, shape, dt))

        lanes_b = []
        for n in range(LANES_B):
            t = Lane()
            t.n = n
            t.x_in = sb2(f"bx_in_{n}", [P, D])
            t.x = sb2(f"bx_{n}", [P, D])
            t.h = sb2(f"bh_{n}", [P, D])
            t.out = sb2(f"bout_{n}", [P, D])
            t.xn = sb2(f"bxn_{n}", [P, D])
            t.y = sb2(f"by_{n}", [P, D])
            t.hT = sb2(f"bhT_{n}", [P, KD, S])
            t.yT = sb2(f"byT_{n}", [P, KD, S])
            t.stats = sb2(f"bstats_{n}", [P, 6])
            t.mv = sb2(f"bmv_{n}", [P, 2])
            t.tiny = sb2(f"btiny_{n}", [P, 4])
            t.a = t.b = psum[:, n, :]
            t.loaded, t.stored = sem(f"b_loaded_{n}"), sem(f"b_stored_{n}")
            nc.sync.dma_start(t.x_in[:], scratch[n]).then_inc(t.loaded, 16)
            lanes_b.append(t)
        passes_b = B // LANES_B
        for name, e in engines.items():
            e.q.sem_inc(loop_sems["b", name], 1)
        for t in lanes_b:
            nc.sync.sem_inc(t.stored, 1)
        with nc.Fori(0, passes_b) as i:
            for name, e in engines.items():
                e.enter(loop_sems["b", name], i, signals.get(("b", name), 1))

            dve.q.wait_ge(dve.sem, i * dve.per_pass + 1)

            def linear(t, n, srcT, ready):
                pe.wait(t.b_free, ready)
                return pe.done(tokens(t.b, srcT, wl[:, n], D))

            def lane_b(t):
                t.a_free = t.b_free = None
                dve.q.wait_ge(t.loaded, 16 * i + 16)
                m = dve.done(dve.q.tensor_copy(t.x[:], t.x_in[:]))
                dve.wait(m)
                xn_free = yield from layernorm(t, t.x_in[:])
                nc.sync.wait_ge(dve.sem, i * dve.per_pass + xn_free.number + 1)
                nc.sync.dma_start(t.x_in[:], scratch[(i + 1) % passes_b * LANES_B + t.n]).then_inc(t.loaded, 16)
                dve.wait(xn_free)
                h_ready = dve.done(dve.q.tensor_copy(t.h[:], t.xn[:]))
                yield
                for blk in range(BLOCKS):
                    hT_ready = yield from two_transposed(t, t.hT, t.h, h_ready)
                    yield
                    y = linear(t, 2 * blk, t.hT, hT_ready)
                    yield
                    dve.wait(y)
                    t.b_free = m = dve.done(dve.q.tensor_tensor(t.y[:], t.b[:, 0:D], biases[2 * blk][:], ALU.add))
                    pool.wait(hT_ready)
                    h_ready = pool.done(pool.q.tensor_tensor(t.h[:], t.h[:], biases[2 * blk + 1][:], ALU.add))
                    m = yield from layernorm(t, t.y[:], m)
                    yield
                    pe.wait(t.a_free, m)
                    m = pe.done(transposes(t.a, t.xn, KD))
                    yield
                    act.wait(m)
                    for k in range(KD):
                        m = act.q.activation(t.yT[:, k, :], t.a[:, k * P:(k + 1) * P], ACT.Gelu,
                                             scale=gamma[:, blk, k:k + 1], bias=beta[:, blk, k:k + 1])
                    t.a_free = m = act.done(m)
                    yield
                    y = linear(t, 2 * blk + 1, t.yT, m)
                    yield
                    dve.wait(y, h_ready)
                    t.b_free = h_ready = dve.done(dve.q.tensor_tensor(t.h[:], t.b[:, 0:D], t.h[:], ALU.add))
                    yield
                dve.wait(h_ready)
                dve.q.wait_ge(t.stored, 16 * i + 1)
                m = dve.done(dve.q.scalar_tensor_tensor(t.out[:], t.h[:], gf["L3"], t.x[:], ALU.mult, ALU.add))
                nc.sync.wait_ge(dve.sem, i * dve.per_pass + m.number + 1)
                nc.sync.dma_start(out[i * LANES_B + t.n], t.out[:]).then_inc(t.stored, 16)

            issue([lane_b(t) for t in lanes_b], ORDER_B)
            for name, e in engines.items():
                signals["b", name] = e.count
        for t in lanes_b:
            nc.sync.wait_ge(t.loaded, 16 * (passes_b + 1))
            nc.sync.wait_ge(t.stored, 16 * passes_b + 1)
        bctx.close()


_OUT = (B, S, D)


def kernel(**inputs):
    import concourse.bacc as bacc
    from concourse.bass_utils import run_bass_kernel_spmd

    x = {n: np.asarray(v) for n, v in inputs.items()}
    c = np.ascontiguousarray
    arrays = {n: c(x[n]) for n in (
        "x", "g_xattn", "g_ffn", "L1_ffn_router_b", "L1_ffn_expert_b", "L3_ffn_biases")}

    def columns(v):
        v = v.reshape(*v.shape[:-1], -1, P)
        return c(np.moveaxis(v, -1, 0))

    arrays["ctxT"] = c(x["ctx_768"].transpose(0, 2, 1))
    kv = x["L0_xattn_Wkv"].reshape(H, 2, D // H, C)
    bkv = x["L0_xattn_bkv"].reshape(H, 2, D // H)
    arrays["L0_wq"] = c(x["L0_xattn_Wq"].T)
    arrays["L0_bq"] = columns(x["L0_xattn_bq"])
    arrays["L0_wk"], arrays["L0_wv"] = (c(kv[:, n].reshape(D, C).T) for n in range(2))
    arrays["L0_bk"], arrays["L0_bv"] = (columns(bkv[:, n].reshape(D)) for n in range(2))
    arrays["L0_wo"] = c(x["L0_xattn_Wo"].T)
    arrays["L0_bo"] = c(x["L0_xattn_bo"])
    for l in ("L2", "L3"):
        for n in "qkvo":
            arrays[f"{l}_w{n}"] = c(x[f"{l}_xattn_W{n}"])
            arrays[f"{l}_b{n}"] = (c if n == "o" else columns)(x[f"{l}_xattn_b{n}"])
    arrays["L1_wq"], arrays["L1_wk"], arrays["L1_wv"] = (c(x["L1_xattn_w_" + n]) for n in "qkv")
    arrays["L1_wo"], arrays["L1_bo"] = c(x["L1_xattn_w_out"]), c(x["L1_xattn_b_out"])
    arrays["L1_router"] = c(x["L1_ffn_router_w"])
    arrays["L1_experts"] = c(x["L1_ffn_expert_w"].transpose(1, 0, 2).reshape(D, E1 * D))
    arrays["L0_w1"], arrays["L0_w2"] = c(x["L0_ffn_w1"].T), c(x["L0_ffn_w2"].T)
    arrays["L0_convb"] = columns(x["L0_ffn_conv_b"])
    arrays["L2s_n1"], arrays["L2s_n2"] = columns(x["L2_ffn_n1_w"]), columns(x["L2_ffn_n2_w"])
    arrays["L3_gamma"], arrays["L3_beta"] = columns(x["L3_ffn_ln_gamma"]), columns(x["L3_ffn_ln_beta"])
    arrays["L0_conv"] = c(x["L0_ffn_conv_w"][:, 0, :])
    qkv = x["L2_ffn_qkv_w"].reshape(3, D, D)
    for n, name in enumerate("qkv"):
        arrays["L2s_w" + name] = c(qkv[n].T)
    arrays["L2s_wo"] = c(x["L2_ffn_o_w"].T)
    arrays["L2s_gate"], arrays["L2s_up"], arrays["L2s_down"] = (c(x[f"L2_ffn_{n}_w"].T) for n in ("gate", "up", "down"))
    arrays["L3_q"] = c(x["L3_ffn_qweights"].transpose(0, 2, 1))
    arrays["L3_s"] = c(x["L3_ffn_scales"].transpose(0, 2, 1))
    arrays["L3_la"] = c(x["L3_ffn_lora_a"])
    arrays["L3_lb"] = c(x["L3_ffn_lora_b"].transpose(0, 2, 1))
    signals = {}
    for _ in range(2):
        nc = bacc.Bacc("TRN2", target_bir_lowering=False, num_devices=1)
        a = {n: nc.dram_tensor("in_" + n, v.shape, mybir.dt.from_np(v.dtype), kind="ExternalInput").ap()
             for n, v in arrays.items()}
        out = nc.dram_tensor("out", _OUT, F32, kind="ExternalOutput").ap()
        build(nc, a, out, signals)
    r = run_bass_kernel_spmd(nc, [{"in_" + n: v for n, v in arrays.items()}], core_ids=[0])
    return r.results[0]["out"]
```
